# Optimizing a Trainium2 kernel written in Bass

```python
import numpy as np
import jax
import jax.numpy as jnp

def _softmax(x, axis=-1):
    return jax.nn.softmax(x, axis=axis)

def _gelu(x):
    return jax.nn.gelu(x, approximate=True)

def _silu(x):
    return jax.nn.silu(x)

def _sigmoid(x):
    return jax.nn.sigmoid(x)

def _layernorm(x, axis=-1, eps=1e-05):
    m = jnp.mean(x, axis=axis, keepdims=True)
    v = jnp.var(x, axis=axis, keepdims=True)
    return (x - m) / jnp.sqrt(v + eps)

def _scatter_add(tgt, idx, src, axis=0):
    return tgt.at[idx].add(src)

def _segment_sum(src, seg, n):
    return jax.ops.segment_sum(src, seg, n)
kernel_name = 'mk_gps_d2_gnn_r32_e562d3'

def setup_inputs(seed: int=0):
    np.random.seed(seed)
    _w = jnp.asarray

    def _rec_inputs():
        import jax
        import jax.numpy as jnp
        _gk = jax.random.key(seed)
        x = -8.776e-05 + 1 * jax.random.normal(jax.random.fold_in(_gk, 1), (625, 256), jnp.float32)
        src = jax.random.randint(jax.random.fold_in(_gk, 2), (20000,), 0, 625, jnp.int32)
        dst = jnp.minimum((625 * jax.random.uniform(jax.random.fold_in(_gk, 3), (20000,)) ** 2.0).astype(jnp.int32), 19999)
        _o = jnp.argsort(dst, stable=True)
        src = src[_o]
        dst = dst[_o]
        return (x, src, dst)
    x, src, dst = _rec_inputs()

    def _L0_gnn_setup():
        import jax, jax.numpy as jnp
        import numpy as np
        N, E, IN_DIM, HEADS, HEAD_DIM = (625, 10000, 256, 4, 64)
        OUT_DIM = HEADS * HEAD_DIM
        NEG_SLOPE = 0.2
        LN_EPS = 1e-05
        SM_EPS = 1e-16

        def _gatv2_block(x, edge_index, W_l, W_r, att, bias, gamma, beta):
            src, dst = (edge_index[0], edge_index[1])
            xl = (x @ W_l).reshape(N, HEADS, HEAD_DIM)
            xr = (x @ W_r).reshape(N, HEADS, HEAD_DIM)
            e = xl[src] + xr[dst]
            e = jnp.where(e >= 0, e, NEG_SLOPE * e)
            score = jnp.einsum('ehd,hd->eh', e, att)
            m = jax.ops.segment_max(score, dst, num_segments=N)
            m = jnp.where(jnp.isfinite(m), m, 0.0)
            ex = jnp.exp(score - m[dst])
            denom = jax.ops.segment_sum(ex, dst, num_segments=N)
            alpha = ex / (denom[dst] + SM_EPS)
            agg = jax.ops.segment_sum(alpha[:, :, None] * xl[src], dst, num_segments=N)
            out = agg.reshape(N, OUT_DIM) + bias
            h = jax.nn.elu(out) + x
            mu = jnp.mean(h, axis=-1, keepdims=True)
            var = jnp.mean(jnp.square(h - mu), axis=-1, keepdims=True)
            return (h - mu) * jax.lax.rsqrt(var + LN_EPS) * gamma + beta
        key = jax.random.key(seed)
        ks = jax.random.split(key, 9)
        s = 1.0 / np.sqrt(IN_DIM)
        return {'x': jax.random.normal(ks[0], (N, IN_DIM), jnp.float32), 'edge_index': jax.random.randint(ks[1], (2, E), 0, N, jnp.int32), 'W_l': jax.random.normal(ks[2], (IN_DIM, OUT_DIM), jnp.float32) * s, 'W_r': jax.random.normal(ks[3], (IN_DIM, OUT_DIM), jnp.float32) * s, 'att': jax.random.normal(ks[4], (HEADS, HEAD_DIM), jnp.float32) * s, 'bias': jnp.zeros((OUT_DIM,), jnp.float32), 'gamma': jnp.ones((OUT_DIM,), jnp.float32), 'beta': jnp.zeros((OUT_DIM,), jnp.float32)}
    _L0_gnn_all = _L0_gnn_setup()
    _L0_gnn_in = {k: v for k, v in _L0_gnn_all.items() if k in ('W_l', 'W_r', 'att', 'bias', 'gamma', 'beta')}
    del _L0_gnn_all

    def _L0_mix_setup():
        import jax, jax.numpy as jnp
        import numpy as np
        B, N, C = (8, 256, 256)
        HEADS, DH, KR = (8, 32, 4)
        INNER = HEADS * DH
        FF = 4 * C
        EPS = 1e-05

        def layernorm(x, g, b):
            mu = jnp.mean(x, axis=-1, keepdims=True)
            var = jnp.mean((x - mu) ** 2, axis=-1, keepdims=True)
            return (x - mu) * jax.lax.rsqrt(var + EPS) * g + b
        key = jax.random.key(seed)
        ks = jax.random.split(key, 16)
        s = 0.02
        return {'x': jax.random.normal(ks[0], (B, N, C), jnp.float32), 'ln1_g': jnp.ones((C,), jnp.float32), 'ln1_b': jnp.zeros((C,), jnp.float32), 'Wx': jax.random.normal(ks[1], (C, INNER), jnp.float32) * s, 'bx': jnp.zeros((INNER,), jnp.float32), 'Wq': jax.random.normal(ks[2], (DH, KR), jnp.float32) * s, 'Wk': jax.random.normal(ks[3], (DH, KR), jnp.float32) * s, 'Wv': jax.random.normal(ks[4], (DH, DH), jnp.float32) * s, 'Wo': jax.random.normal(ks[5], (INNER, C), jnp.float32) * s, 'bo': jnp.zeros((C,), jnp.float32), 'ln2_g': jnp.ones((C,), jnp.float32), 'ln2_b': jnp.zeros((C,), jnp.float32), 'W1': jax.random.normal(ks[6], (C, FF), jnp.float32) * s, 'b1': jnp.zeros((FF,), jnp.float32), 'W2': jax.random.normal(ks[7], (FF, C), jnp.float32) * s, 'b2': jnp.zeros((C,), jnp.float32)}
    _L0_mix_all = _L0_mix_setup()
    _L0_mix_in = {k: v for k, v in _L0_mix_all.items() if k in ('ln1_g', 'ln1_b', 'Wx', 'bx', 'Wq', 'Wk', 'Wv', 'Wo', 'bo', 'ln2_g', 'ln2_b', 'W1', 'b1', 'W2', 'b2')}
    del _L0_mix_all

    def _L0_ffn_setup():
        import jax, jax.numpy as jnp
        import numpy as np
        D_MODEL = 256
        N_EXPERTS = 16
        HIDDEN = 512
        SCALE = 0.02
        key = jax.random.key(seed)
        ks = jax.random.split(key, 5)
        x = jax.random.normal(ks[0], (4, 256, D_MODEL), dtype=jnp.float32)
        gate_w = jax.random.normal(ks[1], (D_MODEL, N_EXPERTS), dtype=jnp.float32) * SCALE
        gate_b = jnp.zeros((N_EXPERTS,), dtype=jnp.float32)
        w1 = jax.random.normal(ks[2], (N_EXPERTS, D_MODEL, HIDDEN), dtype=jnp.float32) * SCALE
        w2 = jax.random.normal(ks[3], (N_EXPERTS, D_MODEL, HIDDEN), dtype=jnp.float32) * SCALE
        w3 = jax.random.normal(ks[4], (N_EXPERTS, HIDDEN, D_MODEL), dtype=jnp.float32) * SCALE
        return {'x': x, 'gate_w': gate_w, 'gate_b': gate_b, 'w1': w1, 'w2': w2, 'w3': w3}
    _L0_ffn_all = _L0_ffn_setup()
    _L0_ffn_in = {k: v for k, v in _L0_ffn_all.items() if k in ('gate_w', 'gate_b', 'w1', 'w2', 'w3')}
    del _L0_ffn_all

    def _L1_gnn_setup():
        import jax, jax.numpy as jnp
        import numpy as np
        N = 50000
        E = 25000
        F = 256
        H = 4
        D = 64
        key = jax.random.key(seed)
        ks = jax.random.split(key, 10)
        s = 0.02
        HD = H * D
        return {'feat': jax.random.normal(ks[0], (N, F), jnp.float32), 'src': jax.random.randint(ks[1], (E,), 0, N), 'dst': jax.random.randint(ks[2], (E,), 0, N), 'Wq': jax.random.normal(ks[3], (HD, F), jnp.float32) * s, 'bq': jnp.zeros((HD,), jnp.float32), 'Wk': jax.random.normal(ks[4], (HD, F), jnp.float32) * s, 'bk': jnp.zeros((HD,), jnp.float32), 'Wv': jax.random.normal(ks[5], (HD, F), jnp.float32) * s, 'bv': jnp.zeros((HD,), jnp.float32), 'Wskip': jax.random.normal(ks[6], (HD, F), jnp.float32) * s, 'bskip': jnp.zeros((HD,), jnp.float32), 'Wgate': jax.random.normal(ks[7], (1, 3 * HD), jnp.float32) * s, 'bgate': jnp.zeros((1,), jnp.float32), 'ln_w': jnp.ones((HD,), jnp.float32), 'ln_b': jnp.zeros((HD,), jnp.float32), 'prelu_a': jnp.float32(0.25)}
    _L1_gnn_all = _L1_gnn_setup()
    _L1_gnn_in = {k: v for k, v in _L1_gnn_all.items() if k in ('Wq', 'bq', 'Wk', 'bk', 'Wv', 'bv', 'Wskip', 'bskip', 'Wgate', 'bgate', 'ln_w', 'ln_b', 'prelu_a')}
    del _L1_gnn_all

    def _L1_mix_setup():
        import jax, jax.numpy as jnp
        import numpy as np
        EPS = 1e-05

        def _layernorm(x, weight, bias):
            mean = jnp.mean(x, axis=-1, keepdims=True)
            std = jnp.std(x, axis=-1, keepdims=True, ddof=1)
            out = (x - mean) / (std + EPS)
            return weight * out + bias
        key = jax.random.key(seed)
        B, N, C = (4, 1024, 256)
        H, hc = (8, C // 8)
        kx, = jax.random.split(key, 1)
        x = jax.random.normal(kx, (B, N, C), dtype=jnp.float32)
        return {'x': x, 'kln_weight': jnp.ones((H, 1, hc), dtype=jnp.float32), 'kln_bias': jnp.zeros((H, 1, hc), dtype=jnp.float32), 'vln_weight': jnp.ones((H, 1, hc), dtype=jnp.float32), 'vln_bias': jnp.zeros((H, 1, hc), dtype=jnp.float32)}
    _L1_mix_all = _L1_mix_setup()
    _L1_mix_in = {k: v for k, v in _L1_mix_all.items() if k in ('kln_weight', 'kln_bias', 'vln_weight', 'vln_bias')}
    del _L1_mix_all

    def _L1_ffn_setup():
        import jax, jax.numpy as jnp
        import numpy as np
        B, T, C = (64, 384, 256)
        NH, NKV = (4, 2)
        HD = C // NH
        NREP = NH // NKV
        NE, TOPK = (8, 2)
        HID = int(8 / 3 * C)
        EPS_RMS = 1e-06

        def _rope_tables(t_len):
            inv_freq = 1.0 / 10000.0 ** (np.arange(0, HD, 2, dtype=np.float32) / HD)
            t = np.arange(t_len, dtype=np.float32)
            freqs = np.outer(t, inv_freq)
            emb = np.concatenate([freqs, freqs], axis=-1)
            return (jnp.asarray(np.cos(emb)), jnp.asarray(np.sin(emb)))

        def _rotate_half(x):
            h = x.shape[-1] // 2
            return jnp.concatenate([-x[..., h:], x[..., :h]], axis=-1)

        def _rmsnorm(v, w):
            return v * jax.lax.rsqrt(jnp.mean(v * v, axis=-1, keepdims=True) + EPS_RMS) * w
        key = jax.random.key(seed)
        ks = jax.random.split(key, 10)
        s = lambda k, shape: jax.random.normal(k, shape, jnp.float32) * 0.02
        return {'x': jax.random.normal(ks[0], (B, T, C), jnp.float32), 'ln1_w': jnp.ones((C,), jnp.float32), 'ln2_w': jnp.ones((C,), jnp.float32), 'wq': s(ks[1], (NH * HD, C)), 'wk': s(ks[2], (NKV * HD, C)), 'wv': s(ks[3], (NKV * HD, C)), 'wo': s(ks[4], (C, C)), 'router_w': s(ks[5], (NE, C)), 'w1': s(ks[6], (NE, HID, C)), 'w2': s(ks[7], (NE, C, HID)), 'w3': s(ks[8], (NE, HID, C))}
    _L1_ffn_all = _L1_ffn_setup()
    _L1_ffn_in = {k: v for k, v in _L1_ffn_all.items() if k in ('ln1_w', 'ln2_w', 'wq', 'wk', 'wv', 'wo', 'router_w', 'w1', 'w2', 'w3')}
    del _L1_ffn_all
    return {'x': x, 'src': src, 'dst': dst, 'L0_gnn_W_l': _L0_gnn_in['W_l'], 'L0_gnn_W_r': _L0_gnn_in['W_r'], 'L0_gnn_att': _L0_gnn_in['att'], 'L0_gnn_bias': _L0_gnn_in['bias'], 'L0_gnn_gamma': _L0_gnn_in['gamma'], 'L0_gnn_beta': _L0_gnn_in['beta'], 'L0_mix_ln1_g': _L0_mix_in['ln1_g'], 'L0_mix_ln1_b': _L0_mix_in['ln1_b'], 'L0_mix_Wx': _L0_mix_in['Wx'], 'L0_mix_bx': _L0_mix_in['bx'], 'L0_mix_Wq': _L0_mix_in['Wq'], 'L0_mix_Wk': _L0_mix_in['Wk'], 'L0_mix_Wv': _L0_mix_in['Wv'], 'L0_mix_Wo': _L0_mix_in['Wo'], 'L0_mix_bo': _L0_mix_in['bo'], 'L0_mix_ln2_g': _L0_mix_in['ln2_g'], 'L0_mix_ln2_b': _L0_mix_in['ln2_b'], 'L0_mix_W1': _L0_mix_in['W1'], 'L0_mix_b1': _L0_mix_in['b1'], 'L0_mix_W2': _L0_mix_in['W2'], 'L0_mix_b2': _L0_mix_in['b2'], 'L0_ffn_gate_w': _L0_ffn_in['gate_w'], 'L0_ffn_gate_b': _L0_ffn_in['gate_b'], 'L0_ffn_w1': _L0_ffn_in['w1'], 'L0_ffn_w2': _L0_ffn_in['w2'], 'L0_ffn_w3': _L0_ffn_in['w3'], 'L1_gnn_Wq': _L1_gnn_in['Wq'], 'L1_gnn_bq': _L1_gnn_in['bq'], 'L1_gnn_Wk': _L1_gnn_in['Wk'], 'L1_gnn_bk': _L1_gnn_in['bk'], 'L1_gnn_Wv': _L1_gnn_in['Wv'], 'L1_gnn_bv': _L1_gnn_in['bv'], 'L1_gnn_Wskip': _L1_gnn_in['Wskip'], 'L1_gnn_bskip': _L1_gnn_in['bskip'], 'L1_gnn_Wgate': _L1_gnn_in['Wgate'], 'L1_gnn_bgate': _L1_gnn_in['bgate'], 'L1_gnn_ln_w': _L1_gnn_in['ln_w'], 'L1_gnn_ln_b': _L1_gnn_in['ln_b'], 'L1_gnn_prelu_a': _L1_gnn_in['prelu_a'], 'L1_mix_kln_weight': _L1_mix_in['kln_weight'], 'L1_mix_kln_bias': _L1_mix_in['kln_bias'], 'L1_mix_vln_weight': _L1_mix_in['vln_weight'], 'L1_mix_vln_bias': _L1_mix_in['vln_bias'], 'L1_ffn_ln1_w': _L1_ffn_in['ln1_w'], 'L1_ffn_ln2_w': _L1_ffn_in['ln2_w'], 'L1_ffn_wq': _L1_ffn_in['wq'], 'L1_ffn_wk': _L1_ffn_in['wk'], 'L1_ffn_wv': _L1_ffn_in['wv'], 'L1_ffn_wo': _L1_ffn_in['wo'], 'L1_ffn_router_w': _L1_ffn_in['router_w'], 'L1_ffn_w1': _L1_ffn_in['w1'], 'L1_ffn_w2': _L1_ffn_in['w2'], 'L1_ffn_w3': _L1_ffn_in['w3']}

def reference(x, src, dst, L0_gnn_W_l, L0_gnn_W_r, L0_gnn_att, L0_gnn_bias, L0_gnn_gamma, L0_gnn_beta, L0_mix_ln1_g, L0_mix_ln1_b, L0_mix_Wx, L0_mix_bx, L0_mix_Wq, L0_mix_Wk, L0_mix_Wv, L0_mix_Wo, L0_mix_bo, L0_mix_ln2_g, L0_mix_ln2_b, L0_mix_W1, L0_mix_b1, L0_mix_W2, L0_mix_b2, L0_ffn_gate_w, L0_ffn_gate_b, L0_ffn_w1, L0_ffn_w2, L0_ffn_w3, L1_gnn_Wq, L1_gnn_bq, L1_gnn_Wk, L1_gnn_bk, L1_gnn_Wv, L1_gnn_bv, L1_gnn_Wskip, L1_gnn_bskip, L1_gnn_Wgate, L1_gnn_bgate, L1_gnn_ln_w, L1_gnn_ln_b, L1_gnn_prelu_a, L1_mix_kln_weight, L1_mix_kln_bias, L1_mix_vln_weight, L1_mix_vln_bias, L1_ffn_ln1_w, L1_ffn_ln2_w, L1_ffn_wq, L1_ffn_wk, L1_ffn_wv, L1_ffn_wo, L1_ffn_router_w, L1_ffn_w1, L1_ffn_w2, L1_ffn_w3):
    import jax
    import jax.numpy as jnp

    def _L0_gnn_ref(x, edge_index, W_l, W_r, att, bias, gamma, beta):
        import jax, jax.numpy as jnp
        import numpy as np
        N, E, IN_DIM, HEADS, HEAD_DIM = (625, 10000, 256, 4, 64)
        OUT_DIM = HEADS * HEAD_DIM
        NEG_SLOPE = 0.2
        LN_EPS = 1e-05
        SM_EPS = 1e-16

        def _gatv2_block(x, edge_index, W_l, W_r, att, bias, gamma, beta):
            src, dst = (edge_index[0], edge_index[1])
            xl = (x @ W_l).reshape(N, HEADS, HEAD_DIM)
            xr = (x @ W_r).reshape(N, HEADS, HEAD_DIM)
            e = xl[src] + xr[dst]
            e = jnp.where(e >= 0, e, NEG_SLOPE * e)
            score = jnp.einsum('ehd,hd->eh', e, att)
            m = jax.ops.segment_max(score, dst, num_segments=N)
            m = jnp.where(jnp.isfinite(m), m, 0.0)
            ex = jnp.exp(score - m[dst])
            denom = jax.ops.segment_sum(ex, dst, num_segments=N)
            alpha = ex / (denom[dst] + SM_EPS)
            agg = jax.ops.segment_sum(alpha[:, :, None] * xl[src], dst, num_segments=N)
            out = agg.reshape(N, OUT_DIM) + bias
            h = jax.nn.elu(out) + x
            mu = jnp.mean(h, axis=-1, keepdims=True)
            var = jnp.mean(jnp.square(h - mu), axis=-1, keepdims=True)
            return (h - mu) * jax.lax.rsqrt(var + LN_EPS) * gamma + beta
        return _gatv2_block(x, edge_index, W_l, W_r, att, bias, gamma, beta)

    def _L0_mix_ref(x, ln1_g, ln1_b, Wx, bx, Wq, Wk, Wv, Wo, bo, ln2_g, ln2_b, W1, b1, W2, b2):
        import jax, jax.numpy as jnp
        import numpy as np
        B, N, C = (8, 256, 256)
        HEADS, DH, KR = (8, 32, 4)
        INNER = HEADS * DH
        FF = 4 * C
        EPS = 1e-05

        def layernorm(x, g, b):
            mu = jnp.mean(x, axis=-1, keepdims=True)
            var = jnp.mean((x - mu) ** 2, axis=-1, keepdims=True)
            return (x - mu) * jax.lax.rsqrt(var + EPS) * g + b
        b, n, c = x.shape
        h = layernorm(x, ln1_g, ln1_b)
        xm = h @ Wx + bx
        xm = xm.reshape(b, n, HEADS, DH).transpose(0, 2, 1, 3)
        q = jax.nn.softmax(xm @ Wq, axis=-1)
        k = jax.nn.softmax(xm @ Wk, axis=-2)
        v = xm @ Wv
        kv = jnp.einsum('bhnr,bhnd->bhrd', k, v)
        qkv = jnp.einsum('bhnr,bhrd->bhnd', q, kv)
        attn = qkv.transpose(0, 2, 1, 3).reshape(b, n, INNER) @ Wo + bo
        fx = attn + x
        h2 = layernorm(fx, ln2_g, ln2_b)
        m = jax.nn.gelu(h2 @ W1 + b1, approximate=False) @ W2 + b2
        return m + fx

    def _L0_ffn_ref(x, gate_w, gate_b, w1, w2, w3):
        import jax, jax.numpy as jnp
        import numpy as np
        D_MODEL = 256
        N_EXPERTS = 16
        HIDDEN = 512
        SCALE = 0.02
        n_experts = w1.shape[0]
        logits = jnp.einsum('bsd,de->bse', x, gate_w) + gate_b
        probs = jax.nn.softmax(logits, axis=-1)
        top_probs, top_idx = jax.lax.top_k(probs, 2)
        top_probs = top_probs / jnp.sum(top_probs, axis=-1, keepdims=True)
        dispatch = jnp.sum(jax.nn.one_hot(top_idx, n_experts, dtype=x.dtype) * top_probs[..., None], axis=-2)
        h1 = jnp.einsum('bsd,edh->bseh', x, w1)
        h2 = jnp.einsum('bsd,edh->bseh', x, w2)
        hidden = jax.nn.silu(h1) * h2
        expert_out = jnp.einsum('bseh,eho->bseo', hidden, w3)
        return jnp.einsum('bseo,bse->bso', expert_out, dispatch)

    def _L1_gnn_ref(feat, src, dst, Wq, bq, Wk, bk, Wv, bv, Wskip, bskip, Wgate, bgate, ln_w, ln_b, prelu_a):
        import jax, jax.numpy as jnp
        import numpy as np
        N = 50000
        E = 25000
        F = 256
        H = 4
        D = 64
        n = feat.shape[0]
        scale = 1.0 / np.sqrt(D).astype(np.float32)
        q = (feat @ Wq.T + bq).reshape(n, H, D)
        k = (feat @ Wk.T + bk).reshape(n, H, D)
        v = (feat @ Wv.T + bv).reshape(n, H, D)
        e = jnp.einsum('ehd,ehd->eh', q[src], k[dst]) * scale
        m = jax.ops.segment_max(e, dst, num_segments=n)
        ex = jnp.exp(e - m[dst])
        denom = jax.ops.segment_sum(ex, dst, num_segments=n)
        sa = ex / denom[dst]
        agg = jax.ops.segment_sum(sa[:, :, None] * v[src], dst, num_segments=n)
        rst = agg.reshape(n, H * D)
        skip = feat @ Wskip.T + bskip
        g = jax.nn.sigmoid(jnp.concatenate([skip, rst, skip - rst], axis=-1) @ Wgate.T + bgate)
        rst = g * skip + (1.0 - g) * rst
        mu = rst.mean(-1, keepdims=True)
        var = rst.var(-1, keepdims=True)
        rst = (rst - mu) * jax.lax.rsqrt(var + 1e-05) * ln_w + ln_b
        return jnp.where(rst >= 0, rst, prelu_a * rst)

    def _L1_mix_ref(x, kln_weight, kln_bias, vln_weight, vln_bias):
        import jax, jax.numpy as jnp
        import numpy as np
        EPS = 1e-05

        def _layernorm(x, weight, bias):
            mean = jnp.mean(x, axis=-1, keepdims=True)
            std = jnp.std(x, axis=-1, keepdims=True, ddof=1)
            out = (x - mean) / (std + EPS)
            return weight * out + bias
        B, N, C = x.shape
        H = kln_weight.shape[0]
        hc = C // H
        qkv = x.reshape(B, N, H, hc).transpose(0, 2, 1, 3)
        q = qkv
        k = _layernorm(qkv, kln_weight, kln_bias)
        v = _layernorm(qkv, vln_weight, vln_bias)
        kv = jnp.einsum('bhnd,bhne->bhde', k, v) / N
        out = jnp.einsum('bhnd,bhde->bhne', q, kv)
        out = out.transpose(0, 2, 1, 3).reshape(B, N, C)
        return out + x

    def _L1_ffn_ref(x, ln1_w, ln2_w, wq, wk, wv, wo, router_w, w1, w2, w3):
        import jax, jax.numpy as jnp
        import numpy as np
        B, T, C = (64, 384, 256)
        NH, NKV = (4, 2)
        HD = C // NH
        NREP = NH // NKV
        NE, TOPK = (8, 2)
        HID = int(8 / 3 * C)
        EPS_RMS = 1e-06

        def _rope_tables(t_len):
            inv_freq = 1.0 / 10000.0 ** (np.arange(0, HD, 2, dtype=np.float32) / HD)
            t = np.arange(t_len, dtype=np.float32)
            freqs = np.outer(t, inv_freq)
            emb = np.concatenate([freqs, freqs], axis=-1)
            return (jnp.asarray(np.cos(emb)), jnp.asarray(np.sin(emb)))

        def _rotate_half(x):
            h = x.shape[-1] // 2
            return jnp.concatenate([-x[..., h:], x[..., :h]], axis=-1)

        def _rmsnorm(v, w):
            return v * jax.lax.rsqrt(jnp.mean(v * v, axis=-1, keepdims=True) + EPS_RMS) * w
        Bx, Tx, Cx = x.shape
        h = _rmsnorm(x, ln1_w)
        q = (h @ wq.T).reshape(Bx, Tx, NH, HD).transpose(0, 2, 1, 3)
        k = (h @ wk.T).reshape(Bx, Tx, NKV, HD).transpose(0, 2, 1, 3)
        v = (h @ wv.T).reshape(Bx, Tx, NKV, HD).transpose(0, 2, 1, 3)
        cos, sin = _rope_tables(Tx)
        cos, sin = (cos[None, None], sin[None, None])
        q = q * cos + _rotate_half(q) * sin
        k = k * cos + _rotate_half(k) * sin
        k = jnp.repeat(k, NREP, axis=1)
        v = jnp.repeat(v, NREP, axis=1)
        scores = jnp.einsum('bhtd,bhsd->bhts', q, k) / jnp.sqrt(jnp.float32(HD))
        causal = jnp.tril(jnp.ones((Tx, Tx), dtype=bool))
        scores = jnp.where(causal[None, None], scores, jnp.float32(-1e+30))
        att = jax.nn.softmax(scores, axis=-1)
        y = jnp.einsum('bhts,bhsd->bhtd', att, v).transpose(0, 2, 1, 3).reshape(Bx, Tx, Cx)
        x = x + y @ wo.T
        flat = _rmsnorm(x, ln2_w).reshape(-1, Cx)
        probs = jax.nn.softmax(flat @ router_w.T, axis=-1)
        tp, ti = jax.lax.top_k(probs, TOPK)
        tp = tp / (jnp.sum(tp, axis=-1, keepdims=True) + 1e-09)
        weights = jnp.sum(tp[..., None] * jax.nn.one_hot(ti, NE, dtype=flat.dtype), axis=1)
        out = jnp.zeros_like(flat)
        for e in range(NE):
            hh = jax.nn.silu(flat @ w1[e].T) * (flat @ w3[e].T)
            out = out + weights[:, e:e + 1] * (hh @ w2[e].T)
        return x + out.reshape(Bx, Tx, Cx)
    edge_index = jnp.stack([src, dst])
    xn = _layernorm(x, axis=-1)
    x = x + _L0_gnn_ref(xn, edge_index, L0_gnn_W_l, L0_gnn_W_r, L0_gnn_att, L0_gnn_bias, L0_gnn_gamma, L0_gnn_beta) + _L0_mix_ref(xn[None], L0_mix_ln1_g, L0_mix_ln1_b, L0_mix_Wx, L0_mix_bx, L0_mix_Wq, L0_mix_Wk, L0_mix_Wv, L0_mix_Wo, L0_mix_bo, L0_mix_ln2_g, L0_mix_ln2_b, L0_mix_W1, L0_mix_b1, L0_mix_W2, L0_mix_b2)[0]
    x = x + _L0_ffn_ref(_layernorm(x, axis=-1)[None], L0_ffn_gate_w, L0_ffn_gate_b, L0_ffn_w1, L0_ffn_w2, L0_ffn_w3)[0]
    xn = _layernorm(x, axis=-1)
    x = x + _L1_gnn_ref(xn, src, dst, L1_gnn_Wq, L1_gnn_bq, L1_gnn_Wk, L1_gnn_bk, L1_gnn_Wv, L1_gnn_bv, L1_gnn_Wskip, L1_gnn_bskip, L1_gnn_Wgate, L1_gnn_bgate, L1_gnn_ln_w, L1_gnn_ln_b, L1_gnn_prelu_a) + _L1_mix_ref(xn[None], L1_mix_kln_weight, L1_mix_kln_bias, L1_mix_vln_weight, L1_mix_vln_bias)[0]
    x = x + _L1_ffn_ref(_layernorm(x, axis=-1)[None], L1_ffn_ln1_w, L1_ffn_ln2_w, L1_ffn_wq, L1_ffn_wk, L1_ffn_wv, L1_ffn_wo, L1_ffn_router_w, L1_ffn_w1, L1_ffn_w2, L1_ffn_w3)[0]
    return x

_drawn_inputs = setup_inputs


def setup_inputs(seed=0):
    import zlib

    import numpy as np

    out = dict(_drawn_inputs(seed))
    spreads = {'L0_gnn_bias': (0.0, 0.1),
     'L0_gnn_gamma': (1.0, 0.2),
     'L0_gnn_beta': (0.0, 0.1),
     'L0_mix_ln1_g': (1.0, 0.6),
     'L0_mix_ln1_b': (0.0, 0.8),
     'L0_mix_bx': (0.0, 0.8),
     'L0_mix_bo': (0.0, 0.1),
     'L0_mix_ln2_g': (1.0, 0.6),
     'L0_mix_ln2_b': (0.0, 0.8),
     'L0_mix_b1': (0.0, 0.603),
     'L0_mix_b2': (0.0, 0.1),
     'L0_ffn_gate_b': (0.0, 0.8),
     'L1_gnn_bq': (0.0, 0.8),
     'L1_gnn_bk': (0.0, 0.8),
     'L1_gnn_bv': (0.0, 0.1),
     'L1_gnn_bskip': (0.0, 0.1),
     'L1_gnn_ln_w': (1.0, 0.2),
     'L1_gnn_ln_b': (0.0, 0.588),
     'L1_mix_kln_weight': (1.0, 0.2),
     'L1_mix_kln_bias': (0.0, 0.6),
     'L1_mix_vln_weight': (1.0, 0.2),
     'L1_mix_vln_bias': (0.0, 0.586),
     'L1_ffn_ln1_w': (1.0, 0.6),
     'L1_ffn_ln2_w': (1.0, 0.6)}
    factors = {'L0_gnn_W_r': 6.106,
     'L0_mix_Wx': 8.0,
     'L0_mix_Wq': 8.0,
     'L0_mix_Wk': 8.0,
     'L0_mix_Wv': 8.0,
     'L0_mix_Wo': 8.0,
     'L0_ffn_gate_w': 8.0,
     'L0_ffn_w1': 8.0,
     'L0_ffn_w2': 8.0,
     'L0_ffn_w3': 8.0,
     'L1_gnn_Wq': 8.0,
     'L1_gnn_Wk': 8.0,
     'L1_gnn_Wgate': 7.593,
     'L1_ffn_wq': 8.0,
     'L1_ffn_wk': 8.0,
     'L1_ffn_wv': 8.0,
     'L1_ffn_wo': 8.0,
     'L1_ffn_router_w': 8.0,
     'L1_ffn_w1': 8.0,
     'L1_ffn_w2': 8.0,
     'L1_ffn_w3': 8.0}
    for name, (base, spread) in spreads.items():
        noise = np.random.default_rng([zlib.crc32(name.encode()), seed]).standard_normal(out[name].shape)
        drawn = base * np.exp(spread * noise) if base else spread * noise
        out[name] = jnp.asarray(drawn.astype(out[name].dtype))
    for name, factor in factors.items():
        out[name] = (out[name] * factor).astype(out[name].dtype)
    return out
```

```python
from contextlib import ExitStack

import numpy as np
import concourse.bass as bass
from concourse import mybir

ALU = mybir.AluOpType
ACT = mybir.ActivationFunctionType
AX = mybir.AxisListType
F32 = mybir.dt.float32
BF16 = mybir.dt.bfloat16
FP16 = mybir.dt.float16
I32 = mybir.dt.int32
U32 = mybir.dt.uint32

N, D, E = 625, 256, 20000
P, T = 125, 5
K2 = D // 128
CHUNKS = [(0, 375, (0, 1, 2)), (375, 250, (3, 4))]
H = 4
HD = D // H
EC = E // P
G = 5
NG = EC // G
NBLK = 8
DH = D // NBLK
KR = 4
FF = 4 * D
NE0, HID0 = 16, 512
NE1, HID1 = 8, 682
HT1 = [(m * 128, min(128, HID1 - m * 128)) for m in range((HID1 + 127) // 128)]
BIG = 1e30
OH = N + 1
BANKS = 8

VECS = [["att", "g_bias", "g_gamma", "g_beta", "ln1_g", "ln1_b", "bo", "ln2_g", "ln2_b", "b2"],
        ["bv", "bskip", "wg_skip", "wg_rst", "wg_diff", "ln_w", "ln_b", "kln_w", "kln_b", "vln_w", "vln_b",
         "rms1", "rms2"]]
V_GATEB = len(VECS[0]) * D
V_SIZE0 = V_GATEB + NE0
V_BGATE = len(VECS[1]) * D
V_PRELU = V_BGATE + 1
V_SIZE = V_PRELU + 1
FB_BX, FB_B1, FB_BQ, FB_BK, FB_SIZE = 0, 2, 10, 12, 14
WCOLS = [[("lr", 512), ("wx", 256), ("wo", 256), ("w1", FF), ("gate0", NE0)],
         [("gq", 256), ("gk", 256), ("gvs", 512), ("aq", 256), ("aqr", 256), ("ak", 256), ("akr", 256), ("av", 128),
          ("ao", 256), ("gate1", NE1)]]
WOFF, W_SIZES = {}, []
for _layer in WCOLS:
    _at = 0
    for _n, _c in _layer:
        WOFF[_n] = (_at, _c)
        _at += _c
    W_SIZES.append(_at)
HT0 = [(m * 128, 128) for m in range(HID0 // 128)]
EXP0 = 2 * 2 * HID0 + (HID0 // 128) * D
EXP1 = 2 * 2 * HID1 + (HID1 // 128) * D


class Chain:

    def __init__(self, eng, sem, base=0):
        self.eng, self.sem, self.base, self.n = eng, sem, base, 0

    def note(self, ins):
        self.n += 1
        return ins.then_inc(self.sem, 1)

    def fence(self):
        self.eng.wait_ge(self.sem, self.base + self.n)

    def link(self, ins):
        self.note(ins)
        self.fence()


ARENA = 18436


def build(nc, x_in, src_in, dst_in, vec0_in, vec1_in, fb_in, w0_in, w1_in, w2_in, mixw_in, exp0_in, exp1_in,
          exp1r_in, rope_in, out):
    ctx = ExitStack()
    with ctx:
        sems = {}

        def sem(name):
            if name not in sems:
                sems[name] = ctx.enter_context(nc.semaphore(name))
            return sems[name]

        def sb(name, shape, dt=F32):
            return ctx.enter_context(nc.sbuf_tensor(name, shape, dt))

        xl_tab = nc.dram_tensor("xl_tab", [N, D], F32).ap()
        xr_tab = nc.dram_tensor("xr_tab", [N, D], F32).ap()
        pair_scores = nc.dram_tensor("pair_scores", [N * N, H], F32).ap()

        vec = sb("vec", [P, V_SIZE])
        fbias = sb("fbias", [128, FB_SIZE])
        wres = sb("wres", [128, K2, max(W_SIZES)])
        mixw = sb("mixw", [128, 4, KR + DH])
        mixk = sb("mixk", [128, K2, NBLK * KR])
        ident = sb("ident", [128, 128])
        lower = sb("lower", [P, N])
        block4 = sb("block4", [NBLK * KR, D])
        block32 = sb("block32", [128, 128])
        iota_n = sb("iota_n", [P, OH], FP16)
        iota_e = sb("iota_e", [P, NE0])
        zero16 = sb("zero16", [1, 512], BF16)
        x, xn, ta, tb, tc, td, te = (sb(n, [P, T, D]) for n in ("x", "xn", "ta", "tb", "tc", "td", "te"))
        xlr = sb("xlr", [P, T, 2 * D])
        fa, fb_, fc, fd = (sb(n, [128, K2, N]) for n in ("fa", "fb", "fc", "fd"))
        kvbd = sb("kvbd", [NBLK * KR, D])
        ckv = sb("ckv", [128, K2, 128])
        stats, mv, rstd = sb("stats", [P, T, 6]), sb("mv", [P, T, 2]), sb("rstd", [P, T])
        hstat = sb("hstat", [P, 4, T * NBLK])
        root = sb("root", [P, 3, T * NBLK])
        kstat = sb("kstat", [NBLK * KR, 3])
        lg, pr = sb("lg", [P, T, NE0]), sb("pr", [P, T, NE0])
        rmax, rsum, rinv = sb("rmax", [P, T]), sb("rsum", [P, T]), sb("rinv", [P, T])
        top8, topi, topf = sb("top8", [P, T, 8]), sb("topi", [P, T, 8], U32), sb("topf", [P, T, 8])
        wtop = sb("wtop", [P, T, 2])
        disp, disp2 = sb("disp", [P, T, NE0]), sb("disp2", [P, T, NE0])
        gpart, gate = sb("gpart", [P, 3, T]), sb("gate", [P, T])
        rmx, rneg, rden, rrec = (sb(n, [P, T * H]) for n in ("rmx", "rneg", "rden", "rrec"))
        rmx_a = sb("rmx_a", [P, T * H])
        srci, dsti, celli = (sb(n, [P, EC], I32) for n in ("srci", "dsti", "celli"))
        srcf, dstf, cellf = (sb(n, [P, EC]) for n in ("srcf", "dstf", "cellf"))
        idx_ring = sb("idx_ring", [P, 4, 3, G], I32)
        sc_ring = sb("sc_ring", [P, 2, G, H])
        cnt = sb("cnt", [P, T, N])
        nmask = sb("nmask", [P, T, N], BF16)

        arena = sb("arena", [128, ARENA])
        gat = arena[0:P, 0:4 * G * D].rearrange("p (s w c) -> p s w c", s=2, w=2)
        at = 4 * G * D
        oh = arena[0:P, at:at + 2 * G * OH].bitcast(BF16).rearrange("p (s w g n) -> p s w g n", s=2, w=2, g=G)
        at += 2 * G * OH
        w2 = arena[:, at:at + FF // 128 * D].rearrange("p (k n) -> p k n", n=D)
        at += FF // 128 * D
        mlp = arena[:, at:at + FF // 128 * N].rearrange("p (k n) -> p k n", n=N)
        assert at + FF // 128 * N <= ARENA
        sdense = arena[0:P, 0:2 * H * N].rearrange("p (s n h) -> p s n h", s=2, h=H)
        at = 2 * H * N
        masked, expd, prob, probT = (arena[0:P, at + i * 3 * N:at + (i + 1) * 3 * N].rearrange("p (s n) -> p s n", s=3)
                                     for i in range(4))
        at += 12 * N
        rope = arena[:, at:at + 2 * N].rearrange("p (w n) -> p w n", w=2)
        assert at + 2 * N <= ARENA
        exw = arena[:, 0:2 * EXP1].rearrange("p (s n) -> p s n", s=2)
        at = 2 * EXP1
        hid = arena[:, at:at + 12 * N].rearrange("p (s m n) -> p s m n", s=2, m=6)
        at += 12 * N
        silu = arena[:, at:at + 2 * 376].rearrange("p (s n) -> p s n", s=2)
        at += 2 * 376
        exw_r = arena[0:HID1 % 128, at:at + 2 * D].rearrange("p (s n) -> p s n", s=2)
        assert at + 2 * D <= ARENA

        banks = [ctx.enter_context(nc.psum_tensor(f"bank{b}", [128, 512], F32)) for b in range(BANKS)]
        full = [sem(f"full{b}") for b in range(BANKS)]
        free = [sem(f"free{b}") for b in range(BANKS)]
        uses = [0] * BANKS
        fulls = [0] * BANKS
        ring = {"at": 0, "n": BANKS}
        ticket = {}

        def V(layer, name):
            i = VECS[layer].index(name) * D
            return vec[:, i:i + D].unsqueeze(1).to_broadcast([P, T, D])

        def Vt(layer, name, width=D):
            i = VECS[layer].index(name) * D
            return vec[:, i:i + width]

        def W(name, k):
            o, c = WOFF[name]
            return wres[:, k, o:o + c]

        def got(eng, name):
            b, n, _ = ticket[name if isinstance(name, tuple) else (name,)]
            eng.wait_ge(full[b], n)
            return banks[b], free[b]

        def read_out(eng, *key):
            last = {}
            for name, (b, _, n) in ticket.items():
                if name[:len(key)] == key:
                    last[b] = max(last.get(b, 0), n)
            assert last, key
            for b, n in last.items():
                eng.wait_ge(free[b], n)

        steps = [(m, h) for m in range(T) for h in range(H)]
        causal_tiles = lambda m: m + 1
        all_tiles = lambda m: T

        def chunks_upto(ns):
            found = []
            for c, (off, w, tiles) in enumerate(CHUNKS):
                tiles = [t for t in tiles if t < ns]
                if tiles:
                    found.append((c, off, len(tiles) * P, tiles))
            return found

        block = ctx.enter_context(nc.Block())

        @block.tensor
        def _(pe):
            def group(name):
                b = ring["at"] % ring["n"]
                ring["at"] += 1
                return bank_for(name, b)

            def bank_for(name, b):
                if uses[b]:
                    pe.wait_ge(free[b], uses[b])
                uses[b] += 1
                fulls[b] += 1
                ticket[name if isinstance(name, tuple) else (name,)] = (b, fulls[b], uses[b])
                return banks[b], full[b]

            def all_free():
                for b in range(BANKS):
                    pe.wait_ge(free[b], uses[b])

            def to_fm(name, src):
                for k in range(K2):
                    for c, (off, w, tiles) in enumerate(CHUNKS):
                        bank, done = group((name, k, c))
                        for t in tiles:
                            mm = pe.transpose(bank[:, t * P - off:t * P - off + P],
                                              src[:, t, k * 128:(k + 1) * 128], ident[0:P, 0:P])
                        mm.then_inc(done, 1)

            def linear_tm(name, f, rhs, width, ks=K2):
                for t in range(T):
                    bank, done = group((name, t))
                    for k in range(ks):
                        mm = pe.matmul(bank[0:P, 0:width], f[:, k, t * P:(t + 1) * P], rhs(k),
                                       start=(k == 0), stop=(k == ks - 1))
                    mm.then_inc(done, 1)

            def linear_fm(name, f, weights, m_tiles, ks=K2):
                for m in range(m_tiles):
                    for c, (off, w, _) in enumerate(CHUNKS):
                        bank, done = group((name, m, c))
                        for k in range(ks):
                            mm = pe.matmul(bank[:, 0:w], W(weights, k)[:, m * 128:(m + 1) * 128],
                                           f[:, k, off:off + w], start=(k == 0), stop=(k == ks - 1))
                        mm.then_inc(done, 1)

            pe.wait_ge(sem("ident"), 2)
            pe.wait_ge(sem("xn0"), T)
            to_fm("xnT0", xn)
            pe.wait_ge(sem("w0_in"), 16)
            read_out(pe, "xnT0")
            linear_tm("lr", fa, lambda k: W("lr", k), 2 * D)

            pe.wait_ge(sem("mixh"), 1)
            to_fm("mixhT", ta)
            read_out(pe, "mixhT")
            linear_fm("xm", fb_, "wx", K2)
            read_out(pe, "xm")
            pe.wait_ge(sem("mixw_in"), 12 * 16)
            for t in range(T):
                bank, done = group(("qv", t))
                for k in range(K2):
                    mm = pe.matmul(bank[0:P, k * 144:k * 144 + 144], fc[:, k, t * P:(t + 1) * P],
                                   mixw[:, :, :].rearrange("p a b -> p (a b)"), start=True, stop=True)
                mm.then_inc(done, 1)
            for c, (off, w, _) in enumerate(CHUNKS):
                bank, done = group(("kT", c))
                for k in range(K2):
                    mm = pe.matmul(bank[0:32, 0:w], mixk[:, k, :], fc[:, k, off:off + w],
                                   start=(k == 0), stop=(k == 1))
                mm.then_inc(done, 1)
            pe.wait_ge(sem("ksoft"), 1)
            bank, done = group("kN")
            for t in range(T):
                mm = pe.transpose(bank[0:P, t * 32:t * 32 + 32], fd[0:32, 0, t * P:(t + 1) * P], ident[0:32, 0:32])
            mm.then_inc(done, 1)
            pe.wait_ge(sem("qsoft"), 1)
            for c, (off, w, tiles) in enumerate(CHUNKS):
                bank, done = group(("qT", c))
                for t in tiles:
                    mm = pe.transpose(bank[0:32, t * P - off:t * P - off + P], te[:, t, 0:32], ident[0:P, 0:P])
                mm.then_inc(done, 1)
            read_out(pe, "kN")
            read_out(pe, "qv")
            bank, done = group("kv")
            for t in range(T):
                mm = pe.matmul(bank[0:32, 0:D], te[:, t, 32:64], td[:, t, :], start=(t == 0), stop=(t == T - 1))
            mm.then_inc(done, 1)
            read_out(pe, "kv")
            read_out(pe, "qT")
            for m in range(K2):
                for c, (off, w, _) in enumerate(CHUNKS):
                    bank, done = group(("qkv", m, c))
                    pe.matmul(bank[:, 0:w], kvbd[:, m * 128:(m + 1) * 128], fd[0:32, 1, off:off + w],
                              start=True, stop=True).then_inc(done, 1)
            read_out(pe, "qkv")
            linear_tm("attn", fb_, lambda k: W("wo", k), D)
            pe.wait_ge(sem("h2"), 1)
            to_fm("h2T", ta)
            read_out(pe, "h2T")
            linear_fm("m1", fb_, "w1", FF // 128)
            read_out(pe, "m1")
            pe.wait_ge(sem("w2_in"), 16)
            linear_tm("m2", mlp, lambda k: w2[:, k, :], D, ks=FF // 128)

            REST = N - 512
            all_free()
            pe.wait_ge(sem("zero16"), 1)

            def zeros(first):
                for m in range(T):
                    pe.matmul(banks[m][0:P, 0:512], zero16[0:1, 0:P], zero16[0:1, 0:512], start=first, stop=not first,
                              skip_group_check=True)
                pe.matmul(banks[5][0:P, 0:4 * REST], zero16[0:1, 0:P], zero16[0:1, 0:4 * REST], start=first,
                          stop=not first, skip_group_check=True)
                return pe.matmul(banks[6][0:P, 0:REST], zero16[0:1, 0:P], zero16[0:1, 0:REST], start=first,
                                 stop=not first, skip_group_check=True)

            zeros(True)
            with pe.Fori(0, NG // 4) as i:
                for b in range(4):
                    s = b % 2
                    pe.wait_ge(sem("onehot"), i * 4 + (b + 1))
                    for j in range(G):
                        for m in range(T):
                            lhsT = oh[:, s, 1, j, m * P:(m + 1) * P]
                            pe.matmul(banks[m][0:P, 0:512], lhsT, oh[:, s, 0, j, 0:512], start=False, stop=False,
                                      skip_group_check=True)
                            rest = banks[5][0:P, m * REST:(m + 1) * REST] if m < 4 else banks[6][0:P, 0:REST]
                            mm = pe.matmul(rest, lhsT, oh[:, s, 0, j, 512:N], start=False, stop=False,
                                           skip_group_check=True)
                    mm.then_inc(sem("onehot_used"), 1)
            zeros(False).then_inc(sem("counted"), 1)
            pe.wait_ge(sem("counts_out"), 1)

            def attend(name, scores, v_rows, tiles_of):
                ring["n"] = 6

                def turn(i):
                    pe.wait_ge(sem(name + "_prob"), i + 1)
                    for c, off, w, tiles in chunks_upto(tiles_of(steps[i][0])):
                        bank, done = group((name, "pT", i, c))
                        for t in tiles:
                            mm = pe.transpose(bank[0:P, t * P - off:t * P - off + P],
                                              prob[:, i % 3, t * P:(t + 1) * P], ident[0:P, 0:P])
                        mm.then_inc(done, 1)

                def sum_v(i):
                    m, h = steps[i]
                    b = 6 + m % 2
                    if h == 0 and uses[b]:
                        pe.wait_ge(free[b], uses[b])
                    read_out(pe, name, "pT", i)
                    for t in range(tiles_of(m)):
                        mm = pe.matmul(banks[b][0:P, h * HD:(h + 1) * HD], probT[:, i % 3, t * P:(t + 1) * P],
                                       v_rows(t, h), start=(t == 0), stop=(t == tiles_of(m) - 1))
                    mm.then_inc(sem(name + "_sum"), 1)
                    if h == H - 1:
                        uses[b] += 1
                        ticket[(name, "agg", m)] = (b, 0, uses[b])

                for i in range(len(steps) + 2):
                    if i < len(steps) and scores:
                        scores(i, *steps[i])
                    if 1 <= i <= len(steps):
                        turn(i - 1)
                    if i >= 2:
                        sum_v(i - 2)
                ring["n"] = BANKS

            attend("l0", None, lambda t, h: xlr[:, t, h * HD:(h + 1) * HD], all_tiles)

            def experts(name, f, n_exp, loads, hts, w_in, w_out):
                all_free()
                units = 2 * len(hts)

                def hidden(e, s):
                    pe.wait_ge(sem(f"{name}_w{s}"), ((e - s) * 8 + 16) * loads)
                    for m, (mo, mw) in enumerate(hts):
                        for c, (off, w, _) in enumerate(CHUNKS):
                            u = m * 2 + c
                            if not (isinstance(e, int) and e == 0 and u < 2):
                                pe.wait_ge(sem(name + "_mul"), e * units + (u - 1))
                            for q in range(2):
                                for k in range(K2):
                                    mm = pe.matmul(banks[2 * c + q][0:mw, 0:w], w_in(s, q, k, mo, mw),
                                                   f[:, k, off:off + w], start=(k == 0), stop=(k == 1))
                            mm.then_inc(sem(name + "_hid"), 1)

                def output(e, s):
                    pe.wait_ge(sem(name + "_mul"), (e + 1) * units)
                    for t in range(T):
                        if t == 0 and not (isinstance(e, int) and e == 0):
                            pe.wait_ge(sem(name + "_acc"), e * T)
                        if t == 4:
                            pe.wait_ge(sem(name + "_acc"), e * T + 1)
                        for m, (mo, mw) in enumerate(hts):
                            mm = pe.matmul(banks[4 + t % 4][0:P, 0:D], hid[0:mw, s, m, t * P:(t + 1) * P],
                                           w_out(s, m), start=(m == 0), stop=(m == len(hts) - 1))
                        mm.then_inc(sem(name + "_out"), 1)

                hidden(0, 0)
                hidden(1, 1)
                output(0, 0)
                with pe.Fori(1, n_exp // 2) as i:
                    hidden(i * 2, 0)
                    output(i * 2 - 1, 1)
                    hidden(i * 2 + 1, 1)
                    output(i * 2, 0)
                output(n_exp - 1, 1)

            pe.wait_ge(sem("xn1"), T)
            to_fm("xnT1", xn)
            read_out(pe, "xnT1")
            linear_tm("gate0", fa, lambda k: W("gate0", k), NE0)
            experts("e0", fa, NE0, 1, HT0,
                    lambda s, q, k, mo, mw: exw[:, s, (q * 2 + k) * HID0 + mo:(q * 2 + k) * HID0 + mo + mw],
                    lambda s, m: exw[:, s, 4 * HID0 + m * D:4 * HID0 + (m + 1) * D])

            pe.wait_ge(sem("e0_acc"), NE0 * T)
            pe.wait_ge(sem("xn2"), T)
            to_fm("xnT2", xn)
            read_out(pe, "xnT2")
            pe.wait_ge(sem("w1_in"), 16)
            linear_fm("gq", fa, "gq", K2)
            linear_fm("gk", fa, "gk", K2)
            linear_tm("gvs", fa, lambda k: W("gvs", k), 2 * D)
            pe.wait_ge(sem("cmix"), 1)
            for k in range(K2):
                bank, done = group(("ckv", k))
                for t in range(T):
                    mm = pe.matmul(bank[:, 0:128], ta[:, t, k * 128:(k + 1) * 128], tb[:, t, k * 128:(k + 1) * 128],
                                   start=(t == 0), stop=(t == T - 1))
                mm.then_inc(done, 1)
            read_out(pe, "ckv")
            for t in range(T):
                bank, done = group(("cout", t))
                for k in range(K2):
                    mm = pe.matmul(bank[0:P, k * 128:(k + 1) * 128], fa[:, k, t * P:(t + 1) * P], ckv[:, k, :],
                                   start=True, stop=True)
                mm.then_inc(done, 1)
            read_out(pe, "gq")
            read_out(pe, "gk")
            read_out(pe, "gvs")

            def l1_scores(i, m, h):
                r, k = (h % 2) * HD, h // 2
                for c, (off, w, _) in enumerate(CHUNKS):
                    bank, done = group(("l1", "s", i, c))
                    pe.matmul(bank[0:P, 0:w], fc[r:r + HD, k, m * P:(m + 1) * P], fb_[r:r + HD, k, off:off + w],
                              start=True, stop=True).then_inc(done, 1)

            attend("l1", l1_scores, lambda t, h: xlr[:, t, h * HD:(h + 1) * HD], all_tiles)

            pe.wait_ge(sem("ah"), 1)
            to_fm("ahT", ta)
            read_out(pe, "ahT")
            for name in ("aq", "aqr", "ak", "akr"):
                linear_fm(name, fa, name, K2)
            linear_tm("av", fa, lambda k: W("av", k), 128)
            pe.wait_ge(sem("roped"), 8)
            read_out(pe, "av")

            def l2_scores(i, m, h):
                r, g = (h % 2) * HD, h // 2
                for c, off, w, _ in chunks_upto(m + 1):
                    bank, done = group(("l2", "s", i, c))
                    pe.matmul(bank[0:P, 0:w], fb_[r:r + HD, g, m * P:(m + 1) * P], fc[r:r + HD, g, off:off + w],
                              start=True, stop=True).then_inc(done, 1)

            attend("l2", l2_scores, lambda t, h: td[:, t, (h // 2) * HD:(h // 2 + 1) * HD], causal_tiles)
            read_out(pe, "l2", "agg")
            to_fm("yT", te)
            read_out(pe, "yT")
            linear_tm("ao", fa, lambda k: W("ao", k), D)

            pe.wait_ge(sem("flat"), 1)
            to_fm("flatT", ta)
            read_out(pe, "flatT")
            linear_tm("gate1", fa, lambda k: W("gate1", k), NE1)
            experts("e1", fa, NE1, 2, HT1,
                    lambda s, q, k, mo, mw: exw[:, s, (q * 2 + k) * HID1 + mo:(q * 2 + k) * HID1 + mo + mw],
                    lambda s, m: exw_r[:, s, :] if m == 5 else exw[:, s, 4 * HID1 + m * D:4 * HID1 + (m + 1) * D])

        @block.vector
        def _(dve):
            own = Chain(dve, sem("dve_own"))
            v = nc.vector

            def inverse_root(dst, src, times, plus):
                n = dst.shape[1]
                val, bits, sq = root[:, 0, 0:n], root[:, 1, 0:n], root[:, 2, 0:n]
                own.link(v.tensor_scalar(val, src, times, plus, ALU.mult, ALU.add))
                own.link(v.tensor_scalar(bits.bitcast(I32), val.bitcast(I32), 1, None, ALU.logical_shift_right))
                own.link(v.tensor_scalar(dst.bitcast(I32), bits.bitcast(I32), -1.0, float(0x5F3759DF), ALU.mult,
                                         ALU.add))
                for _ in range(3):
                    own.link(v.tensor_tensor(sq, dst, dst, ALU.mult))
                    own.link(v.scalar_tensor_tensor(sq, sq, -0.5, val, ALU.mult, ALU.mult))
                    own.link(v.scalar_tensor_tensor(dst, sq, 1.5, dst, ALU.add, ALU.mult))

            def layernorm(src, dst, eps, done):
                for t in range(T):
                    own.note(v.bn_stats(stats[:, t, :], src[:, t, :]))
                own.fence()
                for t in range(T):
                    own.note(v.bn_aggr(mv[:, t, :], stats[:, t, :]))
                own.fence()
                inverse_root(rstd[:, :], mv[:, :, 1], 1.0, eps)
                for t in range(T):
                    v.tensor_scalar(dst[:, t, :], src[:, t, :], mv[:, t, 0:1], rstd[:, t:t + 1], ALU.subtract,
                                    ALU.mult).then_inc(done[0], 1)
                dve.wait_ge(done[0], done[1])

            def affine(dst, layer, g, b, done):
                own.link(v.tensor_tensor(dst[:, :, :], dst[:, :, :], V(layer, g), ALU.mult))
                v.tensor_tensor(dst[:, :, :], dst[:, :, :], V(layer, b), ALU.add).then_inc(done, 1)

            def rmsnorm(src, dst, weight, junk, done):
                for t in range(T):
                    own.note(v.tensor_tensor_reduce(junk[:, t, :], src[:, t, :], src[:, t, :], 1.0 / D, 0.0, ALU.mult,
                                                    ALU.add, rsum[:, t:t + 1]))
                own.fence()
                inverse_root(rstd[:, :], rsum[:, :], 1.0, 1e-6)
                for t in range(T):
                    ins = v.scalar_tensor_tensor(dst[:, t, :], src[:, t, :], rstd[:, t:t + 1], Vt(1, weight), ALU.mult,
                                                 ALU.mult)
                ins.then_inc(done, 1)

            def from_fm(name, dst):
                for c, (off, w, _) in enumerate(CHUNKS):
                    bank, freed = got(dve, (name, 1, c))
                    v.tensor_copy(dst[:, 1, off:off + w], bank[:, 0:w]).then_inc(freed, 1)

            dve.wait_ge(sem("x_in"), 16)
            layernorm(x, xn, 1e-5, (sem("xn0"), T))
            v.memset(zero16[:, :], 0.0).then_inc(sem("zero16"), 1)
            v.memset(cnt[:, :, :], 0.0).then_inc(sem("zeros"), 1)
            own.note(v.memset(mixw[:, :, :], 0.0))
            v.memset(mixk[:, :, :], 0.0).then_inc(sem("mixw0"), 1)
            from_fm("xnT0", fa)
            for t in range(T):
                bank, freed = got(dve, ("lr", t))
                v.tensor_copy(xlr[:, t, :], bank[0:P, :]).then_inc(freed, 1)
            dve.wait_ge(sem("edges_in"), 32)
            own.note(v.tensor_copy(srcf[:, :], srci[:, :]))
            own.note(v.tensor_copy(dstf[:, :], dsti[:, :]))
            own.fence()
            own.link(v.scalar_tensor_tensor(cellf[:, :], dstf[:, :], float(N), srcf[:, :], ALU.mult, ALU.add))
            own.link(v.tensor_copy(celli[:, :], cellf[:, :]))

            layernorm(xn, ta, 1e-5, (sem("ln1"), T))
            dve.wait_ge(sem("vec0_in"), 16)
            affine(ta, 0, "ln1_g", "ln1_b", sem("mixh"))
            own.note(v.tensor_tensor(tb[:, :, :], xn[:, :, :], V(0, "bo"), ALU.add))
            from_fm("mixhT", fb_)
            dve.wait_ge(sem("fb_in"), 16)
            for c, (off, w, _) in enumerate(CHUNKS):
                bank, freed = got(dve, ("xm", 1, c))
                v.tensor_scalar(fc[:, 1, off:off + w], bank[:, 0:w], fbias[:, FB_BX + 1:FB_BX + 2], None, ALU.add)\
                    .then_inc(freed, 1)
            for t in range(T):
                bank, freed = got(dve, ("qv", t))
                qv = bank[0:P, 0:288].rearrange("p (h c) -> p h c", h=NBLK)
                own.note(v.tensor_copy(te[:, t, 0:32].rearrange("p (h r) -> p h r", h=NBLK), qv[:, :, 0:KR]))
                v.tensor_copy(td[:, t, :].rearrange("p (h c) -> p h c", h=NBLK), qv[:, :, KR:KR + DH])\
                    .then_inc(freed, 1)
            for c, (off, w, _) in enumerate(CHUNKS):
                bank, freed = got(dve, ("kT", c))
                v.tensor_copy(fd[0:32, 0, off:off + w], bank[0:32, 0:w]).then_inc(freed, 1)
            read_out(dve, "kT")
            own.link(v.tensor_reduce(kstat[:, 0:1], fd[0:32, 0, :], AX.X, ALU.max))
            v.tensor_scalar(kstat[:, 1:2], kstat[:, 0:1], -1.0, None, ALU.mult).then_inc(sem("kmax"), 1)
            own.fence()
            q4 = te[:, :, 0:32].rearrange("p t (h r) -> p t h r", h=NBLK)
            qst = hstat[:, 0, :].rearrange("p (t h) -> p t h", t=T)
            qsu = hstat[:, 1, :].rearrange("p (t h) -> p t h", t=T)

            def spread(a):
                return a.unsqueeze(3).to_broadcast([P, T, NBLK, KR])

            own.link(v.tensor_reduce(qst, q4, AX.X, ALU.max))
            v.tensor_tensor(q4, q4, spread(qst), ALU.subtract).then_inc(sem("qshift"), 1)
            dve.wait_ge(sem("kexp"), 1)
            own.link(v.reciprocal(kstat[:, 0:1], kstat[:, 2:3]))
            v.tensor_scalar(fd[0:32, 0, :], fd[0:32, 0, :], kstat[:, 0:1], None, ALU.mult).then_inc(sem("ksoft"), 1)
            dve.wait_ge(sem("qexp"), 1)
            own.link(v.tensor_reduce(qst, q4, AX.X, ALU.add))
            own.link(v.reciprocal(qsu, qst))
            v.tensor_tensor(q4, q4, spread(qsu), ALU.mult).then_inc(sem("qsoft"), 1)
            bank, freed = got(dve, "kN")
            v.tensor_copy(te[:, :, 32:64], bank[0:P, 0:160].rearrange("p (t r) -> p t r", t=T))\
                .then_inc(freed, 1)
            for c, (off, w, _) in enumerate(CHUNKS):
                bank, freed = got(dve, ("qT", c))
                v.tensor_copy(fd[0:32, 1, off:off + w], bank[0:32, 0:w]).then_inc(freed, 1)
            bank, freed = got(dve, "kv")
            dve.wait_ge(sem("blocks"), 1)
            v.tensor_tensor(kvbd[:, :], bank[0:32, 0:D], block4[:, :], ALU.mult)\
                .then_inc(freed, 1)
            for c, (off, w, _) in enumerate(CHUNKS):
                bank, freed = got(dve, ("qkv", 1, c))
                v.tensor_copy(fb_[:, 1, off:off + w], bank[:, 0:w]).then_inc(freed, 1)
            for t in range(T):
                bank, freed = got(dve, ("attn", t))
                v.tensor_tensor(tb[:, t, :], bank[0:P, 0:D], tb[:, t, :], ALU.add).then_inc(freed, 1)
            read_out(dve, "attn")
            layernorm(tb, ta, 1e-5, (sem("ln2"), T))
            affine(ta, 0, "ln2_g", "ln2_b", sem("h2"))
            own.link(v.tensor_tensor(tb[:, :, :], tb[:, :, :], V(0, "b2"), ALU.add))
            from_fm("h2T", fb_)
            for t in range(T):
                bank, freed = got(dve, ("m2", t))
                v.tensor_tensor(tb[:, t, :], bank[0:P, 0:D], tb[:, t, :], ALU.add).then_inc(freed, 1)
            read_out(dve, "m2")

            def copy_indices(g, b):
                for w, a in enumerate((srci, dsti, celli)):
                    ins = v.tensor_copy(idx_ring[:, b % 4, w, :], a[:, bass.ds(g * G, G)])
                ins.then_inc(sem("indices"), 1)

            def edge_group(g, b, ch):
                s = b % 2
                static = isinstance(g, int)
                if not (static and g < 2):
                    dve.wait_ge(sem("onehot_used"), g - 1)
                for j in range(G):
                    for w, a in enumerate((srcf, dstf)):
                        ins = v.tensor_scalar(oh[:, s, w, j, :], iota_n[:, :], a[:, bass.ds(g * G + j, 1)], None,
                                              ALU.is_equal)
                ins.then_inc(sem("onehot"), 1)
                dve.wait_ge(sem(f"gathered{s}"), (g - s) * (G * 16) + 2 * G * 16)
                zl, zr = gat[:, s, 0, :], gat[:, s, 1, :]
                ch.link(v.tensor_tensor(zl, zl, zr, ALU.add))
                ch.link(v.scalar_tensor_tensor(zr, zl, 0.2, zl, ALU.mult, ALU.max))
                ch.link(v.tensor_tensor(zl.rearrange("p (g c) -> p g c", g=G), zr.rearrange("p (g c) -> p g c", g=G),
                                        Vt(0, "att").unsqueeze(1).to_broadcast([P, G, D]), ALU.mult))
                if not (static and g < 2):
                    dve.wait_ge(sem("scattered"), (g - 1) * (G * 16))
                v.tensor_reduce(sc_ring[:, s, :, :].rearrange("p g h -> p (g h)"),
                                zl.rearrange("p (a c) -> p a c", c=HD), AX.X, ALU.add).then_inc(sem("scored"), 1)
                if not (static and g + 2 >= NG):
                    copy_indices(g + 2, b + 2)

            dve.wait_ge(sem("iotas"), 2)
            copy_indices(0, 0)
            copy_indices(1, 1)
            ch = Chain(dve, sem("edge_own"))
            for b in range(4):
                edge_group(b, b, ch)
            per = ch.n
            with dve.Fori(1, NG // 4 - 1) as i:
                ch = Chain(dve, sem("edge_own"), i * per)
                for b in range(4):
                    edge_group(i * 4 + b, b, ch)
            ch = Chain(dve, sem("edge_own"), (NG // 4 - 1) * per)
            for b in range(4):
                edge_group(NG - 4 + b, b, ch)

            REST = N - 512
            dve.wait_ge(sem("counted"), 1)
            dve.wait_ge(sem("zeros_out"), T * 16)
            for m in range(T):
                own.note(v.tensor_copy(cnt[:, m, 0:512], banks[m][0:P, :]))
            own.note(v.tensor_copy(cnt[:, 0:4, 512:N], banks[5][0:P, 0:4 * REST].rearrange("p (m n) -> p m n", m=4)))
            v.tensor_copy(cnt[:, 4, 512:N], banks[6][0:P, 0:REST]).then_inc(sem("counts_out"), 1)
            own.fence()
            dve.wait_ge(sem("counts_out"), 1)
            own.link(v.tensor_scalar(nmask[:, :, :], cnt[:, :, :], 0.0, -BIG, ALU.is_equal, ALU.mult))

            def attend(name, take_scores, tiles_of, weigh, guard, dst):
                def maxima(i):
                    m, h = steps[i]
                    take_scores(i, m, h)
                    v.tensor_scalar(rneg[:, i:i + 1], rmx[:, i:i + 1], -1.0, None, ALU.mult)\
                        .then_inc(sem(name + "_max"), 1)

                def weights(i):
                    if not weigh:
                        return
                    m, h = steps[i]
                    dve.wait_ge(sem(name + "_exp"), i + 1)
                    if i >= 3:
                        read_out(dve, name, "pT", i - 3)
                    v.tensor_tensor_reduce(prob[:, i % 3, :], expd[:, i % 3, :], cnt[:, m, :], 1.0, 0.0, ALU.mult,
                                           ALU.add, rden[:, i:i + 1]).then_inc(sem(name + "_prob"), 1)

                def normalize(m):
                    cols = slice(m * H, (m + 1) * H)
                    dve.wait_ge(sem(name + "_prob"), (m + 1) * H)
                    own.link(guard(rrec[:, cols], rden[:, cols]))
                    own.link(v.reciprocal(rrec[:, cols], rrec[:, cols]))
                    dve.wait_ge(sem(name + "_sum"), (m + 1) * H)
                    b = 6 + m % 2
                    v.tensor_tensor(dst[:, m, :].rearrange("p (h c) -> p h c", h=H),
                                    banks[b][0:P, 0:D].rearrange("p (h c) -> p h c", h=H),
                                    rrec[:, cols].unsqueeze(2).to_broadcast([P, H, HD]), ALU.mult)\
                        .then_inc(free[b], 1)

                n = len(steps)
                for i in range(n + 1):
                    if i < n:
                        maxima(i)
                    if i >= 1:
                        weights(i - 1)
                    if i >= 6 and (i - 6) % H == 0:
                        normalize((i - 6) // H)
                normalize(T - 1)
                read_out(dve, name, "agg")

            def l0_take(i, m, h):
                dve.wait_ge(sem(f"sdense{m % 2}"), 16 * (m // 2 + 1))
                v.tensor_tensor_reduce(masked[:, i % 3, :], sdense[:, m % 2, :, h], nmask[:, m, :], 1.0, -3e38,
                                       ALU.add, ALU.max, rmx[:, i:i + 1]).then_inc(sem("l0_taken"), 1)
                dve.wait_ge(sem("l0_taken"), i + 1)

            def from_banks(name, mask, scale, tiles_of):
                def take(i, m, h):
                    parts = chunks_upto(tiles_of(m))
                    for c, off, w, _ in parts:
                        bank, freed = got(dve, (name, "s", i, c))
                        v.tensor_tensor_reduce(
                            masked[:, i % 3, off:off + w], bank[0:P, 0:w], mask(m, off, w), scale, -3e38,
                            ALU.add, ALU.max, (rmx if c == 0 else rmx_a)[:, i:i + 1]).then_inc(freed, 1)
                    read_out(dve, name, "s", i)
                    if len(parts) == 2:
                        own.link(v.tensor_tensor(rmx[:, i:i + 1], rmx[:, i:i + 1], rmx_a[:, i:i + 1], ALU.max))
                return take

            attend("l0", l0_take, all_tiles, True,
                   lambda o, a: v.tensor_scalar(o, a, 1e-16, None, ALU.add), te)
            own.link(v.tensor_tensor(te[:, :, :], te[:, :, :], V(0, "g_bias"), ALU.add))
            v.tensor_scalar(tc[:, :, :], te[:, :, :], 0.0, None, ALU.min).then_inc(sem("elu_min"), 1)
            dve.wait_ge(sem("elu_exp"), 1)
            own.link(v.scalar_tensor_tensor(te[:, :, :], te[:, :, :], 0.0, tc[:, :, :], ALU.max, ALU.add))
            own.link(v.scalar_tensor_tensor(te[:, :, :], te[:, :, :], -1.0, xn[:, :, :], ALU.add, ALU.add))
            layernorm(te, ta, 1e-5, (sem("ln_g0"), T))
            affine(ta, 0, "g_gamma", "g_beta", sem("g0"))
            dve.wait_ge(sem("g0"), 1)
            own.link(v.tensor_tensor(x[:, :, :], x[:, :, :], ta[:, :, :], ALU.add))
            own.link(v.tensor_tensor(x[:, :, :], x[:, :, :], tb[:, :, :], ALU.add))

            def route(name, ne, bias, eps, out_disp):
                for t in range(T):
                    bank, freed = got(dve, (name, t))
                    if bias is None:
                        ins = v.tensor_copy(lg[:, t, 0:ne], bank[0:P, 0:ne])
                    else:
                        ins = v.tensor_tensor(lg[:, t, 0:ne], bank[0:P, 0:ne], bias, ALU.add)
                    ins.then_inc(freed, 1)
                read_out(dve, name)
                wide = lambda a: a[:, :].unsqueeze(2).to_broadcast([P, T, ne])
                own.link(v.tensor_reduce(rmax[:, :], lg[:, :, 0:ne], AX.X, ALU.max))
                v.tensor_tensor(lg[:, :, 0:ne], lg[:, :, 0:ne], wide(rmax), ALU.subtract).then_inc(sem(name + "_sh"), 1)
                dve.wait_ge(sem(name + "_exp"), 1)
                own.link(v.tensor_reduce(rsum[:, :], pr[:, :, 0:ne], AX.X, ALU.add))
                own.link(v.reciprocal(rinv[:, :], rsum[:, :]))
                own.link(v.tensor_tensor(pr[:, :, 0:ne], pr[:, :, 0:ne], wide(rinv), ALU.mult))
                for t in range(T):
                    own.note(v.max(top8[:, t, :], pr[:, t, 0:ne]))
                own.fence()
                for t in range(T):
                    own.note(v.max_index(topi[:, t, :], top8[:, t, :], pr[:, t, 0:ne]))
                own.note(v.tensor_tensor(rsum[:, :], top8[:, :, 0], top8[:, :, 1], ALU.add))
                own.fence()
                own.note(v.tensor_copy(topf[:, :, :], topi[:, :, :]))
                own.link(v.tensor_scalar(rsum[:, :], rsum[:, :], eps, None, ALU.add))
                own.link(v.reciprocal(rinv[:, :], rsum[:, :]))
                own.link(v.tensor_tensor(wtop[:, :, :], top8[:, :, 0:2],
                                         rinv[:, :].unsqueeze(2).to_broadcast([P, T, 2]), ALU.mult))
                for t in range(T):
                    for j, d in enumerate((out_disp, disp2)):
                        own.note(v.tensor_scalar(d[:, t, 0:ne], iota_e[:, 0:ne], topf[:, t, j:j + 1],
                                                 wtop[:, t, j:j + 1], ALU.is_equal, ALU.mult))
                own.fence()
                own.link(v.tensor_tensor(out_disp[:, :, 0:ne], out_disp[:, :, 0:ne], disp2[:, :, 0:ne], ALU.add))

            def experts(name, n_exp, hts):
                units = 2 * len(hts)

                def multiply(e, s):
                    if not (isinstance(e, int) and e < 2):
                        dve.wait_ge(sem(name + "_out"), (e - 1) * T)
                    for m, (mo, mw) in enumerate(hts):
                        for c, (off, w, _) in enumerate(CHUNKS):
                            dve.wait_ge(sem(name + "_silu"), e * units + (m * 2 + c + 1))
                            v.tensor_tensor(hid[0:mw, s, m, off:off + w], banks[2 * c + 1][0:mw, 0:w],
                                            silu[0:mw, c, 0:w], ALU.mult).then_inc(sem(name + "_mul"), 1)

                def accumulate(e):
                    for t in range(T):
                        dve.wait_ge(sem(name + "_out"), e * T + (t + 1))
                        if not (isinstance(e, int) and e == 0):
                            dve.wait_ge(sem(name + "_acc"), (e - 1) * T + (t + 1))
                        v.scalar_tensor_tensor(x[:, t, :], banks[4 + t % 4][0:P, 0:D], disp[:, t, bass.ds(e, 1)],
                                               x[:, t, :], ALU.mult, ALU.add).then_inc(sem(name + "_acc"), 1)

                multiply(0, 0)
                multiply(1, 1)
                accumulate(0)
                with dve.Fori(1, n_exp // 2) as i:
                    multiply(i * 2, 0)
                    accumulate(i * 2 - 1)
                    multiply(i * 2 + 1, 1)
                    accumulate(i * 2)
                accumulate(n_exp - 1)
                dve.wait_ge(sem(name + "_acc"), n_exp * T)

            layernorm(x, xn, 1e-5, (sem("xn1"), T))
            from_fm("xnT1", fa)
            route("gate0", NE0, vec[:, V_GATEB:V_GATEB + NE0], 0.0, disp)
            v.memset(rmx[:, :], 0.0).then_inc(sem("layer0_read"), 1)
            experts("e0", NE0, HT0)

            layernorm(x, xn, 1e-5, (sem("xn2"), T))
            heads = lambda a: a[:, :, :].rearrange("p t (h c) -> p (t h) c", h=NBLK)
            hb = lambda r: hstat[:, r, :].unsqueeze(2).to_broadcast([P, T * NBLK, DH])
            own.link(v.tensor_reduce(hstat[:, 0, :], heads(xn), AX.X, ALU.add))
            own.link(v.tensor_scalar(hstat[:, 0, :], hstat[:, 0, :], 1.0 / DH, None, ALU.mult))
            own.link(v.tensor_tensor(heads(ta), heads(xn), hb(0), ALU.subtract))
            own.link(v.tensor_tensor(tb[:, :, :], ta[:, :, :], ta[:, :, :], ALU.mult))
            own.link(v.tensor_reduce(hstat[:, 1, :], heads(tb), AX.X, ALU.add))
            inverse_root(hstat[:, 2, :], hstat[:, 1, :], 1.0 / (DH - 1), 0.0)
            own.link(v.scalar_tensor_tensor(hstat[:, 1, :], hstat[:, 1, :], 1.0 / (DH - 1), hstat[:, 2, :], ALU.mult,
                                            ALU.mult))
            own.link(v.tensor_scalar(hstat[:, 1, :], hstat[:, 1, :], 1e-5, None, ALU.add))
            own.link(v.reciprocal(hstat[:, 2, :], hstat[:, 1, :]))
            own.link(v.tensor_tensor(heads(ta), heads(ta), hb(2), ALU.mult))
            dve.wait_ge(sem("vec1_in"), 16)
            own.link(v.tensor_tensor(tb[:, :, :], ta[:, :, :], V(1, "vln_w"), ALU.mult))
            own.link(v.tensor_tensor(tb[:, :, :], tb[:, :, :], V(1, "vln_b"), ALU.add))
            affine(ta, 1, "kln_w", "kln_b", sem("cmix"))
            from_fm("xnT2", fa)
            for name, f, bias in (("gq", fb_, FB_BQ), ("gk", fc, FB_BK)):
                for c, (off, w, _) in enumerate(CHUNKS):
                    bank, freed = got(dve, (name, 1, c))
                    v.tensor_scalar(f[:, 1, off:off + w], bank[:, 0:w], fbias[:, bias + 1:bias + 2], None, ALU.add)\
                        .then_inc(freed, 1)
            for t in range(T):
                bank, freed = got(dve, ("gvs", t))
                v.tensor_tensor(xlr[:, t, :], bank[0:P, :], Vt(1, "bv", 2 * D), ALU.add)\
                    .then_inc(freed, 1)
            for k in range(K2):
                bank, freed = got(dve, ("ckv", k))
                v.scalar_tensor_tensor(ckv[:, k, :], bank[:, 0:128], 1.0 / N, block32[:, :], ALU.mult, ALU.mult)\
                    .then_inc(freed, 1)
            for t in range(T):
                bank, freed = got(dve, ("cout", t))
                v.tensor_tensor(tc[:, t, :], bank[0:P, 0:D], xn[:, t, :], ALU.add).then_inc(freed, 1)
            attend("l1", from_banks("l1", lambda m, off, w: nmask[:, m, off:off + w], HD ** -0.5, all_tiles),
                   all_tiles, True, lambda o, a: v.tensor_scalar(o, a, 1e-30, None, ALU.max), te)
            own.link(v.tensor_tensor(ta[:, :, :], xlr[:, :, D:2 * D], te[:, :, :], ALU.subtract))
            for j, (a, w) in enumerate(((xlr[:, :, D:2 * D], "wg_skip"), (te, "wg_rst"), (ta, "wg_diff"))):
                for t in range(T):
                    own.note(v.tensor_tensor_reduce(tb[:, t, :], a[:, t, :], Vt(1, w), 1.0, 0.0, ALU.mult, ALU.add,
                                                    gpart[:, j, t:t + 1]))
                own.fence()
            own.link(v.tensor_tensor(gate[:, :], gpart[:, 0, :], gpart[:, 1, :], ALU.add))
            v.tensor_tensor(gate[:, :], gate[:, :], gpart[:, 2, :], ALU.add).then_inc(sem("glogit"), 1)
            dve.wait_ge(sem("gated"), 1)
            for t in range(T):
                own.note(v.scalar_tensor_tensor(te[:, t, :], ta[:, t, :], gate[:, t:t + 1], te[:, t, :], ALU.mult,
                                                ALU.add))
            own.fence()
            layernorm(te, ta, 1e-5, (sem("ln_g1"), T))
            affine(ta, 1, "ln_w", "ln_b", sem("g1"))
            dve.wait_ge(sem("g1"), 1)
            own.link(v.tensor_scalar(te[:, :, :], ta[:, :, :], 0.0, vec[:, V_PRELU:V_PRELU + 1], ALU.min, ALU.mult))
            own.link(v.scalar_tensor_tensor(ta[:, :, :], ta[:, :, :], 0.0, te[:, :, :], ALU.max, ALU.add))
            own.link(v.tensor_tensor(x[:, :, :], x[:, :, :], ta[:, :, :], ALU.add))
            read_out(dve, "cout")
            own.link(v.tensor_tensor(x[:, :, :], x[:, :, :], tc[:, :, :], ALU.add))

            layernorm(x, xn, 1e-5, (sem("xn3"), T))
            rmsnorm(xn, ta, "rms1", tb, sem("ah"))
            from_fm("ahT", fa)
            dve.wait_ge(sem("rope_in"), 16)
            for name, f in (("aq", fb_), ("ak", fc)):
                for m in range(K2):
                    for c, (off, w, _) in enumerate(CHUNKS):
                        bank, freed = got(dve, (name, m, c))
                        v.tensor_tensor(f[:, m, off:off + w], bank[:, 0:w], rope[:, 0, off:off + w],
                                        ALU.mult).then_inc(freed, 1)
                read_out(dve, name)
                for m in range(K2):
                    for c, (off, w, _) in enumerate(CHUNKS):
                        bank, freed = got(dve, (name + "r", m, c))
                        v.tensor_tensor(fd[:, m, off:off + w], bank[:, 0:w], rope[:, 1, off:off + w],
                                        ALU.mult).then_inc(freed, 1)
                        read_out(dve, name + "r", m, c)
                        v.tensor_tensor(f[:, m, off:off + w], f[:, m, off:off + w], fd[:, m, off:off + w], ALU.add)\
                            .then_inc(sem("roped"), 1)
            for t in range(T):
                bank, freed = got(dve, ("av", t))
                v.tensor_copy(td[:, t, 0:128], bank[0:P, 0:128]).then_inc(freed, 1)
            attend("l2", from_banks("l2", lambda m, off, w: lower[:, (T - 1 - m) * P + off:(T - 1 - m) * P + off + w],
                                    HD ** -0.5, causal_tiles),
                   causal_tiles, False, lambda o, a: v.tensor_copy(o, a), te)
            from_fm("yT", fa)
            for t in range(T):
                bank, freed = got(dve, ("ao", t))
                v.tensor_tensor(tb[:, t, :], bank[0:P, 0:D], xn[:, t, :], ALU.add).then_inc(freed, 1)
            read_out(dve, "ao")
            rmsnorm(tb, ta, "rms2", td, sem("flat"))
            own.link(v.tensor_tensor(x[:, :, :], x[:, :, :], tb[:, :, :], ALU.add))
            from_fm("flatT", fa)
            route("gate1", NE1, None, 1e-9, disp)
            experts("e1", NE1, HT1)

        @block.scalar
        def _(act):
            a = nc.scalar

            def from_fm(name, dst):
                for c, (off, w, _) in enumerate(CHUNKS):
                    bank, freed = got(act, (name, 0, c))
                    a.activation(dst[:, 0, off:off + w], bank[:, 0:w], ACT.Copy).then_inc(freed, 1)

            def biased(name, f, bias, func=ACT.Identity, tiles=(0,)):
                for m in tiles:
                    for c, (off, w, _) in enumerate(CHUNKS):
                        bank, freed = got(act, (name, m, c))
                        a.activation(f[:, m, off:off + w], bank[:, 0:w], func, bias=fbias[:, bias + m:bias + m + 1])\
                            .then_inc(freed, 1)

            from_fm("xnT0", fa)
            from_fm("mixhT", fb_)
            act.wait_ge(sem("fb_in"), 16)
            biased("xm", fc, FB_BX)
            act.wait_ge(sem("kmax"), 1)
            a.activation(fd[0:32, 0, :], fd[0:32, 0, :], ACT.Exp, bias=kstat[:, 1:2], accum_out=kstat[:, 2:3])\
                .then_inc(sem("kexp"), 1)
            act.wait_ge(sem("qshift"), 1)
            a.activation(te[:, :, 0:32], te[:, :, 0:32], ACT.Exp).then_inc(sem("qexp"), 1)
            for c, (off, w, _) in enumerate(CHUNKS):
                bank, freed = got(act, ("qkv", 0, c))
                a.activation(fb_[:, 0, off:off + w], bank[:, 0:w], ACT.Copy).then_inc(freed, 1)
            from_fm("h2T", fb_)
            biased("m1", mlp, FB_B1, ACT.Gelu, range(FF // 128))

            def attend(name, tiles_of, weigh):
                def exponentials(i):
                    w = tiles_of(steps[i][0]) * P
                    act.wait_ge(sem(name + "_max"), i + 1)
                    if weigh:
                        if i >= 3:
                            act.wait_ge(sem(name + "_prob"), i - 2)
                        a.activation(expd[:, i % 3, 0:w], masked[:, i % 3, 0:w], ACT.Exp, bias=rneg[:, i:i + 1])\
                            .then_inc(sem(name + "_exp"), 1)
                    else:
                        if i >= 3:
                            read_out(act, name, "pT", i - 3)
                        a.activation(prob[:, i % 3, 0:w], masked[:, i % 3, 0:w], ACT.Exp, bias=rneg[:, i:i + 1],
                                     accum_out=rden[:, i:i + 1]).then_inc(sem(name + "_prob"), 1)

                def turned_out(i):
                    if i >= 3:
                        act.wait_ge(sem(name + "_sum"), i - 2)
                    for c, off, w, _ in chunks_upto(tiles_of(steps[i][0])):
                        bank, freed = got(act, (name, "pT", i, c))
                        a.activation(probT[:, i % 3, off:off + w], bank[0:P, 0:w], ACT.Copy).then_inc(freed, 1)

                for i in range(len(steps) + 1):
                    if i < len(steps):
                        exponentials(i)
                    if i >= 1:
                        turned_out(i - 1)

            def shares(name, ne):
                act.wait_ge(sem(name + "_sh"), 1)
                a.activation(pr[:, :, 0:ne], lg[:, :, 0:ne], ACT.Exp).then_inc(sem(name + "_exp"), 1)

            def experts(name, n_exp, hts):
                units = 2 * len(hts)

                def units_of(e):
                    for m, (mo, mw) in enumerate(hts):
                        for c, (off, w, _) in enumerate(CHUNKS):
                            u = m * 2 + c
                            act.wait_ge(sem(name + "_hid"), e * units + (u + 1))
                            if not (isinstance(e, int) and e == 0 and u < 2):
                                act.wait_ge(sem(name + "_mul"), e * units + (u - 1))
                            a.activation(silu[0:mw, c, 0:w], banks[2 * c][0:mw, 0:w], ACT.Silu)\
                                .then_inc(sem(name + "_silu"), 1)

                units_of(0)
                with act.Fori(1, n_exp) as e:
                    units_of(e)

            attend("l0", all_tiles, True)
            act.wait_ge(sem("elu_min"), 1)
            a.activation(tc[:, :, :], tc[:, :, :], ACT.Exp).then_inc(sem("elu_exp"), 1)
            from_fm("xnT1", fa)
            shares("gate0", NE0)
            experts("e0", NE0, HT0)
            from_fm("xnT2", fa)
            biased("gq", fb_, FB_BQ)
            biased("gk", fc, FB_BK)
            attend("l1", all_tiles, True)
            act.wait_ge(sem("glogit"), 1)
            a.activation(gate[:, :], gate[:, :], ACT.Sigmoid, bias=vec[:, V_BGATE:V_BGATE + 1])\
                .then_inc(sem("gated"), 1)
            from_fm("ahT", fa)
            attend("l2", causal_tiles, False)
            from_fm("yT", fa)
            from_fm("flatT", fa)
            shares("gate1", NE1)
            experts("e1", NE1, HT1)

        @block.gpsimd
        def _(pool):
            p = nc.gpsimd
            own = Chain(pool, sem("pool_own"))
            own.note(p.memset(ident[:, :], 0.0))
            own.note(p.memset(lower[:, :], 0.0))
            own.note(p.memset(block4[:, :], 1.0))
            own.note(p.memset(block32[:, :], 0.0))
            own.fence()
            p.affine_select(out=ident[:, :], in_=ident[:, :], compare_op=ALU.not_equal, fill=1.0, base=0,
                            pattern=[[-1, 128]], channel_multiplier=1).then_inc(sem("ident"), 2)
            p.iota(iota_n[:, :], pattern=[[1, OH]], base=0, channel_multiplier=0,
                   allow_small_or_imprecise_dtypes=True).then_inc(sem("iotas"), 1)
            p.iota(iota_e[:, :], pattern=[[1, NE0]], base=0, channel_multiplier=0,
                   allow_small_or_imprecise_dtypes=True).then_inc(sem("iotas"), 1)
            own.note(p.affine_select(out=lower[:, :], in_=lower[:, :], compare_op=ALU.is_ge, fill=-BIG,
                                     base=(T - 1) * P, pattern=[[-1, N]], channel_multiplier=1))
            b4 = block4[:, :].rearrange("p (b c) -> p b c", b=NBLK)
            own.link(p.affine_select(out=b4, in_=b4, compare_op=ALU.is_ge, fill=0.0, base=0,
                                     pattern=[[-KR, NBLK], [0, DH]], channel_multiplier=1))
            own.link(p.affine_select(out=b4, in_=b4, compare_op=ALU.is_ge, fill=0.0, base=KR - 1,
                                     pattern=[[KR, NBLK], [0, DH]], channel_multiplier=-1))
            for q in range(4):
                ins = p.memset(block32[32 * q:32 * q + 32, 32 * q:32 * q + 32], 1.0)
            ins.then_inc(sem("blocks"), 1)

            def gather(g, b, j):
                for w, tab in enumerate((xl_tab, xr_tab)):
                    p.indirect_dma_start(
                        out=gat[:, b % 2, w, j * D:(j + 1) * D], out_offset=None, in_=tab,
                        in_offset=bass.IndirectOffsetOnAxis(ap=idx_ring[:, b % 4, w, j:j + 1], axis=0))\
                        .then_inc(sem(f"gathered{b % 2}"), 16)

            def scatter(g, b, j):
                if not (isinstance(g, int) and g == 0 and j == 0):
                    pool.wait_ge(sem("scattered"), g * (G * 16) + j * 16)
                    pool.sem_inc(sem("pool_turn"), 1)
                p.indirect_dma_start(
                    out=pair_scores, in_=sc_ring[:, b % 2, j, :], in_offset=None,
                    out_offset=bass.IndirectOffsetOnAxis(ap=idx_ring[:, b % 4, 2, j:j + 1], axis=0))\
                    .then_inc(sem("scattered"), 16)

            def turn(g, b):
                pool.wait_ge(sem("indices"), g + 1)
                pool.wait_ge(sem("scored"), g - 1)
                pool.sem_inc(sem("pool_turn"), 1)
                for j in range(G):
                    gather(g, b, j)
                    scatter(g - 2, b - 2, j)

            pool.wait_ge(sem("tables"), 32)
            pool.wait_ge(sem("zeros_out"), 16 * T)
            for g in range(2):
                pool.wait_ge(sem("indices"), g + 1)
                for j in range(G):
                    gather(g, g, j)
            turn(2, 2)
            turn(3, 3)
            with pool.Fori(1, NG // 4) as i:
                for b in range(4):
                    turn(i * 4 + b, b)
            for g in (NG - 2, NG - 1):
                pool.wait_ge(sem("scored"), g + 1)
                for j in range(G):
                    scatter(g, g, j)
            pool.wait_ge(sem("scattered"), EC * 16)

        @block.sync
        def _(sp):
            sp.dma_start(x[:, :, :], x_in.rearrange("(t p) d -> p t d", p=P)).then_inc(sem("x_in"), 16)
            sp.dma_start(wres[:, :, 0:W_SIZES[0]], w0_in).then_inc(sem("w0_in"), 16)
            sp.dma_start(srci[:, :], src_in).then_inc(sem("edges_in"), 16)
            sp.dma_start(dsti[:, :], dst_in).then_inc(sem("edges_in"), 16)
            sp.dma_start(vec[:, 0:V_SIZE0], vec0_in.partition_broadcast(P)).then_inc(sem("vec0_in"), 16)
            sp.dma_start(fbias[:, :], fb_in).then_inc(sem("fb_in"), 16)
            sp.wait_ge(sem("zeros"), 1)
            cells = pair_scores.rearrange("(m p n) h -> m p (n h)", m=T, p=P)
            for m in range(T):
                sp.dma_start(cells[m], cnt[:, 0:4, :].rearrange("p m n -> p (m n)")).then_inc(sem("zeros_out"), 16)
            sp.wait_ge(sem("mixw0"), 1)
            for q in range(4):
                rows = slice(32 * q, 32 * q + 32)
                sp.dma_start(mixw[rows, q, :], mixw_in[:, 0:KR + DH]).then_inc(sem("mixw_in"), 16)
                for k in range(K2):
                    at = (4 * k + q) * KR
                    sp.dma_start(mixk[rows, k, at:at + KR], mixw_in[:, KR + DH:]).then_inc(sem("mixw_in"), 16)
            read_out(sp, "lr")
            for w, tab in enumerate((xl_tab, xr_tab)):
                sp.dma_start(tab.rearrange("(t p) d -> p t d", p=P), xlr[:, :, w * D:(w + 1) * D])\
                    .then_inc(sem("tables"), 16)
            sp.dma_start(w2, w2_in).then_inc(sem("w2_in"), 16)
            sp.wait_ge(sem("scattered"), EC * 16)
            sp.wait_ge(sem("counts_out"), 1)
            for m in range(T):
                if m >= 2:
                    sp.wait_ge(sem("l0_taken"), (m - 1) * H)
                sp.dma_start(sdense[:, m % 2, :, :].rearrange("p n h -> p (n h)"), cells[m])\
                    .then_inc(sem(f"sdense{m % 2}"), 16)

            def expert_weights(name, n_exp, main, rest):
                def load(e, s):
                    sp.dma_start(exw[:, s, 0:main.shape[2]], main[bass.ds(e, 1)].rearrange("e p n -> (e p) n"))\
                        .then_inc(sem(f"{name}_w{s}"), 16)
                    if rest is not None:
                        sp.dma_start(exw_r[:, s, :], rest[bass.ds(e, 1)].rearrange("e p n -> (e p) n"))\
                            .then_inc(sem(f"{name}_w{s}"), 16)

                load(0, 0)
                load(1, 1)
                with sp.Fori(1, n_exp // 2) as i:
                    for s in range(2):
                        sp.wait_ge(sem(name + "_out"), (i * 2 + (s - 1)) * T)
                        load(i * 2 + s, s)

            read_out(sp, "l0", "agg")
            expert_weights("e0", NE0, exp0_in, None)
            sp.wait_ge(sem("layer0_read"), 1)
            sp.dma_start(vec[:, 0:V_SIZE], vec1_in.partition_broadcast(P)).then_inc(sem("vec1_in"), 16)
            sp.wait_ge(sem("e0_acc"), T)
            sp.dma_start(wres[:, :, 0:W_SIZES[1]], w1_in).then_inc(sem("w1_in"), 16)
            sp.wait_ge(sem("e0_acc"), NE0 * T)
            sp.dma_start(rope, rope_in).then_inc(sem("rope_in"), 16)
            read_out(sp, "l2", "agg")
            expert_weights("e1", NE1, exp1_in, exp1r_in)
            sp.wait_ge(sem("e1_acc"), NE1 * T)
            sp.dma_start(out.rearrange("(t p) d -> p t d", p=P), x[:, :, :]).then_inc(sem("out"), 16)
            sp.wait_ge(sem("out"), 16)


def kernel(**inputs):
    import concourse.bacc as bacc
    from concourse.bass_utils import run_bass_kernel_spmd

    a = {k: np.asarray(v) for k, v in inputs.items()}

    def halves(*ws):
        w = np.concatenate(ws, axis=-1)
        return w.reshape(K2, 128, w.shape[-1]).transpose(1, 0, 2)

    def columns(v):
        return v.reshape(-1, 128).T

    l0 = [a["L0_gnn_att"], a["L0_gnn_bias"], a["L0_gnn_gamma"], a["L0_gnn_beta"], a["L0_mix_ln1_g"],
          a["L0_mix_ln1_b"], a["L0_mix_bo"], a["L0_mix_ln2_g"], a["L0_mix_ln2_b"], a["L0_mix_b2"],
          a["L0_ffn_gate_b"]]
    l1 = [a["L1_gnn_bv"], a["L1_gnn_bskip"], a["L1_gnn_Wgate"], a["L1_gnn_ln_w"], a["L1_gnn_ln_b"],
          a["L1_mix_kln_weight"], a["L1_mix_kln_bias"], a["L1_mix_vln_weight"], a["L1_mix_vln_bias"],
          a["L1_ffn_ln1_w"], a["L1_ffn_ln2_w"], a["L1_gnn_bgate"], a["L1_gnn_prelu_a"]]
    other = np.arange(D).reshape(H, 2, HD // 2)[:, ::-1].reshape(D)
    wq, wk = a["L1_ffn_wq"].T, a["L1_ffn_wk"].T
    twice = np.repeat(np.arange(128).reshape(2, HD), 2, axis=0).reshape(D)
    wk2 = wk[:, twice]
    inv_freq = 1.0 / 10000.0 ** (np.arange(0, HD, 2, dtype=np.float32) / HD)
    freqs = np.outer(np.arange(N, dtype=np.float32), inv_freq)
    emb = np.concatenate([freqs, freqs], axis=-1)
    sign = np.concatenate([-np.ones(HD // 2), np.ones(HD // 2)])
    rope = np.stack([np.tile(np.cos(emb).T, (2, 1)), np.tile((np.sin(emb) * sign).T, (2, 1))], axis=1)

    def expert(win, wgate, wout):
        n_exp, _, hidden = win.shape
        main = hidden // 128 * 128
        parts = [win.reshape(n_exp, K2, 128, hidden).transpose(0, 2, 1, 3).reshape(n_exp, 128, -1),
                 wgate.reshape(n_exp, K2, 128, hidden).transpose(0, 2, 1, 3).reshape(n_exp, 128, -1),
                 wout[:, :main].reshape(n_exp, -1, 128, D).transpose(0, 2, 1, 3).reshape(n_exp, 128, -1)]
        return np.concatenate(parts, axis=2), wout[:, main:]

    exp0, _ = expert(a["L0_ffn_w1"], a["L0_ffn_w2"], a["L0_ffn_w3"])
    exp1, exp1r = expert(a["L1_ffn_w1"].transpose(0, 2, 1), a["L1_ffn_w3"].transpose(0, 2, 1),
                         a["L1_ffn_w2"].transpose(0, 2, 1))
    arrays = {
        "x": a["x"],
        "src": a["src"].reshape(P, EC),
        "dst": a["dst"].reshape(P, EC),
        "vec0": np.concatenate([v.reshape(-1) for v in l0]),
        "vec1": np.concatenate([v.reshape(-1) for v in l1]),
        "fb": np.concatenate([columns(a[n]) for n in ("L0_mix_bx", "L0_mix_b1", "L1_gnn_bq", "L1_gnn_bk")], axis=1),
        "w0": halves(a["L0_gnn_W_l"], a["L0_gnn_W_r"], a["L0_mix_Wx"], a["L0_mix_Wo"], a["L0_mix_W1"],
                     a["L0_ffn_gate_w"]),
        "w1": halves(a["L1_gnn_Wq"].T, a["L1_gnn_Wk"].T, a["L1_gnn_Wv"].T, a["L1_gnn_Wskip"].T, wq, wq[:, other],
                     wk2, wk2[:, other], a["L1_ffn_wv"].T, a["L1_ffn_wo"].T, a["L1_ffn_router_w"].T),
        "w2": a["L0_mix_W2"].reshape(FF // 128, 128, D).transpose(1, 0, 2),
        "mixw": np.concatenate([a["L0_mix_Wq"], a["L0_mix_Wv"], a["L0_mix_Wk"]], axis=1),
        "exp0": exp0,
        "exp1": exp1,
        "exp1r": exp1r,
        "rope": rope.astype(np.float32),
    }
    nc = bacc.Bacc("TRN2", target_bir_lowering=False, num_devices=1)
    in_map, args = {}, []
    for name, v in arrays.items():
        v = np.ascontiguousarray(v)
        in_map[f"in_{name}"] = v
        args.append(nc.dram_tensor(f"in_{name}", v.shape, mybir.dt.from_np(v.dtype), kind="ExternalInput").ap())
    args.append(nc.dram_tensor("out_x", (N, D), F32, kind="ExternalOutput").ap())
    build(nc, *args)
    return run_bass_kernel_spmd(nc, [in_map], core_ids=[0]).results[0]["out_x"]
```

```python
from contextlib import ExitStack

import numpy as np
import concourse.bass as bass
from concourse import mybir

ALU = mybir.AluOpType
ACT = mybir.ActivationFunctionType
AX = mybir.AxisListType
F32 = mybir.dt.float32
BF16 = mybir.dt.bfloat16
FP16 = mybir.dt.float16
I32 = mybir.dt.int32
U32 = mybir.dt.uint32

N, D, E = 625, 256, 20000
P, T = 125, 5
K2 = D // 128
CHUNKS = [(0, 375, (0, 1, 2)), (375, 250, (3, 4))]
H = 4
HD = D // H
EC = E // P
G = 5
NG = EC // G
NBLK = 8
DH = D // NBLK
KR = 4
FF = 4 * D
NE0, HID0 = 16, 512
NE1, HID1 = 8, 682
BIG = 1e30
OH = N + 1
BANKS = 8
VW = 96
EARLY = 8
PACED = (NG - 8) // 8
EDGE_LINKS = 3
assert NG % 8 == 0 and EARLY % 4 == 0 and EARLY + 4 + 4 * PACED <= NG - 2

VECS = [["att", "g_bias", "g_gamma", "g_beta", "ln1_g", "ln1_b", "bo", "ln2_g", "ln2_b", "b2"],
        ["bv", "bskip", "wg_skip", "wg_rst", "wg_diff", "ln_w", "ln_b", "kln_w", "kln_b", "vln_w", "vln_b",
         "rms1", "rms2"]]
V_GATEB = len(VECS[0]) * D
V_SIZE0 = V_GATEB + NE0
V_BGATE = len(VECS[1]) * D
V_PRELU = V_BGATE + 1
V_SIZE = V_PRELU + 1
FB_BX, FB_B1, FB_BQ, FB_BK, FB_SIZE = 0, 2, 10, 12, 14
WCOLS = [[("lr", 512), ("wx", 256), ("wo", 256), ("w1", FF), ("gate0", NE0)],
         [("gq", 256), ("gk", 256), ("gvs", 512), ("aq", 256), ("aqr", 256), ("ak", 256), ("akr", 256), ("av", 128),
          ("ao", 256), ("gate1", NE1)]]
WOFF, W_SIZES = {}, []
for _layer in WCOLS:
    _at = 0
    for _n, _c in _layer:
        WOFF[_n] = (_at, _c)
        _at += _c
    W_SIZES.append(_at)
SLOTS = 128
NBLK0 = (2 * N - NE0) // SLOTS + NE0
UNITS0 = [[(0, 128), (1, 128), (2, 128), (3, 128)]]
UNITS1 = [[(0, 128), (1, 128), (2, 128), (3, 128)], [(4, 128), (5, HID1 - 5 * 128)]]
NBLK1 = (2 * N - NE1) // SLOTS + NE1
EXP0 = 2 * 2 * HID0 + (HID0 // 128) * D
EXP1 = 2 * 2 * HID1 + (HID1 // 128) * D


def after(eng, sem, value):
    if not (isinstance(value, int) and value <= 0):
        eng.wait_ge(sem, value)


def block_steps(eng, nblk, step):
    for b in range(3):
        step(b, b % 2)
    pairs = (nblk - 3 - 4) // 2
    with eng.Fori(0, pairs) as i:
        step(i * 2 + 3, 1)
        step(i * 2 + 4, 0)
    for b in range(3 + 2 * pairs, nblk):
        step(b, b % 2)


class Chain:

    def __init__(self, eng, sem, base=0):
        self.eng, self.sem, self.base, self.n = eng, sem, base, 0

    def note(self, ins):
        self.n += 1
        return ins.then_inc(self.sem, 1)

    def fence(self):
        self.eng.wait_ge(self.sem, self.base + self.n)

    def link(self, ins):
        self.note(ins)
        self.fence()


ARENA = 18436


def build(nc, x_in, src_in, dst_in, vec0_in, vec1_in, fb_in, w0_in, w1_in, w2_in, mixw_in, exp0_in, exp1_in,
          exp1r_in, rope_in, out):
    ctx = ExitStack()
    with ctx:
        sems = {}

        def sem(name):
            if name not in sems:
                sems[name] = ctx.enter_context(nc.semaphore(name))
            return sems[name]

        def sb(name, shape, dt=F32):
            return ctx.enter_context(nc.sbuf_tensor(name, shape, dt))

        xl_tab = nc.dram_tensor("xl_tab", [N, D], F32).ap()
        xr_tab = nc.dram_tensor("xr_tab", [N, D], F32).ap()
        row_tab = [nc.dram_tensor(f"row_tab{i}", [N, D], F32).ap() for i in range(2)]
        slot_y = nc.dram_tensor("slot_y", [NBLK0 * SLOTS, D], F32).ap()
        pair_scores = nc.dram_tensor("pair_scores", [N * N, H], F32).ap()

        vec = sb("vec", [P, V_SIZE])
        fbias = sb("fbias", [128, FB_SIZE])
        wres = sb("wres", [128, K2, max(W_SIZES)])
        mixw = sb("mixw", [128, 4, KR + DH])
        mixk = sb("mixk", [128, K2, NBLK * KR])
        ident = sb("ident", [128, 128])
        lower = sb("lower", [P, N])
        block4 = sb("block4", [NBLK * KR, D])
        block32 = sb("block32", [128, 128])
        iota_n = sb("iota_n", [P, OH], FP16)
        iota_e = sb("iota_e", [P, NE0])
        zero16 = sb("zero16", [1, 512], BF16)
        x, xn, ta, tb, tc, td, te = (sb(n, [P, T, D]) for n in ("x", "xn", "ta", "tb", "tc", "td", "te"))
        xlr = sb("xlr", [P, T, 2 * D])
        fa, fb_, fc, fd = (sb(n, [128, K2, N]) for n in ("fa", "fb", "fc", "fd"))
        kvbd = sb("kvbd", [NBLK * KR, D])
        ckv = sb("ckv", [128, K2, 128])
        stats, mv, rstd = sb("stats", [P, T, 6]), sb("mv", [P, T, 2]), sb("rstd", [P, T])
        hstat = sb("hstat", [P, 4, T * NBLK])
        root = sb("root", [P, 3, T * NBLK])
        kstat = sb("kstat", [NBLK * KR, 3])
        lg, pr = sb("lg", [P, T, NE0]), sb("pr", [P, T, NE0])
        rmax, rsum, rinv = sb("rmax", [P, T]), sb("rsum", [P, T]), sb("rinv", [P, T])
        top8, topi, topf = sb("top8", [P, T, 8]), sb("topi", [P, T, 8], U32), sb("topf", [P, T, 8])
        wtop = sb("wtop", [P, T, 2])
        pick = sb("pick", [P, 2, T, NE0])
        pick16 = sb("pick16", [P, T, NE0], BF16)
        rank, total = sb("rank", [P, T, NE0]), sb("total", [P, T, NE0])
        nblocks, first, upto = sb("nblocks", [P, NE0]), sb("first", [P, NE0]), sb("upto", [P, NE0])
        eprod = fd[0:P, 0, 0:NE0 * NE0].rearrange("p (a b) -> p a b", b=NE0)
        bcmp = fd[0:P, 1, 0:NBLK0 * NE0].rearrange("p (a b) -> p a b", b=NE0)
        bown = sb("bown", [P, NBLK0])
        nblocks_i, bown_i = sb("nblocks_i", [P, NE0], I32), sb("bown_i", [P, NBLK0], I32)
        slotf, sloti = sb("slotf", [P, 2, T]), sb("sloti", [P, 2, T], I32)
        before = sb("before", [P, P], BF16)
        ones16 = sb("ones16", [P, P], BF16)
        before_e = sb("before_e", [P, NE0, NE0])
        iota_b = sb("iota_b", [P, NBLK0])
        iota_s = sb("iota_s", [P, SLOTS], FP16)
        node_id = sb("node_id", [P, T, 2], FP16)
        slot_rel = sb("slot_rel", [P, 2 * T])
        ids = sb("ids", [SLOTS, 2, 1], I32)
        gpart, gate = sb("gpart", [P, 3, T]), sb("gate", [P, T])
        rmx, rneg, rden, rrec = (sb(n, [P, T * H]) for n in ("rmx", "rneg", "rden", "rrec"))
        rmx_a = sb("rmx_a", [P, T * H])
        srci, dsti, celli = (sb(n, [P, EC], I32) for n in ("srci", "dsti", "celli"))
        srcf, dstf = (sb(n, [P, EC]) for n in ("srcf", "dstf"))
        cellf = tc[:, 0, 0:EC]
        idx_ring = sb("idx_ring", [P, 4, 3, G], I32)
        sc_ring = sb("sc_ring", [P, 2, G, H])
        cnt = sb("cnt", [P, T, N])
        nmask = sb("nmask", [P, T, N], BF16)

        arena = sb("arena", [128, ARENA])
        gat = arena[0:P, 0:4 * G * D].rearrange("p (s w c) -> p s w c", s=2, w=2)
        at = 4 * G * D
        oh = arena[0:P, at:at + 2 * G * OH].bitcast(BF16).rearrange("p (s w g n) -> p s w g n", s=2, w=2, g=G)
        at += 2 * G * OH
        w2 = arena[:, at:at + FF // 128 * D].rearrange("p (k n) -> p k n", n=D)
        at += FF // 128 * D
        mlp = arena[:, at:at + FF // 128 * N].rearrange("p (k n) -> p k n", n=N)
        assert at + FF // 128 * N <= ARENA
        sdense = arena[0:P, 0:2 * H * N].rearrange("p (s n h) -> p s n h", s=2, h=H)
        at = 2 * H * N
        masked, expd, prob, probT = (arena[0:P, at + i * 3 * N:at + (i + 1) * 3 * N].rearrange("p (s n) -> p s n", s=3)
                                     for i in range(4))
        at += 12 * N
        rope = arena[:, at:at + 2 * N].rearrange("p (w n) -> p w n", w=2)
        at += 2 * N
        fq = arena[:, at:at + 2 * K2 * N].rearrange("p (k w n) -> p k w n", k=K2, w=2)
        assert at + 2 * K2 * N <= ARENA
        exw = arena[:, 0:2 * EXP1].rearrange("p (s n) -> p s n", s=2)
        at = 2 * EXP1
        exw_r = arena[0:HID1 % 128, at:at + 2 * D].rearrange("p (s n) -> p s n", s=2)
        at += 2 * D
        xs = arena[:, at:at + 2 * D].rearrange("p (s d) -> p s d", s=2)
        at += 2 * D
        xsT = arena[:, at:at + 2 * K2 * SLOTS].rearrange("p (s k n) -> p s k n", s=2, k=K2)
        at += 2 * K2 * SLOTS
        silu = arena[:, at:at + 2 * 4 * SLOTS].rearrange("p (s m n) -> p s m n", s=2, m=4)
        at += 2 * 4 * SLOTS
        hid = arena[:, at:at + 2 * 6 * SLOTS].rearrange("p (s m n) -> p s m n", s=2, m=6)
        at += 2 * 6 * SLOTS
        ys = arena[:, at:at + 2 * D].rearrange("p (s d) -> p s d", s=2)
        at += 2 * D
        yg = arena[0:P, at:at + 2 * T * D].rearrange("p (k t d) -> p k t d", k=2, t=T)
        at += 2 * T * D
        sel = arena[0:P, at:at + 2 * T * SLOTS].bitcast(FP16).rearrange("p (s q n) -> p s q n", s=2, n=SLOTS)
        assert at + 2 * T * SLOTS <= ARENA

        banks = [ctx.enter_context(nc.psum_tensor(f"bank{b}", [128, 512], F32)) for b in range(BANKS)]
        full = [sem(f"full{b}") for b in range(BANKS)]
        free = [sem(f"free{b}") for b in range(BANKS)]
        uses = [0] * BANKS
        fulls = [0] * BANKS
        ring = {"at": 0, "n": BANKS}
        ticket = {}

        def V(layer, name):
            i = VECS[layer].index(name) * D
            return vec[:, i:i + D].unsqueeze(1).to_broadcast([P, T, D])

        def Vt(layer, name, width=D):
            i = VECS[layer].index(name) * D
            return vec[:, i:i + width]

        def W(name, k):
            o, c = WOFF[name]
            return wres[:, k, o:o + c]

        def got(eng, name):
            b, n, _ = ticket[name if isinstance(name, tuple) else (name,)]
            eng.wait_ge(full[b], n)
            return banks[b], free[b]

        def read_out(eng, *key):
            last = {}
            for name, (b, _, n) in ticket.items():
                if name[:len(key)] == key:
                    last[b] = max(last.get(b, 0), n)
            assert last, key
            for b, n in last.items():
                eng.wait_ge(free[b], n)

        def halves(k, off, w):
            return [(slice(q * HD, (q + 1) * HD), fq[q * HD:(q + 1) * HD, k, q, off:off + w]) for q in range(2)]

        steps = [(m, h) for m in range(T) for h in range(H)]
        causal_tiles = lambda m: m + 1
        all_tiles = lambda m: T

        def chunks_upto(ns):
            found = []
            for c, (off, w, tiles) in enumerate(CHUNKS):
                tiles = [t for t in tiles if t < ns]
                if tiles:
                    found.append((c, off, len(tiles) * P, tiles))
            return found

        def runs(tiles):
            found = []
            for i, (m, rows) in enumerate(tiles):
                if found and found[-1][3] == rows:
                    found[-1][2] += 1
                else:
                    found.append([i, m, 1, rows])
            return found

        block = ctx.enter_context(nc.Block())

        @block.tensor
        def _(pe):
            def group(name):
                b = ring["at"] % ring["n"]
                ring["at"] += 1
                return bank_for(name, b)

            def bank_for(name, b):
                if uses[b]:
                    pe.wait_ge(free[b], uses[b])
                uses[b] += 1
                fulls[b] += 1
                ticket[name if isinstance(name, tuple) else (name,)] = (b, fulls[b], uses[b])
                return banks[b], full[b]

            def all_free():
                for b in range(BANKS):
                    pe.wait_ge(free[b], uses[b])

            def to_fm(name, src):
                for k in range(K2):
                    for c, (off, w, tiles) in enumerate(CHUNKS):
                        bank, done = group((name, k, c))
                        for t in tiles:
                            mm = pe.transpose(bank[:, t * P - off:t * P - off + P],
                                              src[:, t, k * 128:(k + 1) * 128], ident[0:P, 0:P])
                        mm.then_inc(done, 1)

            def linear_tm(name, f, rhs, width, ks=K2):
                for t in range(T):
                    bank, done = group((name, t))
                    for k in range(ks):
                        mm = pe.matmul(bank[0:P, 0:width], f[:, k, t * P:(t + 1) * P], rhs(k),
                                       start=(k == 0), stop=(k == ks - 1))
                    mm.then_inc(done, 1)

            def linear_fm(name, f, weights, m_tiles, ks=K2):
                for m in range(m_tiles):
                    for c, (off, w, _) in enumerate(CHUNKS):
                        bank, done = group((name, m, c))
                        for k in range(ks):
                            mm = pe.matmul(bank[:, 0:w], W(weights, k)[:, m * 128:(m + 1) * 128],
                                           f[:, k, off:off + w], start=(k == 0), stop=(k == ks - 1))
                        mm.then_inc(done, 1)

            pe.wait_ge(sem("ident"), 2)
            pe.wait_ge(sem("xn0"), T)
            to_fm("xnT0", xn)
            pe.wait_ge(sem("wlr_in"), 16)
            read_out(pe, "xnT0")
            linear_tm("lr", fa, lambda k: W("lr", k), 2 * D)

            pe.wait_ge(sem("w0_in"), 16)
            pe.wait_ge(sem("mixh"), 1)
            to_fm("mixhT", ta)
            read_out(pe, "mixhT")
            linear_fm("xm", fb_, "wx", K2)
            read_out(pe, "xm")
            pe.wait_ge(sem("mixw_in"), 12 * 16)
            for t in range(T):
                bank, done = group(("qv", t))
                for k in range(K2):
                    mm = pe.matmul(bank[0:P, k * 144:k * 144 + 144], fc[:, k, t * P:(t + 1) * P],
                                   mixw[:, :, :].rearrange("p a b -> p (a b)"), start=True, stop=True)
                mm.then_inc(done, 1)
            for c, (off, w, _) in enumerate(CHUNKS):
                bank, done = group(("kT", c))
                for k in range(K2):
                    mm = pe.matmul(bank[0:32, 0:w], mixk[:, k, :], fc[:, k, off:off + w],
                                   start=(k == 0), stop=(k == 1))
                mm.then_inc(done, 1)
            pe.wait_ge(sem("ksoft"), 1)
            bank, done = group("kN")
            for t in range(T):
                mm = pe.transpose(bank[0:P, t * 32:t * 32 + 32], fd[0:32, 0, t * P:(t + 1) * P], ident[0:32, 0:32])
            mm.then_inc(done, 1)
            pe.wait_ge(sem("qsoft"), 1)
            for c, (off, w, tiles) in enumerate(CHUNKS):
                bank, done = group(("qT", c))
                for t in tiles:
                    mm = pe.transpose(bank[0:32, t * P - off:t * P - off + P], te[:, t, 0:32], ident[0:P, 0:P])
                mm.then_inc(done, 1)
            read_out(pe, "kN")
            read_out(pe, "qv")
            bank, done = group("kv")
            for t in range(T):
                mm = pe.matmul(bank[0:32, 0:D], te[:, t, 32:64], td[:, t, :], start=(t == 0), stop=(t == T - 1))
            mm.then_inc(done, 1)
            read_out(pe, "kv")
            read_out(pe, "qT")
            for m in range(K2):
                for c, (off, w, _) in enumerate(CHUNKS):
                    bank, done = group(("qkv", m, c))
                    pe.matmul(bank[:, 0:w], kvbd[:, m * 128:(m + 1) * 128], fd[0:32, 1, off:off + w],
                              start=True, stop=True).then_inc(done, 1)
            read_out(pe, "qkv")
            linear_tm("attn", fb_, lambda k: W("wo", k), D)
            pe.wait_ge(sem("h2"), 1)
            to_fm("h2T", ta)
            read_out(pe, "h2T")
            linear_fm("m1", fb_, "w1", FF // 128)
            read_out(pe, "m1")
            pe.wait_ge(sem("w2_in"), 16)
            linear_tm("m2", mlp, lambda k: w2[:, k, :], D, ks=FF // 128)

            REST = N - 512
            all_free()
            pe.wait_ge(sem("zero16"), 1)

            def zeros(first):
                for m in range(T):
                    pe.matmul(banks[m][0:P, 0:512], zero16[0:1, 0:P], zero16[0:1, 0:512], start=first, stop=not first,
                              skip_group_check=True)
                pe.matmul(banks[5][0:P, 0:4 * REST], zero16[0:1, 0:P], zero16[0:1, 0:4 * REST], start=first,
                          stop=not first, skip_group_check=True)
                return pe.matmul(banks[6][0:P, 0:REST], zero16[0:1, 0:P], zero16[0:1, 0:REST], start=first,
                                 stop=not first, skip_group_check=True)

            zeros(True)
            with pe.Fori(0, NG // 4) as i:
                for b in range(4):
                    s = b % 2
                    pe.wait_ge(sem("onehot"), i * 4 + (b + 1))
                    for j in range(G):
                        for m in range(T):
                            lhsT = oh[:, s, 1, j, m * P:(m + 1) * P]
                            pe.matmul(banks[m][0:P, 0:512], lhsT, oh[:, s, 0, j, 0:512], start=False, stop=False,
                                      skip_group_check=True)
                            rest = banks[5][0:P, m * REST:(m + 1) * REST] if m < 4 else banks[6][0:P, 0:REST]
                            mm = pe.matmul(rest, lhsT, oh[:, s, 0, j, 512:N], start=False, stop=False,
                                           skip_group_check=True)
                    mm.then_inc(sem("onehot_used"), 1)
            zeros(False).then_inc(sem("counted"), 1)
            pe.wait_ge(sem("counts_out"), 1)

            def attend(name, scores, v_rows, tiles_of):
                ring["n"] = 6

                def turn(i):
                    pe.wait_ge(sem(name + "_prob"), i + 1)
                    for c, off, w, tiles in chunks_upto(tiles_of(steps[i][0])):
                        bank, done = group((name, "pT", i, c))
                        for t in tiles:
                            mm = pe.transpose(bank[0:P, t * P - off:t * P - off + P],
                                              prob[:, i % 3, t * P:(t + 1) * P], ident[0:P, 0:P])
                        mm.then_inc(done, 1)

                def sum_v(i):
                    m, h = steps[i]
                    b = 6 + m % 2
                    if h == 0 and uses[b]:
                        pe.wait_ge(free[b], uses[b])
                    read_out(pe, name, "pT", i)
                    for t in range(tiles_of(m)):
                        mm = pe.matmul(banks[b][0:P, h * 128:h * 128 + VW], probT[:, i % 3, t * P:(t + 1) * P],
                                       v_rows(t, h), start=(t == 0), stop=(t == tiles_of(m) - 1))
                    mm.then_inc(sem(name + "_sum"), 1)
                    if h == H - 1:
                        uses[b] += 1
                        ticket[(name, "agg", m)] = (b, 0, uses[b])

                if scores:
                    scores(0, *steps[0])
                for i in range(len(steps) + 3):
                    if i + 1 < len(steps) and scores:
                        scores(i + 1, *steps[i + 1])
                    if 2 <= i < len(steps) + 2:
                        turn(i - 2)
                    if i >= 3:
                        sum_v(i - 3)
                ring["n"] = BANKS

            attend("l0", None, lambda t, h: xlr[:, t, h * HD:h * HD + VW], all_tiles)

            def experts(name, nblk, units, w_in, w_out, n_out):
                nu = len(units)

                def row_nodes(b, s):
                    pe.wait_ge(sem(name + "_sel"), b + 1)
                    after(pe, sem(name + "_ids"), b)
                    for q in range(2 * T):
                        mm = pe.matmul(banks[7][:, 0:2], sel[:, s, q, :], node_id[:, q % T, :], start=(q == 0),
                                       stop=(q == 2 * T - 1))
                    mm.then_inc(sem(name + "_nodes"), 1)

                def turn_rows(b, s):
                    pe.wait_ge(sem(f"{name}_xs{s}"), (b - s) * 8 + 16)
                    after(pe, sem(name + "_xsT"), b)
                    for k in range(K2):
                        mm = pe.transpose(banks[0][:, k * 128:(k + 1) * 128], xs[:, s, k * 128:(k + 1) * 128],
                                          ident[:, :])
                    mm.then_inc(sem(name + "_turned"), 1)

                def hidden(b, s):
                    pe.wait_ge(sem(f"{name}_in{s}"), (b - s) * 8 + 16)
                    pe.wait_ge(sem(name + "_xsT"), b + 1)
                    for j, tiles in enumerate(units):
                        buf = j if nu == 2 else s
                        after(pe, sem(name + "_mul"), b * nu + (j - 1))
                        for q in range(2):
                            for i, (m, rows) in enumerate(tiles):
                                for k in range(K2):
                                    mm = pe.matmul(banks[1 + 2 * q + buf][0:rows, i * SLOTS:(i + 1) * SLOTS],
                                                   w_in(s, q, k, m, rows), xsT[:, s, k, :],
                                                   start=(k == 0), stop=(k == 1))
                        mm.then_inc(sem(name + "_hid"), 1)

                def output(b, s):
                    pe.wait_ge(sem(name + f"_wout{s}"), ((b - s) * 8 + 16) * n_out)
                    pe.wait_ge(sem(name + "_mul"), b * nu + nu)
                    after(pe, sem(name + "_ycopied"), b - 1)
                    flat = [x for tiles in units for x in tiles]
                    for m, rows in flat:
                        mm = pe.matmul(banks[5 + s][:, 0:D], hid[0:rows, s, m, :], w_out(s, m), start=(m == 0),
                                       stop=(m == len(flat) - 1))
                    mm.then_inc(sem(name + "_out"), 1)

                def step(b, s):
                    if not (isinstance(b, int) and b + 2 >= nblk):
                        row_nodes(b + 2, s)
                    if not (isinstance(b, int) and b + 1 >= nblk):
                        turn_rows(b + 1, 1 - s)
                    hidden(b, s)
                    if not (isinstance(b, int) and b == 0):
                        output(b - 1, 1 - s)

                all_free()
                row_nodes(0, 0)
                row_nodes(1, 1)
                turn_rows(0, 0)
                block_steps(pe, nblk, step)
                output(nblk - 1, (nblk - 1) % 2)

            def ranks(name, ne):
                pe.wait_ge(sem(name + "_picked"), 1)
                for what, m in (("rank", before), ("total", ones16)):
                    bank, done = group((name, what))
                    pe.matmul(bank[0:P, 0:T * NE0], m[:, :], pick16[:, :, :].rearrange("p t e -> p (t e)"),
                              start=True, stop=True).then_inc(done, 1)

            pe.wait_ge(sem("xn1"), T)
            to_fm("xnT1", xn)
            read_out(pe, "xnT1")
            linear_tm("gate0", fa, lambda k: W("gate0", k), NE0)
            ranks("e0", NE0)
            experts("e0", NBLK0, UNITS0,
                    lambda s, q, k, m, rows: exw[:, s, (q * 2 + k) * HID0 + m * 128:(q * 2 + k) * HID0 + m * 128 + rows],
                    lambda s, m: exw[:, s, 4 * HID0 + m * D:4 * HID0 + (m + 1) * D], 1)

            pe.wait_ge(sem("xn2"), T)
            to_fm("xnT2", xn)
            read_out(pe, "xnT2")
            pe.wait_ge(sem("w1_in"), 16)
            linear_fm("gq", fa, "gq", K2)
            linear_fm("gk", fa, "gk", K2)
            linear_tm("gvs", fa, lambda k: W("gvs", k), 2 * D)
            pe.wait_ge(sem("cmix"), 1)
            for k in range(K2):
                bank, done = group(("ckv", k))
                for t in range(T):
                    mm = pe.matmul(bank[:, 0:128], ta[:, t, k * 128:(k + 1) * 128], tb[:, t, k * 128:(k + 1) * 128],
                                   start=(t == 0), stop=(t == T - 1))
                mm.then_inc(done, 1)
            read_out(pe, "ckv")
            for t in range(T):
                bank, done = group(("cout", t))
                for k in range(K2):
                    mm = pe.matmul(bank[0:P, k * 128:(k + 1) * 128], fa[:, k, t * P:(t + 1) * P], ckv[:, k, :],
                                   start=True, stop=True)
                mm.then_inc(done, 1)
            read_out(pe, "gq")
            read_out(pe, "gk")
            read_out(pe, "gvs")

            def l1_scores(i, m, h):
                k = h // 2
                for c, (off, w, _) in enumerate(CHUNKS):
                    bank, done = group(("l1", "s", i, c))
                    pe.matmul(bank[0:P, 0:w], fc[:, k, m * P:(m + 1) * P], fq[:, k, h % 2, off:off + w],
                              start=True, stop=True).then_inc(done, 1)

            pe.wait_ge(sem("fq_zeros"), 2)
            attend("l1", l1_scores, lambda t, h: xlr[:, t, h * HD:h * HD + VW], all_tiles)

            pe.wait_ge(sem("ah"), 1)
            to_fm("ahT", ta)
            read_out(pe, "ahT")
            for name in ("aq", "aqr", "ak", "akr"):
                linear_fm(name, fa, name, K2)
            linear_tm("av", fa, lambda k: W("av", k), 128)
            pe.wait_ge(sem("roped"), 12)
            read_out(pe, "av")

            def l2_scores(i, m, h):
                g = h // 2
                for c, off, w, _ in chunks_upto(m + 1):
                    bank, done = group(("l2", "s", i, c))
                    pe.matmul(bank[0:P, 0:w], fq[:, g, h % 2, m * P:(m + 1) * P], fc[:, g, off:off + w],
                              start=True, stop=True).then_inc(done, 1)

            attend("l2", l2_scores, lambda t, h: td[:, t, (h // 2) * HD:(h // 2) * HD + VW], causal_tiles)
            read_out(pe, "l2", "agg")
            to_fm("yT", te)
            read_out(pe, "yT")
            linear_tm("ao", fa, lambda k: W("ao", k), D)

            pe.wait_ge(sem("flat"), 1)
            to_fm("flatT", ta)
            read_out(pe, "flatT")
            linear_tm("gate1", fa, lambda k: W("gate1", k), NE1)
            ranks("e1", NE1)
            experts("e1", NBLK1, UNITS1,
                    lambda s, q, k, m, rows: exw[:, s, (q * 2 + k) * HID1 + m * 128:(q * 2 + k) * HID1 + m * 128 + rows],
                    lambda s, m: exw_r[:, s, :] if m == 5 else exw[:, s, 4 * HID1 + m * D:4 * HID1 + (m + 1) * D], 2)

        @block.vector
        def _(dve):
            own = Chain(dve, sem("dve_own"))
            v = nc.vector

            def inverse_root(dst, src, times, plus):
                n = dst.shape[1]
                val, bits, sq = root[:, 0, 0:n], root[:, 1, 0:n], root[:, 2, 0:n]
                own.link(v.tensor_scalar(val, src, times, plus, ALU.mult, ALU.add))
                own.link(v.tensor_scalar(bits.bitcast(I32), val.bitcast(I32), 1, None, ALU.logical_shift_right))
                own.link(v.tensor_scalar(dst.bitcast(I32), bits.bitcast(I32), -1.0, float(0x5F3759DF), ALU.mult,
                                         ALU.add))
                for _ in range(3):
                    own.link(v.tensor_tensor(sq, dst, dst, ALU.mult))
                    own.link(v.scalar_tensor_tensor(sq, sq, -0.5, val, ALU.mult, ALU.mult))
                    own.link(v.scalar_tensor_tensor(dst, sq, 1.5, dst, ALU.add, ALU.mult))

            def layernorm(src, dst, eps, done):
                for t in range(T):
                    own.note(v.bn_stats(stats[:, t, :], src[:, t, :]))
                own.fence()
                for t in range(T):
                    own.note(v.bn_aggr(mv[:, t, :], stats[:, t, :]))
                own.fence()
                inverse_root(rstd[:, :], mv[:, :, 1], 1.0, eps)
                for t in range(T):
                    v.tensor_scalar(dst[:, t, :], src[:, t, :], mv[:, t, 0:1], rstd[:, t:t + 1], ALU.subtract,
                                    ALU.mult).then_inc(done[0], 1)
                dve.wait_ge(done[0], done[1])

            def affine(dst, layer, g, b, done):
                own.link(v.tensor_tensor(dst[:, :, :], dst[:, :, :], V(layer, g), ALU.mult))
                v.tensor_tensor(dst[:, :, :], dst[:, :, :], V(layer, b), ALU.add).then_inc(done, 1)

            def rmsnorm(src, dst, weight, junk, done):
                for t in range(T):
                    own.note(v.tensor_tensor_reduce(junk[:, t, :], src[:, t, :], src[:, t, :], 1.0 / D, 0.0, ALU.mult,
                                                    ALU.add, rsum[:, t:t + 1]))
                own.fence()
                inverse_root(rstd[:, :], rsum[:, :], 1.0, 1e-6)
                for t in range(T):
                    ins = v.scalar_tensor_tensor(dst[:, t, :], src[:, t, :], rstd[:, t:t + 1], Vt(1, weight), ALU.mult,
                                                 ALU.mult)
                ins.then_inc(done, 1)

            def from_fm(name, dst):
                for c, (off, w, _) in enumerate(CHUNKS):
                    bank, freed = got(dve, (name, 1, c))
                    v.tensor_copy(dst[:, 1, off:off + w], bank[:, 0:w]).then_inc(freed, 1)

            def copy_indices(g, b):
                for w, a in enumerate((srci, dsti, celli)):
                    ins = v.tensor_copy(idx_ring[:, b % 4, w, :], a[:, bass.ds(g * G, G)])
                ins.then_inc(sem("indices"), 1)

            def score_group(g, b, ch):
                s = b % 2
                static = isinstance(g, int)
                dve.wait_ge(sem(f"gathered{s}"), (g - s) * (G * 16) + 2 * G * 16)
                zl, zr = gat[:, s, 0, :], gat[:, s, 1, :]
                ch.link(v.tensor_tensor(zl, zl, zr, ALU.add))
                ch.link(v.scalar_tensor_tensor(zr, zl, 0.2, zl, ALU.mult, ALU.max))
                ch.link(v.tensor_tensor(zl.rearrange("p (g c) -> p g c", g=G), zr.rearrange("p (g c) -> p g c", g=G),
                                        Vt(0, "att").unsqueeze(1).to_broadcast([P, G, D]), ALU.mult))
                if not (static and g < 2):
                    dve.wait_ge(sem("scattered"), (g - 1) * (G * 16))
                v.tensor_reduce(sc_ring[:, s, :, :].rearrange("p g h -> p (g h)"),
                                zl.rearrange("p (a c) -> p a c", c=HD), AX.X, ALU.add).then_inc(sem("scored"), 1)
                if not (static and g + 2 >= NG):
                    copy_indices(g + 2, b + 2)

            def onehots(g, b):
                s = b % 2
                after(dve, sem("onehot_used"), g - 1)
                for j in range(G):
                    for w, a in enumerate((srcf, dstf)):
                        ins = v.tensor_scalar(oh[:, s, w, j, :], iota_n[:, :], a[:, bass.ds(g * G + j, 1)], None,
                                              ALU.is_equal)
                ins.then_inc(sem("onehot"), 1)

            early = Chain(dve, sem("edge_own"))

            def score_early(*groups):
                for g in groups:
                    score_group(g, g, early)

            v.memset(cnt[:, :, :], 0.0).then_inc(sem("zeros"), 1)
            v.memset(zero16[:, :], 0.0).then_inc(sem("zero16"), 1)
            own.note(v.memset(mixw[:, :, :], 0.0))
            v.memset(mixk[:, :, :], 0.0).then_inc(sem("mixw0"), 1)
            dve.wait_ge(sem("x_in"), 16)
            layernorm(x, xn, 1e-5, (sem("xn0"), T))
            dve.wait_ge(sem("edges_in"), 32)
            own.note(v.tensor_copy(srcf[:, :], srci[:, :]))
            own.note(v.tensor_copy(dstf[:, :], dsti[:, :]))
            own.fence()
            own.link(v.scalar_tensor_tensor(cellf[:, :], dstf[:, :], float(N), srcf[:, :], ALU.mult, ALU.add))
            own.link(v.tensor_copy(celli[:, :], cellf[:, :]))

            copy_indices(0, 0)
            copy_indices(1, 1)
            from_fm("xnT0", fa)
            for t in range(T):
                bank, freed = got(dve, ("lr", t))
                v.tensor_copy(xlr[:, t, :], bank[0:P, :]).then_inc(freed, 1)
            layernorm(xn, ta, 1e-5, (sem("ln1"), T))
            dve.wait_ge(sem("vec0_in"), 16)
            affine(ta, 0, "ln1_g", "ln1_b", sem("mixh"))
            own.note(v.tensor_tensor(tb[:, :, :], xn[:, :, :], V(0, "bo"), ALU.add))
            from_fm("mixhT", fb_)
            dve.wait_ge(sem("fb_in"), 16)
            for c, (off, w, _) in enumerate(CHUNKS):
                bank, freed = got(dve, ("xm", 1, c))
                v.tensor_scalar(fc[:, 1, off:off + w], bank[:, 0:w], fbias[:, FB_BX + 1:FB_BX + 2], None, ALU.add)\
                    .then_inc(freed, 1)
            for t in range(T):
                bank, freed = got(dve, ("qv", t))
                qv = bank[0:P, 0:288].rearrange("p (h c) -> p h c", h=NBLK)
                own.note(v.tensor_copy(te[:, t, 0:32].rearrange("p (h r) -> p h r", h=NBLK), qv[:, :, 0:KR]))
                v.tensor_copy(td[:, t, :].rearrange("p (h c) -> p h c", h=NBLK), qv[:, :, KR:KR + DH])\
                    .then_inc(freed, 1)
            score_early(0)
            for c, (off, w, _) in enumerate(CHUNKS):
                bank, freed = got(dve, ("kT", c))
                v.tensor_copy(fd[0:32, 0, off:off + w], bank[0:32, 0:w]).then_inc(freed, 1)
            read_out(dve, "kT")
            own.link(v.tensor_reduce(kstat[:, 0:1], fd[0:32, 0, :], AX.X, ALU.max))
            v.tensor_scalar(kstat[:, 1:2], kstat[:, 0:1], -1.0, None, ALU.mult).then_inc(sem("kmax"), 1)
            own.fence()
            q4 = te[:, :, 0:32].rearrange("p t (h r) -> p t h r", h=NBLK)
            qst = hstat[:, 0, :].rearrange("p (t h) -> p t h", t=T)
            qsu = hstat[:, 1, :].rearrange("p (t h) -> p t h", t=T)

            def spread(a):
                return a.unsqueeze(3).to_broadcast([P, T, NBLK, KR])

            own.link(v.tensor_reduce(qst, q4, AX.X, ALU.max))
            v.tensor_tensor(q4, q4, spread(qst), ALU.subtract).then_inc(sem("qshift"), 1)
            dve.wait_ge(sem("kexp"), 1)
            own.link(v.reciprocal(kstat[:, 0:1], kstat[:, 2:3]))
            v.tensor_scalar(fd[0:32, 0, :], fd[0:32, 0, :], kstat[:, 0:1], None, ALU.mult).then_inc(sem("ksoft"), 1)
            dve.wait_ge(sem("qexp"), 1)
            own.link(v.tensor_reduce(qst, q4, AX.X, ALU.add))
            own.link(v.reciprocal(qsu, qst))
            v.tensor_tensor(q4, q4, spread(qsu), ALU.mult).then_inc(sem("qsoft"), 1)
            score_early(1)
            bank, freed = got(dve, "kN")
            v.tensor_copy(te[:, :, 32:64], bank[0:P, 0:160].rearrange("p (t r) -> p t r", t=T))\
                .then_inc(freed, 1)
            for c, (off, w, _) in enumerate(CHUNKS):
                bank, freed = got(dve, ("qT", c))
                v.tensor_copy(fd[0:32, 1, off:off + w], bank[0:32, 0:w]).then_inc(freed, 1)
            bank, freed = got(dve, "kv")
            dve.wait_ge(sem("blocks"), 1)
            v.tensor_tensor(kvbd[:, :], bank[0:32, 0:D], block4[:, :], ALU.mult)\
                .then_inc(freed, 1)
            for c, (off, w, _) in enumerate(CHUNKS):
                bank, freed = got(dve, ("qkv", 1, c))
                v.tensor_copy(fb_[:, 1, off:off + w], bank[:, 0:w]).then_inc(freed, 1)
            for t in range(T):
                bank, freed = got(dve, ("attn", t))
                v.tensor_tensor(tb[:, t, :], bank[0:P, 0:D], tb[:, t, :], ALU.add).then_inc(freed, 1)
            read_out(dve, "attn")
            score_early(2)
            layernorm(tb, ta, 1e-5, (sem("ln2"), T))
            affine(ta, 0, "ln2_g", "ln2_b", sem("h2"))
            own.link(v.tensor_tensor(tb[:, :, :], tb[:, :, :], V(0, "b2"), ALU.add))
            from_fm("h2T", fb_)
            score_early(3, 4)
            for t in range(T):
                bank, freed = got(dve, ("m2", t))
                v.tensor_tensor(tb[:, t, :], bank[0:P, 0:D], tb[:, t, :], ALU.add).then_inc(freed, 1)
            read_out(dve, "m2")
            score_early(*range(5, EARLY))

            def scores_and_onehots(z, n, o, per, ch):
                for b in range(n):
                    score_group(z + b, b, ch)
                    for c in range(per):
                        onehots(o + (b * per + c), c % 2)

            dve.wait_ge(sem("iotas"), 4)
            scores_and_onehots(EARLY, 4, 0, 2, early)
            with dve.Fori(0, PACED) as i:
                scores_and_onehots(i * 4 + (EARLY + 4), 4, i * 8 + 8, 2,
                                   Chain(dve, sem("edge_own"), i * (4 * EDGE_LINKS) + (EARLY + 4) * EDGE_LINKS))
            for z in range(EARLY + 4 + 4 * PACED, NG):
                score_group(z, z, Chain(dve, sem("edge_own"), z * EDGE_LINKS))

            REST = N - 512
            dve.wait_ge(sem("counted"), 1)
            dve.wait_ge(sem("zeros_out"), T * 16)
            for m in range(T):
                own.note(v.tensor_copy(cnt[:, m, 0:512], banks[m][0:P, :]))
            own.note(v.tensor_copy(cnt[:, 0:4, 512:N], banks[5][0:P, 0:4 * REST].rearrange("p (m n) -> p m n", m=4)))
            v.tensor_copy(cnt[:, 4, 512:N], banks[6][0:P, 0:REST]).then_inc(sem("counts_out"), 1)
            own.fence()
            dve.wait_ge(sem("counts_out"), 1)
            own.link(v.tensor_scalar(nmask[:, :, :], cnt[:, :, :], 0.0, -BIG, ALU.is_equal, ALU.mult))

            def attend(name, take_scores, tiles_of, weigh, guard, dst):
                def maxima(i):
                    m, h = steps[i]
                    if not weigh and i >= 3:
                        dve.wait_ge(sem(name + "_prob"), i - 2)
                    take_scores(i, m, h)
                    v.tensor_scalar(rneg[:, i:i + 1], rmx[:, i:i + 1], -1.0, None, ALU.mult)\
                        .then_inc(sem(name + "_max"), 1)

                def weights(i):
                    if not weigh:
                        return
                    m, h = steps[i]
                    dve.wait_ge(sem(name + "_exp"), i + 1)
                    if i >= 3:
                        read_out(dve, name, "pT", i - 3)
                    v.tensor_tensor_reduce(prob[:, i % 3, :], expd[:, i % 3, :], cnt[:, m, :], 1.0, 0.0, ALU.mult,
                                           ALU.add, rden[:, i:i + 1]).then_inc(sem(name + "_prob"), 1)

                def normalize(m):
                    cols = slice(m * H, (m + 1) * H)
                    dve.wait_ge(sem(name + "_prob"), (m + 1) * H)
                    own.link(guard(rrec[:, cols], rden[:, cols]))
                    own.link(v.reciprocal(rrec[:, cols], rrec[:, cols]))
                    dve.wait_ge(sem(name + "_sum"), (m + 1) * H)
                    b = 6 + m % 2
                    v.tensor_tensor(dst[:, m, :].rearrange("p (h c) -> p h c", h=H),
                                    banks[b][0:P, :].rearrange("p (h c) -> p h c", h=H)[:, :, 0:HD],
                                    rrec[:, cols].unsqueeze(2).to_broadcast([P, H, HD]), ALU.mult)\
                        .then_inc(free[b], 1)

                n = len(steps)
                for i in range(n + 2):
                    if i < n:
                        maxima(i)
                    if i >= 2:
                        weights(i - 2)
                    if i >= 7 and (i - 7) % H == 0:
                        normalize((i - 7) // H)
                normalize(T - 1)
                read_out(dve, name, "agg")

            def l0_take(i, m, h):
                dve.wait_ge(sem(f"sdense{m % 2}"), 16 * (m // 2 + 1))
                v.tensor_tensor_reduce(masked[:, i % 3, :], sdense[:, m % 2, :, h], nmask[:, m, :], 1.0, -3e38,
                                       ALU.add, ALU.max, rmx[:, i:i + 1]).then_inc(sem("l0_taken"), 1)
                dve.wait_ge(sem("l0_taken"), i + 1)

            def from_banks(name, mask, scale, tiles_of):
                def take(i, m, h):
                    parts = chunks_upto(tiles_of(m))
                    for c, off, w, _ in parts:
                        bank, freed = got(dve, (name, "s", i, c))
                        v.tensor_tensor_reduce(
                            masked[:, i % 3, off:off + w], bank[0:P, 0:w], mask(m, off, w), scale, -3e38,
                            ALU.add, ALU.max, (rmx if c == 0 else rmx_a)[:, i:i + 1]).then_inc(freed, 1)
                    read_out(dve, name, "s", i)
                    if len(parts) == 2:
                        own.link(v.tensor_tensor(rmx[:, i:i + 1], rmx[:, i:i + 1], rmx_a[:, i:i + 1], ALU.max))
                return take

            attend("l0", l0_take, all_tiles, True,
                   lambda o, a: v.tensor_scalar(o, a, 1e-16, None, ALU.add), te)
            own.link(v.tensor_tensor(te[:, :, :], te[:, :, :], V(0, "g_bias"), ALU.add))
            v.tensor_scalar(tc[:, :, :], te[:, :, :], 0.0, None, ALU.min).then_inc(sem("elu_min"), 1)
            dve.wait_ge(sem("elu_exp"), 1)
            own.link(v.scalar_tensor_tensor(te[:, :, :], te[:, :, :], 0.0, tc[:, :, :], ALU.max, ALU.add))
            own.link(v.scalar_tensor_tensor(te[:, :, :], te[:, :, :], -1.0, xn[:, :, :], ALU.add, ALU.add))
            layernorm(te, ta, 1e-5, (sem("ln_g0"), T))
            affine(ta, 0, "g_gamma", "g_beta", sem("g0"))
            dve.wait_ge(sem("g0"), 1)
            own.link(v.tensor_tensor(x[:, :, :], x[:, :, :], ta[:, :, :], ALU.add))
            own.link(v.tensor_tensor(x[:, :, :], x[:, :, :], tb[:, :, :], ALU.add))

            def route(name, gate_name, ne, nblk, bias, eps):
                for t in range(T):
                    bank, freed = got(dve, (gate_name, t))
                    if bias is None:
                        ins = v.tensor_copy(lg[:, t, 0:ne], bank[0:P, 0:ne])
                    else:
                        ins = v.tensor_tensor(lg[:, t, 0:ne], bank[0:P, 0:ne], bias, ALU.add)
                    ins.then_inc(freed, 1)
                read_out(dve, gate_name)
                wide = lambda a: a[:, :].unsqueeze(2).to_broadcast([P, T, ne])
                own.link(v.tensor_reduce(rmax[:, :], lg[:, :, 0:ne], AX.X, ALU.max))
                v.tensor_tensor(lg[:, :, 0:ne], lg[:, :, 0:ne], wide(rmax), ALU.subtract)\
                    .then_inc(sem(gate_name + "_sh"), 1)
                dve.wait_ge(sem(gate_name + "_exp"), 1)
                own.link(v.tensor_reduce(rsum[:, :], pr[:, :, 0:ne], AX.X, ALU.add))
                own.link(v.reciprocal(rinv[:, :], rsum[:, :]))
                own.link(v.tensor_tensor(pr[:, :, 0:ne], pr[:, :, 0:ne], wide(rinv), ALU.mult))
                for t in range(T):
                    own.note(v.max(top8[:, t, :], pr[:, t, 0:ne]))
                own.fence()
                for t in range(T):
                    own.note(v.max_index(topi[:, t, :], top8[:, t, :], pr[:, t, 0:ne]))
                own.fence()
                own.link(v.tensor_copy(topf[:, :, :], topi[:, :, :]))
                for t in range(T):
                    for j in range(2):
                        own.note(v.tensor_scalar(pick[:, j, t, :], iota_e[:, :], topf[:, t, j:j + 1], None,
                                                 ALU.is_equal))
                own.fence()
                v.tensor_tensor(pick16[:, :, :], pick[:, 0, :, :], pick[:, 1, :, :], ALU.add)\
                    .then_inc(sem(name + "_picked"), 1)
                own.link(v.tensor_tensor(rsum[:, :], top8[:, :, 0], top8[:, :, 1], ALU.add))
                own.link(v.tensor_scalar(rsum[:, :], rsum[:, :], eps, None, ALU.add))
                own.link(v.reciprocal(rinv[:, :], rsum[:, :]))
                own.link(v.tensor_tensor(wtop[:, :, :], top8[:, :, 0:2],
                                         rinv[:, :].unsqueeze(2).to_broadcast([P, T, 2]), ALU.mult))
                for what, dst in (("rank", rank), ("total", total)):
                    bank, freed = got(dve, (name, what))
                    v.tensor_copy(dst[:, :, :].rearrange("p t e -> p (t e)"), bank[0:P, 0:T * NE0])\
                        .then_inc(freed, 1)
                read_out(dve, name, "rank")
                read_out(dve, name, "total")
                for t in range(1, T):
                    own.note(v.tensor_tensor(rank[:, t, :], rank[:, t, :], total[:, t - 1, :], ALU.add))
                    own.link(v.tensor_tensor(total[:, t, :], total[:, t, :], total[:, t - 1, :], ALU.add))
                own.link(v.tensor_scalar(nblocks_i[:, :], total[:, T - 1, :], float(SLOTS - 1), None, ALU.add))
                own.link(v.tensor_scalar(nblocks_i[:, :], nblocks_i[:, :], SLOTS.bit_length() - 1, None,
                                         ALU.logical_shift_right))
                own.link(v.tensor_copy(nblocks[:, :], nblocks_i[:, :]))
                own.link(v.tensor_tensor(eprod[:, :, :], before_e[:, :, :],
                                         nblocks[:, :].unsqueeze(1).to_broadcast([P, NE0, NE0]), ALU.mult))
                own.link(v.tensor_reduce(first[:, :], eprod[:, :, :], AX.X, ALU.add))
                own.link(v.tensor_tensor(upto[:, :], first[:, :], nblocks[:, :], ALU.add))
                own.link(v.tensor_tensor(bcmp[:, 0:nblk, 0:ne], iota_b[:, 0:nblk].unsqueeze(2).to_broadcast([P, nblk, ne]),
                                         upto[:, 0:ne].unsqueeze(1).to_broadcast([P, nblk, ne]), ALU.is_ge))
                own.link(v.tensor_reduce(bown[:, 0:nblk], bcmp[:, 0:nblk, 0:ne], AX.X, ALU.add))
                v.tensor_scalar(bown_i[:, 0:nblk], bown[:, 0:nblk], float(ne - 1), None, ALU.min)\
                    .then_inc(sem(name + "_owners"), 1)
                own.link(v.tensor_scalar(first[:, :], first[:, :], float(SLOTS), None, ALU.mult))
                own.link(v.tensor_tensor(rank[:, :, :], rank[:, :, :],
                                         first[:, :].unsqueeze(1).to_broadcast([P, T, NE0]), ALU.add))
                for j in range(2):
                    own.link(v.tensor_tensor(pick[:, j, :, :], pick[:, j, :, :], rank[:, :, :], ALU.mult))
                    own.link(v.tensor_reduce(slotf[:, j, :], pick[:, j, :, :], AX.X, ALU.add))
                own.note(v.tensor_copy(slot_rel[:, :], slotf[:, :, :].rearrange("p j t -> p (j t)")))
                v.tensor_copy(sloti[:, :, :], slotf[:, :, :]).then_inc(sem(name + "_slots"), 1)
                own.fence()

            def experts(name, nblk, units):
                nu = len(units)

                def select(b, s):
                    after(dve, sem(name + "_nodes"), b - 1)
                    after(dve, sem(name + "_shift"), b)
                    v.tensor_tensor(sel[:, s, :, :], iota_s[:, :].unsqueeze(1).to_broadcast([P, 2 * T, SLOTS]),
                                    slot_rel[:, :].unsqueeze(2).to_broadcast([P, 2 * T, SLOTS]), ALU.is_equal)\
                        .then_inc(sem(name + "_sel"), 1)
                    dve.wait_ge(sem(name + "_sel"), b + 1)
                    v.tensor_scalar(slot_rel[:, :], slot_rel[:, :], float(SLOTS), None, ALU.subtract)\
                        .then_inc(sem(name + "_shift"), 1)

                def node_ids(b, s):
                    dve.wait_ge(sem(name + "_nodes"), b + 1)
                    after(dve, sem(name + "_turned"), b - 1)
                    v.tensor_copy(ids[:, s, :], banks[7][:, 0:1]).then_inc(sem(name + "_ids"), 1)

                def step(b, s):
                    if not (isinstance(b, int) and b + 2 >= nblk):
                        node_ids(b + 2, s)
                    if not (isinstance(b, int) and b + 3 >= nblk):
                        select(b + 3, 1 - s)
                    after(dve, sem(name + "_out"), b - 1)
                    for j, tiles in enumerate(units):
                        buf = j if nu == 2 else s
                        dve.wait_ge(sem(name + "_silu"), b * nu + (j + 1))
                        for i0, m0, n, rows in runs(tiles):
                            ins = v.tensor_tensor(hid[0:rows, s, m0:m0 + n, :],
                                                  banks[3 + buf][0:rows, i0 * SLOTS:(i0 + n) * SLOTS]
                                                  .rearrange("p (m n) -> p m n", n=SLOTS),
                                                  silu[0:rows, buf, i0:i0 + n, :], ALU.mult)
                        ins.then_inc(sem(name + "_mul"), 1)
                    if not (isinstance(b, int) and b == 0):
                        copy_y(b - 1, 1 - s)

                def copy_y(b, s):
                    dve.wait_ge(sem(name + "_out"), b + 1)
                    if not (isinstance(b, int) and b < 2):
                        dve.wait_ge(sem(f"{name}_stored{s}"), (b - s) * 8)
                    v.tensor_copy(ys[:, s, :], banks[5 + s][:, 0:D]).then_inc(sem(name + "_ycopied"), 1)

                select(0, 0)
                select(1, 1)
                node_ids(0, 0)
                node_ids(1, 1)
                select(2, 0)
                block_steps(dve, nblk, step)
                copy_y(nblk - 1, (nblk - 1) % 2)
                dve.wait_ge(sem(name + "_back"), 2 * T * 16)
                for j in range(2):
                    for t in range(T):
                        v.scalar_tensor_tensor(x[:, t, :], yg[:, j, t, :], wtop[:, t, j:j + 1], x[:, t, :],
                                               ALU.mult, ALU.add).then_inc(sem(name + "_added"), 1)
                    dve.wait_ge(sem(name + "_added"), (j + 1) * T)

            layernorm(x, xn, 1e-5, (sem("xn1"), T))
            from_fm("xnT1", fa)
            route("e0", "gate0", NE0, NBLK0, vec[:, V_GATEB:V_GATEB + NE0], 0.0)
            experts("e0", NBLK0, UNITS0)

            layernorm(x, xn, 1e-5, (sem("xn2"), T))
            heads = lambda a: a[:, :, :].rearrange("p t (h c) -> p (t h) c", h=NBLK)
            hb = lambda r: hstat[:, r, :].unsqueeze(2).to_broadcast([P, T * NBLK, DH])
            own.link(v.tensor_reduce(hstat[:, 0, :], heads(xn), AX.X, ALU.add))
            own.link(v.tensor_scalar(hstat[:, 0, :], hstat[:, 0, :], 1.0 / DH, None, ALU.mult))
            own.link(v.tensor_tensor(heads(ta), heads(xn), hb(0), ALU.subtract))
            own.link(v.tensor_tensor(tb[:, :, :], ta[:, :, :], ta[:, :, :], ALU.mult))
            own.link(v.tensor_reduce(hstat[:, 1, :], heads(tb), AX.X, ALU.add))
            inverse_root(hstat[:, 2, :], hstat[:, 1, :], 1.0 / (DH - 1), 0.0)
            own.link(v.scalar_tensor_tensor(hstat[:, 1, :], hstat[:, 1, :], 1.0 / (DH - 1), hstat[:, 2, :], ALU.mult,
                                            ALU.mult))
            own.link(v.tensor_scalar(hstat[:, 1, :], hstat[:, 1, :], 1e-5, None, ALU.add))
            own.link(v.reciprocal(hstat[:, 2, :], hstat[:, 1, :]))
            own.link(v.tensor_tensor(heads(ta), heads(ta), hb(2), ALU.mult))
            dve.wait_ge(sem("vec1_in"), 16)
            own.link(v.tensor_tensor(tb[:, :, :], ta[:, :, :], V(1, "vln_w"), ALU.mult))
            own.link(v.tensor_tensor(tb[:, :, :], tb[:, :, :], V(1, "vln_b"), ALU.add))
            affine(ta, 1, "kln_w", "kln_b", sem("cmix"))
            from_fm("xnT2", fa)
            for c, (off, w, _) in enumerate(CHUNKS):
                bank, freed = got(dve, ("gq", 1, c))
                for rows, to in halves(1, off, w):
                    ins = v.tensor_scalar(to, bank[rows, 0:w], fbias[rows, FB_BQ + 1:FB_BQ + 2], None, ALU.add)
                ins.then_inc(freed, 1)
            for c, (off, w, _) in enumerate(CHUNKS):
                bank, freed = got(dve, ("gk", 1, c))
                v.tensor_scalar(fc[:, 1, off:off + w], bank[:, 0:w], fbias[:, FB_BK + 1:FB_BK + 2], None, ALU.add)\
                    .then_inc(freed, 1)
            for t in range(T):
                bank, freed = got(dve, ("gvs", t))
                v.tensor_tensor(xlr[:, t, :], bank[0:P, :], Vt(1, "bv", 2 * D), ALU.add)\
                    .then_inc(freed, 1)
            for k in range(K2):
                bank, freed = got(dve, ("ckv", k))
                v.scalar_tensor_tensor(ckv[:, k, :], bank[:, 0:128], 1.0 / N, block32[:, :], ALU.mult, ALU.mult)\
                    .then_inc(freed, 1)
            for t in range(T):
                bank, freed = got(dve, ("cout", t))
                v.tensor_tensor(tc[:, t, :], bank[0:P, 0:D], xn[:, t, :], ALU.add).then_inc(freed, 1)
            attend("l1", from_banks("l1", lambda m, off, w: nmask[:, m, off:off + w], HD ** -0.5, all_tiles),
                   all_tiles, True, lambda o, a: v.tensor_scalar(o, a, 1e-30, None, ALU.max), te)
            own.link(v.tensor_tensor(ta[:, :, :], xlr[:, :, D:2 * D], te[:, :, :], ALU.subtract))
            for j, (a, w) in enumerate(((xlr[:, :, D:2 * D], "wg_skip"), (te, "wg_rst"), (ta, "wg_diff"))):
                for t in range(T):
                    own.note(v.tensor_tensor_reduce(tb[:, t, :], a[:, t, :], Vt(1, w), 1.0, 0.0, ALU.mult, ALU.add,
                                                    gpart[:, j, t:t + 1]))
                own.fence()
            own.link(v.tensor_tensor(gate[:, :], gpart[:, 0, :], gpart[:, 1, :], ALU.add))
            v.tensor_tensor(gate[:, :], gate[:, :], gpart[:, 2, :], ALU.add).then_inc(sem("glogit"), 1)
            dve.wait_ge(sem("gated"), 1)
            for t in range(T):
                own.note(v.scalar_tensor_tensor(te[:, t, :], ta[:, t, :], gate[:, t:t + 1], te[:, t, :], ALU.mult,
                                                ALU.add))
            own.fence()
            layernorm(te, ta, 1e-5, (sem("ln_g1"), T))
            affine(ta, 1, "ln_w", "ln_b", sem("g1"))
            dve.wait_ge(sem("g1"), 1)
            own.link(v.tensor_scalar(te[:, :, :], ta[:, :, :], 0.0, vec[:, V_PRELU:V_PRELU + 1], ALU.min, ALU.mult))
            own.link(v.scalar_tensor_tensor(ta[:, :, :], ta[:, :, :], 0.0, te[:, :, :], ALU.max, ALU.add))
            own.link(v.tensor_tensor(x[:, :, :], x[:, :, :], ta[:, :, :], ALU.add))
            read_out(dve, "cout")
            own.link(v.tensor_tensor(x[:, :, :], x[:, :, :], tc[:, :, :], ALU.add))

            layernorm(x, xn, 1e-5, (sem("xn3"), T))
            rmsnorm(xn, ta, "rms1", tb, sem("ah"))
            from_fm("ahT", fa)
            dve.wait_ge(sem("rope_in"), 16)
            for name, f in (("aq", fb_), ("ak", fc)):
                for m in range(K2):
                    for c, (off, w, _) in enumerate(CHUNKS):
                        bank, freed = got(dve, (name, m, c))
                        v.tensor_tensor(f[:, m, off:off + w], bank[:, 0:w], rope[:, 0, off:off + w],
                                        ALU.mult).then_inc(freed, 1)
                read_out(dve, name)
                for m in range(K2):
                    for c, (off, w, _) in enumerate(CHUNKS):
                        bank, freed = got(dve, (name + "r", m, c))
                        v.tensor_tensor(fd[:, m, off:off + w], bank[:, 0:w], rope[:, 1, off:off + w],
                                        ALU.mult).then_inc(freed, 1)
                        read_out(dve, name + "r", m, c)
                        for rows, to in (halves(m, off, w) if name == "aq" else [(slice(0, 128), f[:, m, off:off + w])]):
                            v.tensor_tensor(to, f[rows, m, off:off + w], fd[rows, m, off:off + w], ALU.add)\
                                .then_inc(sem("roped"), 1)
            for t in range(T):
                bank, freed = got(dve, ("av", t))
                v.tensor_copy(td[:, t, 0:128], bank[0:P, 0:128]).then_inc(freed, 1)
            attend("l2", from_banks("l2", lambda m, off, w: lower[:, (T - 1 - m) * P + off:(T - 1 - m) * P + off + w],
                                    HD ** -0.5, causal_tiles),
                   causal_tiles, False, lambda o, a: v.tensor_copy(o, a), te)
            from_fm("yT", fa)
            for t in range(T):
                bank, freed = got(dve, ("ao", t))
                v.tensor_tensor(tb[:, t, :], bank[0:P, 0:D], xn[:, t, :], ALU.add).then_inc(freed, 1)
            read_out(dve, "ao")
            rmsnorm(tb, ta, "rms2", td, sem("flat"))
            own.link(v.tensor_tensor(x[:, :, :], x[:, :, :], tb[:, :, :], ALU.add))
            from_fm("flatT", fa)
            route("e1", "gate1", NE1, NBLK1, None, 1e-9)
            experts("e1", NBLK1, UNITS1)

        @block.scalar
        def _(act):
            a = nc.scalar

            def from_fm(name, dst):
                for c, (off, w, _) in enumerate(CHUNKS):
                    bank, freed = got(act, (name, 0, c))
                    a.activation(dst[:, 0, off:off + w], bank[:, 0:w], ACT.Copy).then_inc(freed, 1)

            def biased(name, f, bias, func=ACT.Identity, tiles=(0,)):
                for m in tiles:
                    for c, (off, w, _) in enumerate(CHUNKS):
                        bank, freed = got(act, (name, m, c))
                        a.activation(f[:, m, off:off + w], bank[:, 0:w], func, bias=fbias[:, bias + m:bias + m + 1])\
                            .then_inc(freed, 1)

            from_fm("xnT0", fa)
            from_fm("mixhT", fb_)
            act.wait_ge(sem("fb_in"), 16)
            biased("xm", fc, FB_BX)
            act.wait_ge(sem("kmax"), 1)
            a.activation(fd[0:32, 0, :], fd[0:32, 0, :], ACT.Exp, bias=kstat[:, 1:2], accum_out=kstat[:, 2:3])\
                .then_inc(sem("kexp"), 1)
            act.wait_ge(sem("qshift"), 1)
            a.activation(te[:, :, 0:32], te[:, :, 0:32], ACT.Exp).then_inc(sem("qexp"), 1)
            for c, (off, w, _) in enumerate(CHUNKS):
                bank, freed = got(act, ("qkv", 0, c))
                a.activation(fb_[:, 0, off:off + w], bank[:, 0:w], ACT.Copy).then_inc(freed, 1)
            from_fm("h2T", fb_)
            biased("m1", mlp, FB_B1, ACT.Gelu, range(FF // 128))

            def attend(name, tiles_of, weigh):
                def exponentials(i):
                    w = tiles_of(steps[i][0]) * P
                    act.wait_ge(sem(name + "_max"), i + 1)
                    if weigh:
                        if i >= 3:
                            act.wait_ge(sem(name + "_prob"), i - 2)
                        a.activation(expd[:, i % 3, 0:w], masked[:, i % 3, 0:w], ACT.Exp, bias=rneg[:, i:i + 1])\
                            .then_inc(sem(name + "_exp"), 1)
                    else:
                        if i >= 3:
                            read_out(act, name, "pT", i - 3)
                        a.activation(prob[:, i % 3, 0:w], masked[:, i % 3, 0:w], ACT.Exp, bias=rneg[:, i:i + 1],
                                     accum_out=rden[:, i:i + 1]).then_inc(sem(name + "_prob"), 1)

                def turned_out(i):
                    if i >= 3:
                        act.wait_ge(sem(name + "_sum"), i - 2)
                    for c, off, w, _ in chunks_upto(tiles_of(steps[i][0])):
                        bank, freed = got(act, (name, "pT", i, c))
                        a.activation(probT[:, i % 3, off:off + w], bank[0:P, 0:w], ACT.Copy).then_inc(freed, 1)

                for i in range(len(steps) + 2):
                    if i < len(steps):
                        exponentials(i)
                    if i >= 2:
                        turned_out(i - 2)

            def shares(name, ne):
                act.wait_ge(sem(name + "_sh"), 1)
                a.activation(pr[:, :, 0:ne], lg[:, :, 0:ne], ACT.Exp).then_inc(sem(name + "_exp"), 1)

            def experts(name, nblk, units):
                nu = len(units)

                def copy_turned(b, s):
                    act.wait_ge(sem(name + "_turned"), b + 1)
                    after(act, sem(name + "_hid"), (b - 1) * nu)
                    a.activation(xsT[:, s, :, :], banks[0][:, 0:2 * SLOTS].rearrange("p (k n) -> p k n", k=K2),
                                 ACT.Copy).then_inc(sem(name + "_xsT"), 1)

                def store(b, s):
                    act.wait_ge(sem(name + "_ycopied"), b + 1)
                    act.dma_start(slot_y[bass.ds(b * SLOTS, SLOTS), :], ys[:, s, :])\
                        .then_inc(sem(f"{name}_stored{s}"), 16)

                def step(b, s):
                    static = isinstance(b, int)
                    if not (static and b + 1 >= nblk):
                        copy_turned(b + 1, 1 - s)
                    for j, tiles in enumerate(units):
                        buf = j if nu == 2 else s
                        act.wait_ge(sem(name + "_hid"), b * nu + (j + 1))
                        after(act, sem(name + "_mul"), b * nu + (j - 1))
                        for i0, m0, n, rows in runs(tiles):
                            ins = a.activation(silu[0:rows, buf, i0:i0 + n, :],
                                               banks[1 + buf][0:rows, i0 * SLOTS:(i0 + n) * SLOTS]
                                               .rearrange("p (m n) -> p m n", n=SLOTS), ACT.Silu)
                        ins.then_inc(sem(name + "_silu"), 1)
                    if not (static and b == 0):
                        store(b - 1, 1 - s)

                copy_turned(0, 0)
                block_steps(act, nblk, step)
                store(nblk - 1, (nblk - 1) % 2)

            attend("l0", all_tiles, True)
            act.wait_ge(sem("elu_min"), 1)
            a.activation(tc[:, :, :], tc[:, :, :], ACT.Exp).then_inc(sem("elu_exp"), 1)
            from_fm("xnT1", fa)
            shares("gate0", NE0)
            experts("e0", NBLK0, UNITS0)
            from_fm("xnT2", fa)
            act.wait_ge(sem("e0_added"), 2 * T)
            for c, (off, w, _) in enumerate(CHUNKS):
                bank, freed = got(act, ("gq", 0, c))
                for rows, to in halves(0, off, w):
                    ins = a.activation(to, bank[rows, 0:w], ACT.Identity, bias=fbias[rows, FB_BQ:FB_BQ + 1])
                ins.then_inc(freed, 1)
            biased("gk", fc, FB_BK)
            attend("l1", all_tiles, True)
            act.wait_ge(sem("glogit"), 1)
            a.activation(gate[:, :], gate[:, :], ACT.Sigmoid, bias=vec[:, V_BGATE:V_BGATE + 1])\
                .then_inc(sem("gated"), 1)
            from_fm("ahT", fa)
            attend("l2", causal_tiles, False)
            from_fm("yT", fa)
            from_fm("flatT", fa)
            shares("gate1", NE1)
            experts("e1", NBLK1, UNITS1)

        @block.gpsimd
        def _(pool):
            p = nc.gpsimd
            own = Chain(pool, sem("pool_own"))
            own.note(p.memset(ident[:, :], 0.0))
            own.note(p.memset(lower[:, :], 0.0))
            own.note(p.memset(block4[:, :], 1.0))
            own.note(p.memset(block32[:, :], 0.0))
            own.fence()
            p.affine_select(out=ident[:, :], in_=ident[:, :], compare_op=ALU.not_equal, fill=1.0, base=0,
                            pattern=[[-1, 128]], channel_multiplier=1).then_inc(sem("ident"), 2)
            p.iota(iota_n[:, :], pattern=[[1, OH]], base=0, channel_multiplier=0,
                   allow_small_or_imprecise_dtypes=True).then_inc(sem("iotas"), 1)
            p.iota(iota_s[:, :], pattern=[[1, SLOTS]], base=0, channel_multiplier=0,
                   allow_small_or_imprecise_dtypes=True).then_inc(sem("iotas"), 1)
            p.iota(node_id[:, :, :], pattern=[[P, T], [0, 2]], base=0, channel_multiplier=1,
                   allow_small_or_imprecise_dtypes=True).then_inc(sem("iotas"), 1)
            p.iota(iota_e[:, :], pattern=[[1, NE0]], base=0, channel_multiplier=0,
                   allow_small_or_imprecise_dtypes=True).then_inc(sem("iotas"), 1)
            own.note(p.affine_select(out=lower[:, :], in_=lower[:, :], compare_op=ALU.is_ge, fill=-BIG,
                                     base=(T - 1) * P, pattern=[[-1, N]], channel_multiplier=1))
            b4 = block4[:, :].rearrange("p (b c) -> p b c", b=NBLK)
            own.link(p.affine_select(out=b4, in_=b4, compare_op=ALU.is_ge, fill=0.0, base=0,
                                     pattern=[[-KR, NBLK], [0, DH]], channel_multiplier=1))
            own.link(p.affine_select(out=b4, in_=b4, compare_op=ALU.is_ge, fill=0.0, base=KR - 1,
                                     pattern=[[KR, NBLK], [0, DH]], channel_multiplier=-1))
            own.note(p.memset(before[:, :], 1.0))
            own.note(p.memset(before_e[:, :, :], 1.0))
            own.fence()
            own.note(p.affine_select(out=before[:, :], in_=before[:, :], compare_op=ALU.is_gt, fill=0.0, base=0,
                                     pattern=[[1, P]], channel_multiplier=-1))
            own.note(p.affine_select(out=before_e[:, :, :], in_=before_e[:, :, :], compare_op=ALU.is_gt, fill=0.0,
                                     base=0, pattern=[[1, NE0], [-1, NE0]], channel_multiplier=0))
            own.note(p.memset(ones16[:, :], 1.0))
            own.note(p.iota(iota_b[:, :], pattern=[[1, NBLK0]], base=0, channel_multiplier=0,
                            allow_small_or_imprecise_dtypes=True))
            own.fence()
            for q in range(4):
                ins = p.memset(block32[32 * q:32 * q + 32, 32 * q:32 * q + 32], 1.0)
            ins.then_inc(sem("blocks"), 1)

            def gather(g, b, j):
                for w, tab in enumerate((xl_tab, xr_tab)):
                    p.indirect_dma_start(
                        out=gat[:, b % 2, w, j * D:(j + 1) * D], out_offset=None, in_=tab,
                        in_offset=bass.IndirectOffsetOnAxis(ap=idx_ring[:, b % 4, w, j:j + 1], axis=0))\
                        .then_inc(sem(f"gathered{b % 2}"), 16)

            def scatter(g, b, j):
                if not (isinstance(g, int) and g == 0 and j == 0):
                    pool.wait_ge(sem("scattered"), g * (G * 16) + j * 16)
                    pool.sem_inc(sem("pool_turn"), 1)
                p.indirect_dma_start(
                    out=pair_scores, in_=sc_ring[:, b % 2, j, :], in_offset=None,
                    out_offset=bass.IndirectOffsetOnAxis(ap=idx_ring[:, b % 4, 2, j:j + 1], axis=0))\
                    .then_inc(sem("scattered"), 16)

            def turn(g, b):
                pool.wait_ge(sem("indices"), g + 1)
                pool.wait_ge(sem("scored"), g - 1)
                pool.sem_inc(sem("pool_turn"), 1)
                for j in range(G):
                    gather(g, b, j)
                    scatter(g - 2, b - 2, j)

            pool.wait_ge(sem("tables"), 32)
            for g in range(2):
                pool.wait_ge(sem("indices"), g + 1)
                for j in range(G):
                    gather(g, g, j)
            pool.wait_ge(sem("zeros_out"), 16 * T)
            turn(2, 2)
            turn(3, 3)
            with pool.Fori(1, NG // 4) as i:
                for b in range(4):
                    turn(i * 4 + b, b)
            for g in (NG - 2, NG - 1):
                pool.wait_ge(sem("scored"), g + 1)
                for j in range(G):
                    scatter(g, g, j)
            pool.wait_ge(sem("scattered"), EC * 16)

            def choices(name, tab, nblk):
                def gather_rows(b, s):
                    pool.wait_ge(sem(name + "_ids"), b + 1)
                    after(pool, sem(name + "_turned"), b - 1)
                    pool.sem_inc(sem("pool_turn"), 1)
                    p.indirect_dma_start(out=xs[:, s, :], out_offset=None, in_=tab,
                                         in_offset=bass.IndirectOffsetOnAxis(ap=ids[:, s, :], axis=0))\
                        .then_inc(sem(f"{name}_xs{s}"), 16)

                pool.wait_ge(sem(name + "_tab"), 16)
                block_steps(pool, nblk, gather_rows)
                for s in range(2):
                    pool.wait_ge(sem(f"{name}_stored{s}"), 16 * ((nblk + 1 - s) // 2))
                for j in range(2):
                    for t in range(T):
                        p.indirect_dma_start(out=yg[:, j, t, :], out_offset=None, in_=slot_y,
                                             in_offset=bass.IndirectOffsetOnAxis(ap=sloti[:, j, t:t + 1], axis=0))\
                            .then_inc(sem(name + "_back"), 16)

            choices("e0", row_tab[0], NBLK0)
            pool.wait_ge(sem("e0_added"), 2 * T)
            for q in range(2):
                p.memset(fq[(1 - q) * HD:(2 - q) * HD, :, q, :], 0.0).then_inc(sem("fq_zeros"), 1)
            choices("e1", row_tab[1], NBLK1)

        @block.sync
        def _(sp):
            sp.dma_start(x[:, :, :], x_in.rearrange("(t p) d -> p t d", p=P)).then_inc(sem("x_in"), 16)
            n_lr = WOFF["lr"][1]
            sp.dma_start(wres[:, :, 0:n_lr], w0_in[:, :, 0:n_lr]).then_inc(sem("wlr_in"), 16)
            sp.dma_start(srci[:, :], src_in).then_inc(sem("edges_in"), 16)
            sp.dma_start(dsti[:, :], dst_in).then_inc(sem("edges_in"), 16)
            sp.dma_start(vec[:, 0:V_SIZE0], vec0_in.partition_broadcast(P)).then_inc(sem("vec0_in"), 16)
            sp.dma_start(fbias[:, :], fb_in).then_inc(sem("fb_in"), 16)
            sp.dma_start(wres[:, :, n_lr:W_SIZES[0]], w0_in[:, :, n_lr:]).then_inc(sem("w0_in"), 16)
            sp.wait_ge(sem("mixw0"), 1)
            for q in range(4):
                rows = slice(32 * q, 32 * q + 32)
                sp.dma_start(mixw[rows, q, :], mixw_in[:, 0:KR + DH]).then_inc(sem("mixw_in"), 16)
                for k in range(K2):
                    at = (4 * k + q) * KR
                    sp.dma_start(mixk[rows, k, at:at + KR], mixw_in[:, KR + DH:]).then_inc(sem("mixw_in"), 16)
            cells = pair_scores.rearrange("(m p n) h -> m p (n h)", m=T, p=P)

            def zero_cells(tiles):
                for m in tiles:
                    sp.dma_start(cells[m], cnt[:, 0:4, :].rearrange("p m n -> p (m n)"))\
                        .then_inc(sem("zeros_out"), 16)

            sp.wait_ge(sem("zeros"), 1)
            zero_cells(range(3))
            read_out(sp, "lr")
            for w, tab in enumerate((xl_tab, xr_tab)):
                sp.dma_start(tab.rearrange("(t p) d -> p t d", p=P), xlr[:, :, w * D:(w + 1) * D])\
                    .then_inc(sem("tables"), 16)
            zero_cells(range(3, T))
            sp.dma_start(w2, w2_in).then_inc(sem("w2_in"), 16)
            sp.wait_ge(sem("scattered"), EC * 16)
            sp.wait_ge(sem("counts_out"), 1)
            for m in range(T):
                if m >= 2:
                    sp.wait_ge(sem("l0_taken"), (m - 1) * H)
                sp.dma_start(sdense[:, m % 2, :, :].rearrange("p n h -> p (n h)"), cells[m])\
                    .then_inc(sem(f"sdense{m % 2}"), 16)

            def expert_weights(name, nblk, nu, hid_cols, main, rest):
                end_in, end = 4 * hid_cols, main.shape[2]

                def owned(b, *weights):
                    owner = sp.value_load(bown_i[0:1, bass.ds(b, 1)], min_val=0, max_val=main.shape[0] - 1)
                    return [w[bass.ds(owner, 1)].rearrange("e p n -> (e p) n") for w in weights]

                def load_out(b, s):
                    w, *w_rest = owned(b, main, *rest)
                    after(sp, sem(name + "_out"), b - 1)
                    sp.dma_start(exw[:, s, end_in:end], w[:, end_in:end]).then_inc(sem(f"{name}_wout{s}"), 16)
                    for part in w_rest:
                        sp.dma_start(exw_r[:, s, :], part).then_inc(sem(f"{name}_wout{s}"), 16)

                def load(b, s):
                    w, = owned(b, main)
                    after(sp, sem(name + "_hid"), (b - 1) * nu)
                    sp.dma_start(exw[:, s, 0:end_in], w[:, 0:end_in]).then_inc(sem(f"{name}_in{s}"), 16)
                    if not (isinstance(b, int) and b == 0):
                        load_out(b - 1, 1 - s)

                sp.wait_ge(sem(name + "_owners"), 1)
                block_steps(sp, nblk, load)
                load_out(nblk - 1, (nblk - 1) % 2)

            def store_rows(name, tab, src):
                sp.dma_start(tab.rearrange("(t p) d -> p t d", p=P), src[:, :, :]).then_inc(sem(name + "_tab"), 16)

            sp.wait_ge(sem("xn1"), T)
            store_rows("e0", row_tab[0], xn)
            expert_weights("e0", NBLK0, 1, HID0, exp0_in, [])
            sp.wait_ge(sem("e0_slots"), 1)
            sp.dma_start(wres[:, :, 0:W_SIZES[1]], w1_in).then_inc(sem("w1_in"), 16)
            sp.dma_start(vec[:, 0:V_SIZE], vec1_in.partition_broadcast(P)).then_inc(sem("vec1_in"), 16)
            sp.wait_ge(sem("e0_added"), 2 * T)
            sp.dma_start(rope, rope_in).then_inc(sem("rope_in"), 16)
            read_out(sp, "l2", "agg")
            sp.wait_ge(sem("flat"), 1)
            store_rows("e1", row_tab[1], ta)
            expert_weights("e1", NBLK1, 2, HID1, exp1_in, [exp1r_in])
            sp.wait_ge(sem("e1_added"), 2 * T)
            sp.dma_start(out.rearrange("(t p) d -> p t d", p=P), x[:, :, :]).then_inc(sem("out"), 16)
            sp.wait_ge(sem("out"), 16)


def kernel(**inputs):
    import concourse.bacc as bacc
    from concourse.bass_utils import run_bass_kernel_spmd

    a = {k: np.asarray(v) for k, v in inputs.items()}

    def halves(*ws):
        w = np.concatenate(ws, axis=-1)
        return w.reshape(K2, 128, w.shape[-1]).transpose(1, 0, 2)

    def columns(v):
        return v.reshape(-1, 128).T

    l0 = [a["L0_gnn_att"], a["L0_gnn_bias"], a["L0_gnn_gamma"], a["L0_gnn_beta"], a["L0_mix_ln1_g"],
          a["L0_mix_ln1_b"], a["L0_mix_bo"], a["L0_mix_ln2_g"], a["L0_mix_ln2_b"], a["L0_mix_b2"],
          a["L0_ffn_gate_b"]]
    l1 = [a["L1_gnn_bv"], a["L1_gnn_bskip"], a["L1_gnn_Wgate"], a["L1_gnn_ln_w"], a["L1_gnn_ln_b"],
          a["L1_mix_kln_weight"], a["L1_mix_kln_bias"], a["L1_mix_vln_weight"], a["L1_mix_vln_bias"],
          a["L1_ffn_ln1_w"], a["L1_ffn_ln2_w"], a["L1_gnn_bgate"], a["L1_gnn_prelu_a"]]
    other = np.arange(D).reshape(H, 2, HD // 2)[:, ::-1].reshape(D)
    wq, wk = a["L1_ffn_wq"].T, a["L1_ffn_wk"].T
    twice = np.repeat(np.arange(128).reshape(2, HD), 2, axis=0).reshape(D)
    wk2 = wk[:, twice]
    inv_freq = 1.0 / 10000.0 ** (np.arange(0, HD, 2, dtype=np.float32) / HD)
    freqs = np.outer(np.arange(N, dtype=np.float32), inv_freq)
    emb = np.concatenate([freqs, freqs], axis=-1)
    sign = np.concatenate([-np.ones(HD // 2), np.ones(HD // 2)])
    rope = np.stack([np.tile(np.cos(emb).T, (2, 1)), np.tile((np.sin(emb) * sign).T, (2, 1))], axis=1)

    def expert(win, wgate, wout):
        n_exp, _, hidden = win.shape
        main = hidden // 128 * 128
        parts = [win.reshape(n_exp, K2, 128, hidden).transpose(0, 2, 1, 3).reshape(n_exp, 128, -1),
                 wgate.reshape(n_exp, K2, 128, hidden).transpose(0, 2, 1, 3).reshape(n_exp, 128, -1),
                 wout[:, :main].reshape(n_exp, -1, 128, D).transpose(0, 2, 1, 3).reshape(n_exp, 128, -1)]
        return np.concatenate(parts, axis=2), wout[:, main:]

    exp0, _ = expert(a["L0_ffn_w1"], a["L0_ffn_w2"], a["L0_ffn_w3"])
    exp1, exp1r = expert(a["L1_ffn_w1"].transpose(0, 2, 1), a["L1_ffn_w3"].transpose(0, 2, 1),
                         a["L1_ffn_w2"].transpose(0, 2, 1))
    arrays = {
        "x": a["x"],
        "src": a["src"].reshape(P, EC),
        "dst": a["dst"].reshape(P, EC),
        "vec0": np.concatenate([v.reshape(-1) for v in l0]),
        "vec1": np.concatenate([v.reshape(-1) for v in l1]),
        "fb": np.concatenate([columns(a[n]) for n in ("L0_mix_bx", "L0_mix_b1", "L1_gnn_bq", "L1_gnn_bk")], axis=1),
        "w0": halves(a["L0_gnn_W_l"], a["L0_gnn_W_r"], a["L0_mix_Wx"], a["L0_mix_Wo"], a["L0_mix_W1"],
                     a["L0_ffn_gate_w"]),
        "w1": halves(a["L1_gnn_Wq"].T, a["L1_gnn_Wk"].T, a["L1_gnn_Wv"].T, a["L1_gnn_Wskip"].T, wq, wq[:, other],
                     wk2, wk2[:, other], a["L1_ffn_wv"].T, a["L1_ffn_wo"].T, a["L1_ffn_router_w"].T),
        "w2": a["L0_mix_W2"].reshape(FF // 128, 128, D).transpose(1, 0, 2),
        "mixw": np.concatenate([a["L0_mix_Wq"], a["L0_mix_Wv"], a["L0_mix_Wk"]], axis=1),
        "exp0": exp0,
        "exp1": exp1,
        "exp1r": exp1r,
        "rope": rope.astype(np.float32),
    }
    nc = bacc.Bacc("TRN2", target_bir_lowering=False, num_devices=1)
    in_map, args = {}, []
    for name, v in arrays.items():
        v = np.ascontiguousarray(v)
        in_map[f"in_{name}"] = v
        args.append(nc.dram_tensor(f"in_{name}", v.shape, mybir.dt.from_np(v.dtype), kind="ExternalInput").ap())
    args.append(nc.dram_tensor("out_x", (N, D), F32, kind="ExternalOutput").ap())
    build(nc, *args)
    return run_bass_kernel_spmd(nc, [in_map], core_ids=[0]).results[0]["out_x"]
```

```python
from contextlib import ExitStack

import numpy as np
import concourse.bass as bass
from concourse import mybir

ALU = mybir.AluOpType
ACT = mybir.ActivationFunctionType
AX = mybir.AxisListType
F32 = mybir.dt.float32
BF16 = mybir.dt.bfloat16
F32R = mybir.dt.float32r
FP16 = mybir.dt.float16
I32 = mybir.dt.int32
U32 = mybir.dt.uint32

N, D, E = 625, 256, 20000
P, T = 125, 5
K2 = D // 128
CHUNKS = [(0, 375, (0, 1, 2)), (375, 250, (3, 4))]
H = 4
HD = D // H
EC = E // P
G = 5
NG = EC // G
NBLK = 8
DH = D // NBLK
KR = 4
FF = 4 * D
NE0, HID0 = 16, 512
NE1, HID1 = 8, 682
BIG = 1e30
OH = N + 1
BANKS = 8
SINGLE = 6
LOWEST = -3e38
VW = 96
LATE = SINGLE + 2
ONEHOTS = (2, 2)
BEHIND = LATE - sum(ONEHOTS)
assert BEHIND % 2 == 0 and len(ONEHOTS) == LATE - 6
EDGE_LINKS = 3
ROUNDS = [(0, 2), (2, 2)]
XR_COLS = sum(n for _, n in ROUNDS)
ROUND_COUNTS = [range(0, 2), range(2, G)]
NODE_TILES = [(0, 1), (2, 3, 4)]
assert (NG - LATE) % 4 == 0 and LATE % 4 == 0 and NG - LATE > 8

VECS = [["att", "g_bias", "g_gamma", "g_beta", "ln1_g", "ln1_b", "bo", "ln2_g", "ln2_b", "b2"],
        ["bv", "bskip", "wg_skip", "wg_rst", "wg_diff", "ln_w", "ln_b", "kln_w", "kln_b", "vln_w", "vln_b",
         "rms1", "rms2"]]
V_GATEB = len(VECS[0]) * D
V_SIZE0 = V_GATEB + NE0
V_BGATE = len(VECS[1]) * D
V_PRELU = V_BGATE + 1
V_SIZE = V_PRELU + 1
FB_BX, FB_B1, FB_BQ, FB_BK, FB_SIZE = 0, 2, 10, 12, 14
WCOLS = [[("lr", 512), ("wx", 256), ("wo", 256), ("w1", FF), ("gate0", NE0)],
         [("gq", 256), ("gk", 256), ("gvs", 512), ("aq", 256), ("aqr", 256), ("ak", 256), ("akr", 256), ("av", 128),
          ("ao", 256), ("gate1", NE1)]]
WOFF, W_SIZES = {}, []
for _layer in WCOLS:
    _at = 0
    for _n, _c in _layer:
        WOFF[_n] = (_at, _c)
        _at += _c
    W_SIZES.append(_at)
SLOTS = 128
NBLK0 = (2 * N - NE0) // SLOTS + NE0
HT0, HT1 = 128, 114
TILES0 = [(m, min(HT0, HID0 - m * HT0)) for m in range((HID0 + HT0 - 1) // HT0)]
TILES1 = [(m, min(HT1, HID1 - m * HT1)) for m in range((HID1 + HT1 - 1) // HT1)]
UNITS0 = [TILES0]
UNITS1 = [TILES1[:4], TILES1[4:]]
NBLK1 = (2 * N - NE1) // SLOTS + NE1


def after(eng, sem, value):
    if not (isinstance(value, int) and value <= 0):
        eng.wait_ge(sem, value)


def block_steps(eng, nblk, step):
    for b in range(3):
        step(b, b % 2)
    pairs = (nblk - 3 - 4) // 2
    with eng.Fori(0, pairs) as i:
        step(i * 2 + 3, 1)
        step(i * 2 + 4, 0)
    for b in range(3 + 2 * pairs, nblk):
        step(b, b % 2)


def scores_written(which, g, j, b):
    if isinstance(g, int) and g < SINGLE:
        return 16 * (g * G + j) * (1 - which)
    odd = (b + j) % 2
    before = 16 * SINGLE * G * (1 - which) + 8 * (j - SINGLE * G + odd * (1 - 2 * which))
    return g * (8 * G) + before


class Chain:

    def __init__(self, eng, sem, base=0):
        self.eng, self.sem, self.base, self.n = eng, sem, base, 0

    def note(self, ins):
        self.n += 1
        return ins.then_inc(self.sem, 1)

    def fence(self):
        self.eng.wait_ge(self.sem, self.base + self.n)

    def link(self, ins):
        self.note(ins)
        self.fence()


ARENA = 18436


def build(nc, x_in, src_in, dst_in, dst_cols_in, vec0_in, vec1_in, fb_in, w0_in, w1_in, w2_in, mixw_in, exp0_in,
          exp0o_in, exp1_in, exp1o_in, exp1r_in, rope_in, out):
    ctx = ExitStack()
    with ctx:
        sems = {}

        def sem(name):
            if name not in sems:
                sems[name] = ctx.enter_context(nc.semaphore(name))
            return sems[name]

        def sb(name, shape, dt=F32):
            return ctx.enter_context(nc.sbuf_tensor(name, shape, dt))

        xl_tab = nc.dram_tensor("xl_tab", [N, D], F32).ap()
        xr_tab = nc.dram_tensor("xr_tab", [N, D], F32).ap()
        row_tab = [nc.dram_tensor(f"row_tab{i}", [N, D], F32).ap() for i in range(2)]
        slot_y = nc.dram_tensor("slot_y", [NBLK0 * SLOTS, D], F32).ap()
        pair_scores = [nc.dram_tensor(f"pair_scores{i}", [N * N, H], F32).ap() for i in range(2)]

        vec = sb("vec", [P, V_SIZE])
        fbias = sb("fbias", [128, FB_SIZE])
        wres = sb("wres", [128, K2, max(W_SIZES)])
        mixw = sb("mixw", [128, 4, KR + DH])
        mixk = sb("mixk", [128, K2, NBLK * KR])
        ident = sb("ident", [128, 128])
        lower = sb("lower", [P, N])
        block4 = sb("block4", [NBLK * KR, D])
        block32 = sb("block32", [128, 128])
        iota_n = sb("iota_n", [P, OH], FP16)
        iota_e = sb("iota_e", [P, NE0])
        zero16 = sb("zero16", [1, 512], BF16)
        x, xn, ta, tb, tc, td, te = (sb(n, [P, T, D]) for n in ("x", "xn", "ta", "tb", "tc", "td", "te"))
        xlr = sb("xlr", [P, T, 2 * D])
        fa, fb_, fc, fd = (sb(n, [128, K2, N]) for n in ("fa", "fb", "fc", "fd"))
        kvbd = sb("kvbd", [NBLK * KR, D])
        ckv = sb("ckv", [128, K2, 128])
        stats, mv, rstd = sb("stats", [P, T, 6]), sb("mv", [P, T, 2]), sb("rstd", [P, T])
        hstat = sb("hstat", [P, 4, T * NBLK])
        root = sb("root", [P, 3, T * NBLK])
        kstat = sb("kstat", [NBLK * KR, 3])
        lg, pr = sb("lg", [P, T, NE0]), sb("pr", [P, T, NE0])
        rmax, rsum, rinv = sb("rmax", [P, T]), sb("rsum", [P, T]), sb("rinv", [P, T])
        top8, topi, topf = sb("top8", [P, T, 8]), sb("topi", [P, T, 8], U32), sb("topf", [P, T, 8])
        wtop = sb("wtop", [P, T, 2])
        pick = sb("pick", [P, 2, T, NE0])
        pick16 = sb("pick16", [P, T, NE0], BF16)
        rank, total = sb("rank", [P, T, NE0]), sb("total", [P, T, NE0])
        nblocks, first, upto = sb("nblocks", [P, NE0]), sb("first", [P, NE0]), sb("upto", [P, NE0])
        eprod = fd[0:P, 0, 0:NE0 * NE0].rearrange("p (a b) -> p a b", b=NE0)
        bcmp = fd[0:P, 1, 0:NBLK0 * NE0].rearrange("p (a b) -> p a b", b=NE0)
        bown = sb("bown", [P, NBLK0])
        nblocks_i, bown_i = sb("nblocks_i", [P, NE0], I32), sb("bown_i", [P, NBLK0], I32)
        slotf, sloti = sb("slotf", [P, 2, T]), sb("sloti", [P, 2, T], I32)
        before = sb("before", [P, P], BF16)
        ones16 = sb("ones16", [P, P], BF16)
        before_e = sb("before_e", [P, NE0, NE0])
        iota_b = sb("iota_b", [P, NBLK0])
        node_f = sb("node_f", [P, T])
        iota_s = sb("iota_s", [P, SLOTS], FP16)
        node_id = sb("node_id", [P, T, 2], FP16)
        slot_rel = sb("slot_rel", [P, 2 * T])
        ids = sb("ids", [SLOTS, 2, 1], I32)
        gpart, gate = sb("gpart", [P, 3, T]), sb("gate", [P, T])
        rmx, rneg, rden, rrec = (sb(n, [P, T * H]) for n in ("rmx", "rneg", "rden", "rrec"))
        rmx_a = sb("rmx_a", [P, T * H])
        edge_ids = sb("edge_ids", [P, 3, EC], I32)
        srci, dsti, celli = (edge_ids[:, w, :] for w in range(3))
        srcf, dstf = (sb(n, [P, EC]) for n in ("srcf", "dstf"))
        cellf = tc[:, 0, 0:EC]
        idx_ring = sb("idx_ring", [P, 4, 3, G], I32)
        sc_ring = sb("sc_ring", [P, 2, G, H])
        cnt = sb("cnt", [P, T, N])
        nmask = sb("nmask", [P, T, N], BF16)

        with nc.sbuf_tensor("arena", [128, ARENA], F32) as arena:
            pass
        sb("pad0", [128, G * D])
        late_hi = sb("late_hi", [128, T, D], F32R)
        sb("pad1", [128, G * D])
        late_lo = sb("late_lo", [128, T, D], F32R)
        sb("pad2", [128, 2 * G * OH])
        late_ohT = sb("late_ohT", [128, 2, T, G * P], F32R)
        gat = arena[0:P, 0:4 * G * D].rearrange("p (s w c) -> p s w c", s=2, w=2)
        at = 4 * G * D
        oh = arena[0:P, at:at + 2 * G * OH].bitcast(BF16).rearrange("p (s w g n) -> p s w g n", s=2, w=2, g=G)
        at += 2 * G * OH
        ohT, xr_hi, xr_lo = late_ohT[0:P], late_hi[0:P], late_lo[0:P]
        gat_xr = arena[0:P, ARENA - 2 * D:].rearrange("p (s c) -> p s c", s=2)
        assert at + 2 * T * G * P <= ARENA - 2 * D
        dst_row = fc[0:P, :, :].rearrange("p k n -> p (k n)").bitcast(I32).rearrange("p (s n) -> p s n", s=2)
        xr_parts = [xr_hi, xr_lo]
        w2 = arena[:, at:at + FF // 128 * D].rearrange("p (k n) -> p k n", n=D)
        at += FF // 128 * D
        mlp = arena[:, at:at + FF // 128 * N].rearrange("p (k n) -> p k n", n=N)
        assert at + FF // 128 * N <= ARENA
        sdense = arena[0:P, 0:4 * H * N].rearrange("p (s w n h) -> p s w n h", s=2, w=2, h=H)
        at = 4 * H * N
        masked, expd, prob, probT = (arena[0:P, at + i * 3 * N:at + (i + 1) * 3 * N].rearrange("p (s n) -> p s n", s=3)
                                     for i in range(4))
        assert at + 12 * N <= ARENA
        at = 0
        rope = arena[:, at:at + 2 * N].rearrange("p (w n) -> p w n", w=2)
        at += 2 * N
        fq = arena[:, at:at + 2 * K2 * N].rearrange("p (k w n) -> p k w n", k=K2, w=2)
        assert at + 2 * K2 * N <= 4 * H * N
        exw = arena[:, 0:2 * 4 * HID1].rearrange("p (s n) -> p s n", s=2)
        at = 2 * 4 * HID1
        exo = arena[:, at:at + 2 * 5 * D].rearrange("p (s n) -> p s n", s=2)
        at += 2 * 5 * D
        exo_r = arena[0:TILES1[-1][1], at:at + 2 * D].rearrange("p (s n) -> p s n", s=2)
        at += 2 * D
        xs = arena[:, at:at + 2 * D].rearrange("p (s d) -> p s d", s=2)
        at += 2 * D
        xsT = arena[:, at:at + 2 * K2 * SLOTS].rearrange("p (s k n) -> p s k n", s=2, k=K2)
        at += 2 * K2 * SLOTS
        silu = arena[:, at:at + 2 * 4 * SLOTS].rearrange("p (s m n) -> p s m n", s=2, m=4)
        at += 2 * 4 * SLOTS
        hid = arena[:, at:at + 2 * 6 * SLOTS].rearrange("p (s m n) -> p s m n", s=2, m=6)
        at += 2 * 6 * SLOTS
        ys = arena[:, at:at + 2 * D].rearrange("p (s d) -> p s d", s=2)
        at += 2 * D
        yg = arena[0:P, at:at + 2 * T * D].rearrange("p (k t d) -> p k t d", k=2, t=T)
        at += 2 * T * D
        sel = arena[0:P, at:at + 2 * T * SLOTS].bitcast(FP16).rearrange("p (s q n) -> p s q n", s=2, n=SLOTS)
        assert at + 2 * T * SLOTS <= ARENA

        banks = [ctx.enter_context(nc.psum_tensor(f"bank{b}", [128, 512], F32)) for b in range(BANKS)]
        full = [sem(f"full{b}") for b in range(BANKS)]
        free = [sem(f"free{b}") for b in range(BANKS)]
        uses = [0] * BANKS
        fulls = [0] * BANKS
        ring = {"at": 0, "n": BANKS}
        ticket = {}

        def V(layer, name):
            i = VECS[layer].index(name) * D
            return vec[:, i:i + D].unsqueeze(1).to_broadcast([P, T, D])

        def Vt(layer, name, width=D):
            i = VECS[layer].index(name) * D
            return vec[:, i:i + width]

        def W(name, k):
            o, c = WOFF[name]
            return wres[:, k, o:o + c]

        def got(eng, name):
            b, n, _ = ticket[name if isinstance(name, tuple) else (name,)]
            eng.wait_ge(full[b], n)
            return banks[b], free[b]

        def read_out(eng, *key):
            last = {}
            for name, (b, _, n) in ticket.items():
                if name[:len(key)] == key:
                    last[b] = max(last.get(b, 0), n)
            assert last, key
            for b, n in last.items():
                eng.wait_ge(free[b], n)

        def halves(k, off, w):
            return [(slice(q * HD, (q + 1) * HD), fq[q * HD:(q + 1) * HD, k, q, off:off + w]) for q in range(2)]

        steps = [(m, h) for m in range(T) for h in range(H)]
        causal_tiles = lambda m: m + 1
        all_tiles = lambda m: T

        def chunks_upto(ns):
            found = []
            for c, (off, w, tiles) in enumerate(CHUNKS):
                tiles = [t for t in tiles if t < ns]
                if tiles:
                    found.append((c, off, len(tiles) * P, tiles))
            return found

        def runs(tiles):
            found = []
            for i, (m, rows) in enumerate(tiles):
                if found and found[-1][3] == rows:
                    found[-1][2] += 1
                else:
                    found.append([i, m, 1, rows])
            return found

        block = ctx.enter_context(nc.Block())

        @block.tensor
        def _(pe):
            def group(name):
                b = ring["at"] % ring["n"]
                ring["at"] += 1
                return bank_for(name, b)

            def bank_for(name, b):
                if uses[b]:
                    pe.wait_ge(free[b], uses[b])
                uses[b] += 1
                fulls[b] += 1
                ticket[name if isinstance(name, tuple) else (name,)] = (b, fulls[b], uses[b])
                return banks[b], full[b]

            def all_free():
                for b in range(BANKS):
                    pe.wait_ge(free[b], uses[b])

            def to_fm(name, src):
                for k in range(K2):
                    for c, (off, w, tiles) in enumerate(CHUNKS):
                        bank, done = group((name, k, c))
                        for t in tiles:
                            mm = pe.transpose(bank[:, t * P - off:t * P - off + P],
                                              src[:, t, k * 128:(k + 1) * 128], ident[0:P, 0:P])
                        mm.then_inc(done, 1)

            def linear_tm(name, f, rhs, width, ks=K2):
                for t in range(T):
                    bank, done = group((name, t))
                    for k in range(ks):
                        mm = pe.matmul(bank[0:P, 0:width], f[:, k, t * P:(t + 1) * P], rhs(k),
                                       start=(k == 0), stop=(k == ks - 1))
                    mm.then_inc(done, 1)

            def linear_fm(name, f, weights, m_tiles, ks=K2):
                for m in range(m_tiles):
                    for c, (off, w, _) in enumerate(CHUNKS):
                        bank, done = group((name, m, c))
                        for k in range(ks):
                            mm = pe.matmul(bank[:, 0:w], W(weights, k)[:, m * 128:(m + 1) * 128],
                                           f[:, k, off:off + w], start=(k == 0), stop=(k == ks - 1))
                        mm.then_inc(done, 1)

            pe.wait_ge(sem("ident"), 2)
            pe.wait_ge(sem("xn0"), T)
            to_fm("xnT0", xn)
            pe.wait_ge(sem("wlr_in"), 16)
            read_out(pe, "xnT0")
            linear_tm("lr", fa, lambda k: W("lr", k), 2 * D)

            pe.wait_ge(sem("w0_in"), 16)
            pe.wait_ge(sem("mixh"), 1)
            to_fm("mixhT", ta)
            read_out(pe, "mixhT")
            linear_fm("xm", fb_, "wx", K2)
            read_out(pe, "xm")
            pe.wait_ge(sem("mixw_in"), 12 * 16)
            for t in range(T):
                bank, done = group(("qv", t))
                for k in range(K2):
                    mm = pe.matmul(bank[0:P, k * 144:k * 144 + 144], fc[:, k, t * P:(t + 1) * P],
                                   mixw[:, :, :].rearrange("p a b -> p (a b)"), start=True, stop=True)
                mm.then_inc(done, 1)
            for c, (off, w, _) in enumerate(CHUNKS):
                bank, done = group(("kT", c))
                for k in range(K2):
                    mm = pe.matmul(bank[0:32, 0:w], mixk[:, k, :], fc[:, k, off:off + w],
                                   start=(k == 0), stop=(k == 1))
                mm.then_inc(done, 1)
            pe.wait_ge(sem("ksoft"), 1)
            bank, done = group("kN")
            for t in range(T):
                mm = pe.transpose(bank[0:P, t * 32:t * 32 + 32], fd[0:32, 0, t * P:(t + 1) * P], ident[0:32, 0:32])
            mm.then_inc(done, 1)
            pe.wait_ge(sem("qsoft"), 1)
            for c, (off, w, tiles) in enumerate(CHUNKS):
                bank, done = group(("qT", c))
                for t in tiles:
                    mm = pe.transpose(bank[0:32, t * P - off:t * P - off + P], te[:, t, 0:32], ident[0:P, 0:P])
                mm.then_inc(done, 1)
            read_out(pe, "kN")
            read_out(pe, "qv")
            bank, done = group("kv")
            for t in range(T):
                mm = pe.matmul(bank[0:32, 0:D], te[:, t, 32:64], td[:, t, :], start=(t == 0), stop=(t == T - 1))
            mm.then_inc(done, 1)
            read_out(pe, "kv")
            read_out(pe, "qT")
            for m in range(K2):
                for c, (off, w, _) in enumerate(CHUNKS):
                    bank, done = group(("qkv", m, c))
                    pe.matmul(bank[:, 0:w], kvbd[:, m * 128:(m + 1) * 128], fd[0:32, 1, off:off + w],
                              start=True, stop=True).then_inc(done, 1)
            read_out(pe, "qkv")
            linear_tm("attn", fb_, lambda k: W("wo", k), D)
            pe.wait_ge(sem("h2"), 1)
            to_fm("h2T", ta)
            read_out(pe, "h2T")
            linear_fm("m1", fb_, "w1", FF // 128)
            read_out(pe, "m1")
            pe.wait_ge(sem("w2_in"), 16)
            linear_tm("m2", mlp, lambda k: w2[:, k, :], D, ks=FF // 128)

            REST = N - 512
            all_free()
            pe.wait_ge(sem("zero16"), 1)

            def zeros(first):
                for m in range(T):
                    pe.matmul(banks[m][0:P, 0:512], zero16[0:1, 0:P], zero16[0:1, 0:512], start=first, stop=not first,
                              skip_group_check=True)
                pe.matmul(banks[5][0:P, 0:4 * REST], zero16[0:1, 0:P], zero16[0:1, 0:4 * REST], start=first,
                          stop=not first, skip_group_check=True)
                return pe.matmul(banks[6][0:P, 0:REST], zero16[0:1, 0:P], zero16[0:1, 0:REST], start=first,
                                 stop=not first, skip_group_check=True)

            zeros(True)
            def count(s, columns):
                for j in columns:
                    for m in range(T):
                        lhsT = oh[:, s, 1, j, m * P:(m + 1) * P]
                        pe.matmul(banks[m][0:P, 0:512], lhsT, oh[:, s, 0, j, 0:512], start=False, stop=False,
                                  skip_group_check=True)
                        rest = banks[5][0:P, m * REST:(m + 1) * REST] if m < 4 else banks[6][0:P, 0:REST]
                        mm = pe.matmul(rest, lhsT, oh[:, s, 0, j, 512:N], start=False, stop=False,
                                       skip_group_check=True)
                return mm

            def count_group(g, s):
                pe.wait_ge(sem("onehot"), g + 1)
                count(s, range(G)).then_inc(sem("onehot_used"), 1)

            with pe.Fori(0, (LATE - BEHIND) // 2) as i:
                for s in range(2):
                    count_group(i * 2 + s, s)

            def late_group(g, b):
                s = b % 2
                pe.wait_ge(sem("onehotT"), g - (LATE - 1))
                for r, (first, n) in enumerate(ROUNDS):
                    after(pe, sem("xr_read"), g * len(ROUNDS) + (r - LATE * len(ROUNDS)))
                    for j in range(n):
                        for part in range(2):
                            for t in range(T):
                                mm = pe.matmul(banks[7][0:P, j * D:(j + 1) * D],
                                               ohT[:, s, t, (first + j) * P:(first + j + 1) * P],
                                               xr_parts[part][:, t, :], start=(part == 0 and t == 0),
                                               stop=(part == 1 and t == T - 1))
                    mm.then_inc(sem("xr_made"), 1)
                    if r == 0:
                        pe.wait_ge(sem("onehot"), g + (1 - BEHIND))
                    mm = count(s, ROUND_COUNTS[r])
                mm.then_inc(sem("onehot_used"), 1)

            pe.wait_ge(sem("xr_parts"), 1)
            for b in range(4):
                late_group(LATE + b, b)
            with pe.Fori(LATE // 4 + 1, NG // 4) as i:
                for b in range(4):
                    late_group(i * 4 + b, b)
            for g in range(NG - BEHIND, NG):
                count_group(g, g % 2)
            zeros(False).then_inc(sem("counted"), 1)
            pe.wait_ge(sem("counts_out"), 1)

            def attend(name, scores, v_rows, tiles_of):
                ring["n"] = 6

                def turn(i):
                    pe.wait_ge(sem(name + "_prob"), i + 1)
                    for c, off, w, tiles in chunks_upto(tiles_of(steps[i][0])):
                        bank, done = group((name, "pT", i, c))
                        for t in tiles:
                            mm = pe.transpose(bank[0:P, t * P - off:t * P - off + P],
                                              prob[:, i % 3, t * P:(t + 1) * P], ident[0:P, 0:P])
                        mm.then_inc(done, 1)

                def sum_v(i):
                    m, h = steps[i]
                    b = 6 + m % 2
                    if h == 0 and uses[b]:
                        pe.wait_ge(free[b], uses[b])
                    read_out(pe, name, "pT", i)
                    for t in range(tiles_of(m)):
                        mm = pe.matmul(banks[b][0:P, h * 128:h * 128 + VW], probT[:, i % 3, t * P:(t + 1) * P],
                                       v_rows(t, h), start=(t == 0), stop=(t == tiles_of(m) - 1))
                    mm.then_inc(sem(name + "_sum"), 1)
                    if h == H - 1:
                        uses[b] += 1
                        ticket[(name, "agg", m)] = (b, 0, uses[b])

                if scores:
                    scores(0, *steps[0])
                for i in range(len(steps) + 3):
                    if i + 1 < len(steps) and scores:
                        scores(i + 1, *steps[i + 1])
                    if 2 <= i < len(steps) + 2:
                        turn(i - 2)
                    if i >= 3:
                        sum_v(i - 3)
                ring["n"] = BANKS

            attend("l0", None, lambda t, h: xlr[:, t, h * HD:h * HD + VW], all_tiles)

            def experts(name, nblk, units, w_in, w_out, n_out):
                nu = len(units)

                def row_nodes(b, s):
                    pe.wait_ge(sem(name + "_sel"), b + 1)
                    after(pe, sem(name + "_ids"), b)
                    for q in range(2 * T):
                        mm = pe.matmul(banks[7][:, 0:2], sel[:, s, q, :], node_id[:, q % T, :], start=(q == 0),
                                       stop=(q == 2 * T - 1))
                    mm.then_inc(sem(name + "_nodes"), 1)

                def turn_rows(b, s):
                    pe.wait_ge(sem(f"{name}_xs{s}"), (b - s) * 8 + 16)
                    after(pe, sem(name + "_xsT"), b)
                    for k in range(K2):
                        mm = pe.transpose(banks[0][:, k * 128:(k + 1) * 128], xs[:, s, k * 128:(k + 1) * 128],
                                          ident[:, :])
                    mm.then_inc(sem(name + "_turned"), 1)

                def hidden(b, s):
                    pe.wait_ge(sem(f"{name}_in{s}"), (b - s) * 8 + 16)
                    pe.wait_ge(sem(name + "_xsT"), b + 1)
                    for j, tiles in enumerate(units):
                        buf = j if nu == 2 else s
                        after(pe, sem(name + "_mul"), b * nu + (j - 1))
                        for q in range(2):
                            for i, (m, rows) in enumerate(tiles):
                                for k in range(K2):
                                    mm = pe.matmul(banks[1 + 2 * q + buf][0:rows, i * SLOTS:(i + 1) * SLOTS],
                                                   w_in(s, q, k, m, rows), xsT[:, s, k, :],
                                                   start=(k == 0), stop=(k == 1))
                        mm.then_inc(sem(name + "_hid"), 1)

                def output(b, s):
                    pe.wait_ge(sem(name + f"_wout{s}"), ((b - s) * 8 + 16) * n_out)
                    pe.wait_ge(sem(name + "_mul"), b * nu + nu)
                    after(pe, sem(name + "_ycopied"), b - 1)
                    flat = [x for tiles in units for x in tiles]
                    for m, rows in flat:
                        mm = pe.matmul(banks[5 + s][:, 0:D], hid[0:rows, s, m, :], w_out(s, m), start=(m == 0),
                                       stop=(m == len(flat) - 1))
                    mm.then_inc(sem(name + "_out"), 1)

                def step(b, s):
                    if not (isinstance(b, int) and b + 2 >= nblk):
                        row_nodes(b + 2, s)
                    if not (isinstance(b, int) and b + 1 >= nblk):
                        turn_rows(b + 1, 1 - s)
                    hidden(b, s)
                    if not (isinstance(b, int) and b == 0):
                        output(b - 1, 1 - s)

                all_free()
                row_nodes(0, 0)
                row_nodes(1, 1)
                turn_rows(0, 0)
                block_steps(pe, nblk, step)
                output(nblk - 1, (nblk - 1) % 2)

            def ranks(name, ne):
                pe.wait_ge(sem(name + "_picked"), 1)
                for what, m in (("rank", before), ("total", ones16)):
                    bank, done = group((name, what))
                    pe.matmul(bank[0:P, 0:T * NE0], m[:, :], pick16[:, :, :].rearrange("p t e -> p (t e)"),
                              start=True, stop=True).then_inc(done, 1)

            pe.wait_ge(sem("xn1"), T)
            to_fm("xnT1", xn)
            read_out(pe, "xnT1")
            linear_tm("gate0", fa, lambda k: W("gate0", k), NE0)
            ranks("e0", NE0)
            experts("e0", NBLK0, UNITS0,
                    lambda s, q, k, m, rows: exw[:, s, (q * 2 + k) * HID0 + m * HT0:(q * 2 + k) * HID0 + m * HT0 + rows],
                    lambda s, m: exo[:, s, m * D:(m + 1) * D], 1)

            pe.wait_ge(sem("xn2"), T)
            to_fm("xnT2", xn)
            read_out(pe, "xnT2")
            pe.wait_ge(sem("w1_in"), 16)
            linear_fm("gq", fa, "gq", K2)
            linear_fm("gk", fa, "gk", K2)
            linear_tm("gvs", fa, lambda k: W("gvs", k), 2 * D)
            read_out(pe, "gq")
            read_out(pe, "gk")
            read_out(pe, "gvs")

            def l1_scores(i, m, h):
                k = h // 2
                for c, (off, w, _) in enumerate(CHUNKS):
                    bank, done = group(("l1", "s", i, c))
                    pe.matmul(bank[0:P, 0:w], fc[:, k, m * P:(m + 1) * P], fq[:, k, h % 2, off:off + w],
                              start=True, stop=True).then_inc(done, 1)

            pe.wait_ge(sem("fq_zeros"), 2)
            attend("l1", l1_scores, lambda t, h: xlr[:, t, h * HD:h * HD + VW], all_tiles)

            pe.wait_ge(sem("cmix"), 1)
            for k in range(K2):
                bank, done = group(("ckv", k))
                for t in range(T):
                    mm = pe.matmul(bank[:, 0:128], td[:, t, k * 128:(k + 1) * 128], tc[:, t, k * 128:(k + 1) * 128],
                                   start=(t == 0), stop=(t == T - 1))
                mm.then_inc(done, 1)
            read_out(pe, "ckv")
            for t in range(T):
                bank, done = group(("cout", t))
                for k in range(K2):
                    mm = pe.matmul(bank[0:P, k * 128:(k + 1) * 128], fa[:, k, t * P:(t + 1) * P], ckv[:, k, :],
                                   start=True, stop=True)
                mm.then_inc(done, 1)

            pe.wait_ge(sem("ah"), 1)
            to_fm("ahT", ta)
            read_out(pe, "ahT")
            for name in ("aq", "aqr", "ak", "akr"):
                linear_fm(name, fa, name, K2)
            linear_tm("av", fa, lambda k: W("av", k), 128)
            pe.wait_ge(sem("roped"), 12)
            read_out(pe, "av")

            def l2_scores(i, m, h):
                g = h // 2
                for c, off, w, _ in chunks_upto(m + 1):
                    bank, done = group(("l2", "s", i, c))
                    pe.matmul(bank[0:P, 0:w], fq[:, g, h % 2, m * P:(m + 1) * P], fc[:, g, off:off + w],
                              start=True, stop=True).then_inc(done, 1)

            attend("l2", l2_scores, lambda t, h: td[:, t, (h // 2) * HD:(h // 2) * HD + VW], causal_tiles)
            read_out(pe, "l2", "agg")
            to_fm("yT", te)
            read_out(pe, "yT")
            linear_tm("ao", fa, lambda k: W("ao", k), D)

            pe.wait_ge(sem("flat"), 1)
            to_fm("flatT", ta)
            read_out(pe, "flatT")
            linear_tm("gate1", fa, lambda k: W("gate1", k), NE1)
            ranks("e1", NE1)
            experts("e1", NBLK1, UNITS1,
                    lambda s, q, k, m, rows: exw[:, s, (q * 2 + k) * HID1 + m * HT1:(q * 2 + k) * HID1 + m * HT1 + rows],
                    lambda s, m: exo_r[:, s, :] if m == 5 else exo[0:HT1, s, m * D:(m + 1) * D], 2)

        @block.vector
        def _(dve):
            own = Chain(dve, sem("dve_own"))
            v = nc.vector

            def inverse_root(dst, src, times, plus):
                n = dst.shape[1]
                val, bits, sq = root[:, 0, 0:n], root[:, 1, 0:n], root[:, 2, 0:n]
                own.link(v.tensor_scalar(val, src, times, plus, ALU.mult, ALU.add))
                own.link(v.tensor_scalar(bits.bitcast(I32), val.bitcast(I32), 1, None, ALU.logical_shift_right))
                own.link(v.tensor_scalar(dst.bitcast(I32), bits.bitcast(I32), -1.0, float(0x5F3759DF), ALU.mult,
                                         ALU.add))
                for _ in range(3):
                    own.link(v.tensor_tensor(sq, dst, dst, ALU.mult))
                    own.link(v.scalar_tensor_tensor(sq, sq, -0.5, val, ALU.mult, ALU.mult))
                    own.link(v.scalar_tensor_tensor(dst, sq, 1.5, dst, ALU.add, ALU.mult))

            def layernorm(src, dst, eps, done, stats_of=range(T)):
                for t in stats_of:
                    own.note(v.bn_stats(stats[:, t, :], src[:, t, :]))
                own.fence()
                for t in range(T):
                    own.note(v.bn_aggr(mv[:, t, :], stats[:, t, :]))
                own.fence()
                inverse_root(rstd[:, :], mv[:, :, 1], 1.0, eps)
                for t in range(T):
                    v.tensor_scalar(dst[:, t, :], src[:, t, :], mv[:, t, 0:1], rstd[:, t:t + 1], ALU.subtract,
                                    ALU.mult).then_inc(done[0], 1)
                dve.wait_ge(done[0], done[1])

            def affine(dst, layer, g, b, done):
                own.link(v.tensor_tensor(dst[:, :, :], dst[:, :, :], V(layer, g), ALU.mult))
                v.tensor_tensor(dst[:, :, :], dst[:, :, :], V(layer, b), ALU.add).then_inc(done, 1)

            def rmsnorm(src, dst, weight, junk, done):
                for t in range(T):
                    own.note(v.tensor_tensor_reduce(junk[:, t, :], src[:, t, :], src[:, t, :], 1.0 / D, 0.0, ALU.mult,
                                                    ALU.add, rsum[:, t:t + 1]))
                own.fence()
                inverse_root(rstd[:, :], rsum[:, :], 1.0, 1e-6)
                for t in range(T):
                    ins = v.scalar_tensor_tensor(dst[:, t, :], src[:, t, :], rstd[:, t:t + 1], Vt(1, weight), ALU.mult,
                                                 ALU.mult)
                ins.then_inc(done, 1)

            def from_fm(name, dst):
                for c, (off, w, _) in enumerate(CHUNKS):
                    bank, freed = got(dve, (name, 1, c))
                    v.tensor_copy(dst[:, 1, off:off + w], bank[:, 0:w]).then_inc(freed, 1)

            def copy_indices(g, b):
                v.tensor_copy(idx_ring[:, b % 4, :, :], edge_ids[:, :, bass.ds(g * G, G)]).then_inc(sem("indices"), 1)

            def score_group(g, b, ch):
                s = b % 2
                dve.wait_ge(sem(f"gathered{s}"), (g - s) * (G * 16) + 2 * G * 16)
                zl, zr = gat[:, s, 0, :], gat[:, s, 1, :]
                ch.link(v.tensor_tensor(zl, zl, zr, ALU.add))
                finish_scores(g, b, ch, zr)

            def finish_scores(g, b, ch, zr):
                s = b % 2
                static = isinstance(g, int)
                zl = gat[:, s, 0, :]
                ch.link(v.scalar_tensor_tensor(zr, zl, 0.2, zl, ALU.mult, ALU.max))
                ch.link(v.tensor_tensor(zl.rearrange("p (g c) -> p g c", g=G), zr.rearrange("p (g c) -> p g c", g=G),
                                        Vt(0, "att").unsqueeze(1).to_broadcast([P, G, D]), ALU.mult))
                if not (static and g < 2):
                    for w in range(1 if static and g - 1 <= SINGLE else 2):
                        after(dve, sem(f"scattered{w}"), scores_written(w, g - 1, 0, b - 1))
                v.tensor_reduce(sc_ring[:, s, :, :].rearrange("p g h -> p (g h)"),
                                zl.rearrange("p (a c) -> p a c", c=HD), AX.X, ALU.add).then_inc(sem("scored"), 1)
                if not (static and g + 2 >= NG):
                    copy_indices(g + 2, b + 2)

            def onehots(g, b):
                s = b % 2
                after(dve, sem("onehot_used"), g - 1)
                onehot_columns(g, s, range(G)).then_inc(sem("onehot"), 1)

            def onehot_columns(g, s, columns):
                for j in columns:
                    for w, a in enumerate((srcf, dstf)):
                        ins = v.tensor_scalar(oh[:, s, w, j, :], iota_n[:, :], a[:, bass.ds(g * G + j, 1)], None,
                                              ALU.is_equal)
                return ins

            def onehots_by_node(g, b, tiles):
                s = b % 2
                if 0 in tiles:
                    dve.wait_ge(sem(f"dst_row{s}"), g * 8 + (16 - 8 * (LATE + s)))
                    after(dve, sem("xr_made"), g * len(ROUNDS) - len(ROUNDS) * (LATE + 1))
                for t in tiles:
                    ins = v.tensor_scalar(ohT[:, s, t, :], dst_row[:, s, :], node_f[:, t:t + 1], None, ALU.is_equal)
                if T - 1 in tiles:
                    ins.then_inc(sem("onehotT"), 1)

            def late_group(g, b, ch):
                s = b % 2
                more = not (isinstance(g, int) and g + 1 >= NG)
                rows = G + G - XR_COLS
                dve.wait_ge(sem(f"late{s}"), g * (8 * rows) + (16 * rows - 8 * rows * (LATE + s)))
                for r, (first, n) in enumerate(ROUNDS):
                    dve.wait_ge(sem("xr_made"), g * len(ROUNDS) + (r + 1 - LATE * len(ROUNDS)))
                    zl = gat[:, s, 0, first * D:(first + n) * D]
                    v.tensor_tensor(zl, zl, banks[7][0:P, 0:n * D], ALU.add).then_inc(sem("xr_read"), 1)
                    if r == 0:
                        last = gat[:, s, 0, XR_COLS * D:]
                        ch.note(v.tensor_tensor(last, last, gat_xr[:, s, :], ALU.add))
                        dve.wait_ge(sem("onehot_used"), g - BEHIND)
                    ins = onehot_columns(g + (1 - BEHIND), 1 - s, ROUND_COUNTS[r])
                    if r == len(ROUNDS) - 1:
                        ins.then_inc(sem("onehot"), 1)
                    if more:
                        onehots_by_node(g + 1, b + 1, NODE_TILES[r])
                dve.wait_ge(sem("xr_read"), g * len(ROUNDS) + (1 - LATE) * len(ROUNDS))
                ch.fence()
                finish_scores(g, b, ch, tc[:, :, :].rearrange("p t d -> p (t d)"))

            early = Chain(dve, sem("edge_own"))

            def score_early(*groups):
                for g in groups:
                    score_group(g, g, early)

            v.memset(cnt[:, :, :], LOWEST).then_inc(sem("blank"), 1)
            v.memset(zero16[:, :], 0.0).then_inc(sem("zero16"), 1)
            own.note(v.memset(mixw[:, :, :], 0.0))
            v.memset(mixk[:, :, :], 0.0).then_inc(sem("mixw0"), 1)
            dve.wait_ge(sem("x_in"), 16)
            layernorm(x, xn, 1e-5, (sem("xn0"), T))
            dve.wait_ge(sem("edges_in"), 32)
            own.note(v.tensor_copy(srcf[:, :], srci))
            own.note(v.tensor_copy(dstf[:, :], dsti))
            own.fence()
            own.link(v.scalar_tensor_tensor(cellf[:, :], dstf[:, :], float(N), srcf[:, :], ALU.mult, ALU.add))
            own.link(v.tensor_copy(celli, cellf))

            copy_indices(0, 0)
            copy_indices(1, 1)
            from_fm("xnT0", fa)
            for t in range(T):
                bank, freed = got(dve, ("lr", t))
                v.tensor_copy(xlr[:, t, :], bank[0:P, :]).then_inc(freed, 1)
            layernorm(xn, ta, 1e-5, (sem("ln"), T))
            dve.wait_ge(sem("vec0_in"), 16)
            affine(ta, 0, "ln1_g", "ln1_b", sem("mixh"))
            own.note(v.tensor_tensor(tb[:, :, :], xn[:, :, :], V(0, "bo"), ALU.add))
            from_fm("mixhT", fb_)
            dve.wait_ge(sem("fb_in"), 16)
            for c, (off, w, _) in enumerate(CHUNKS):
                bank, freed = got(dve, ("xm", 1, c))
                v.tensor_scalar(fc[:, 1, off:off + w], bank[:, 0:w], fbias[:, FB_BX + 1:FB_BX + 2], None, ALU.add)\
                    .then_inc(freed, 1)
            for t in range(T):
                bank, freed = got(dve, ("qv", t))
                qv = bank[0:P, 0:288].rearrange("p (h c) -> p h c", h=NBLK)
                own.note(v.tensor_copy(te[:, t, 0:32].rearrange("p (h r) -> p h r", h=NBLK), qv[:, :, 0:KR]))
                v.tensor_copy(td[:, t, :].rearrange("p (h c) -> p h c", h=NBLK), qv[:, :, KR:KR + DH])\
                    .then_inc(freed, 1)
            score_early(0)
            for c, (off, w, _) in enumerate(CHUNKS):
                bank, freed = got(dve, ("kT", c))
                v.tensor_copy(fd[0:32, 0, off:off + w], bank[0:32, 0:w]).then_inc(freed, 1)
            read_out(dve, "kT")
            own.link(v.tensor_reduce(kstat[:, 0:1], fd[0:32, 0, :], AX.X, ALU.max))
            v.tensor_scalar(kstat[:, 1:2], kstat[:, 0:1], -1.0, None, ALU.mult).then_inc(sem("kmax"), 1)
            own.fence()
            q4 = te[:, :, 0:32].rearrange("p t (h r) -> p t h r", h=NBLK)
            qst = hstat[:, 0, :].rearrange("p (t h) -> p t h", t=T)
            qsu = hstat[:, 1, :].rearrange("p (t h) -> p t h", t=T)

            def spread(a):
                return a.unsqueeze(3).to_broadcast([P, T, NBLK, KR])

            own.link(v.tensor_reduce(qst, q4, AX.X, ALU.max))
            v.tensor_tensor(q4, q4, spread(qst), ALU.subtract).then_inc(sem("qshift"), 1)
            dve.wait_ge(sem("kexp"), 1)
            own.link(v.reciprocal(kstat[:, 0:1], kstat[:, 2:3]))
            v.tensor_scalar(fd[0:32, 0, :], fd[0:32, 0, :], kstat[:, 0:1], None, ALU.mult).then_inc(sem("ksoft"), 1)
            dve.wait_ge(sem("qexp"), 1)
            own.link(v.tensor_reduce(qst, q4, AX.X, ALU.add))
            own.link(v.reciprocal(qsu, qst))
            v.tensor_tensor(q4, q4, spread(qsu), ALU.mult).then_inc(sem("qsoft"), 1)
            score_early(1)
            bank, freed = got(dve, "kN")
            v.tensor_copy(te[:, :, 32:64], bank[0:P, 0:160].rearrange("p (t r) -> p t r", t=T))\
                .then_inc(freed, 1)
            for c, (off, w, _) in enumerate(CHUNKS):
                bank, freed = got(dve, ("qT", c))
                v.tensor_copy(fd[0:32, 1, off:off + w], bank[0:32, 0:w]).then_inc(freed, 1)
            bank, freed = got(dve, "kv")
            dve.wait_ge(sem("blocks"), 1)
            v.tensor_tensor(kvbd[:, :], bank[0:32, 0:D], block4[:, :], ALU.mult)\
                .then_inc(freed, 1)
            for c, (off, w, _) in enumerate(CHUNKS):
                bank, freed = got(dve, ("qkv", 1, c))
                v.tensor_copy(fb_[:, 1, off:off + w], bank[:, 0:w]).then_inc(freed, 1)
            for t in range(T):
                bank, freed = got(dve, ("attn", t))
                v.tensor_tensor(tb[:, t, :], bank[0:P, 0:D], tb[:, t, :], ALU.add).then_inc(freed, 1)
            read_out(dve, "attn")
            score_early(2)
            layernorm(tb, ta, 1e-5, (sem("ln"), 2 * T))
            affine(ta, 0, "ln2_g", "ln2_b", sem("h2"))
            own.link(v.tensor_tensor(tb[:, :, :], tb[:, :, :], V(0, "b2"), ALU.add))
            from_fm("h2T", fb_)
            score_early(3, 4)
            for t in range(T):
                bank, freed = got(dve, ("m2", t))
                v.tensor_tensor(tb[:, t, :], bank[0:P, 0:D], tb[:, t, :], ALU.add).then_inc(freed, 1)
                if t == 1:
                    score_early(5)
            read_out(dve, "m2")
            dve.wait_ge(sem("iotas"), 5)
            own.link(v.tensor_tensor(x[:, :, :], x[:, :, :], tb[:, :, :], ALU.add))
            o = 0
            for g, n in zip(range(6, LATE), ONEHOTS):
                for _ in range(n):
                    onehots(o, o % 2)
                    o += 1
                if g < LATE - 1:
                    score_early(g)

            xr = xlr[:, :, D:2 * D]
            onehots_by_node(LATE, 0, range(T))
            own.link(v.tensor_copy(xr_hi, xr))
            onehots(o, o % 2)
            score_early(LATE - 1)
            v.tensor_tensor(xr_lo, xr, xr_hi.bitcast(F32), ALU.subtract).then_inc(sem("xr_parts"), 1)
            late0 = LATE * EDGE_LINKS
            per = EDGE_LINKS
            ch = Chain(dve, sem("edge_own"), late0)
            for b in range(4):
                late_group(LATE + b, b, ch)
            with dve.Fori(LATE // 4 + 1, NG // 4 - 1) as i:
                ch = Chain(dve, sem("edge_own"), i * (4 * per) + (late0 - LATE * per))
                for b in range(4):
                    late_group(i * 4 + b, b, ch)
            ch = Chain(dve, sem("edge_own"), late0 + (NG - 4 - LATE) * per)
            for b in range(4):
                late_group(NG - 4 + b, b, ch)
            for g in range(NG - BEHIND + 1, NG):
                onehots(g, g % 2)

            def merge_scores(m):
                dve.wait_ge(sem(f"sdense{m % 2}"), 32 * (m // 2 + 1))
                both = sdense[:, m % 2, :, :, :].rearrange("p w n h -> p w (n h)")
                own.link(v.tensor_tensor(both[:, 0, :], both[:, 0, :], both[:, 1, :], ALU.max))

            merge_scores(0)
            REST = N - 512
            dve.wait_ge(sem("counted"), 1)
            for w in range(2):
                dve.wait_ge(sem(f"blank{w}"), T * 16)
            for m in range(T):
                own.note(v.tensor_copy(cnt[:, m, 0:512], banks[m][0:P, :]))
            own.note(v.tensor_copy(cnt[:, 0:4, 512:N], banks[5][0:P, 0:4 * REST].rearrange("p (m n) -> p m n", m=4)))
            v.tensor_copy(cnt[:, 4, 512:N], banks[6][0:P, 0:REST]).then_inc(sem("counts_out"), 1)
            own.fence()
            dve.wait_ge(sem("counts_out"), 1)
            own.link(v.tensor_scalar(nmask[:, :, :], cnt[:, :, :], 0.0, -BIG, ALU.is_equal, ALU.mult))

            def attend(name, take_scores, tiles_of, weigh, guard, dst, beside=None):
                def maxima(i):
                    m, h = steps[i]
                    if not weigh and i >= 3:
                        dve.wait_ge(sem(name + "_prob"), i - 2)
                    take_scores(i, m, h)
                    v.tensor_scalar(rneg[:, i:i + 1], rmx[:, i:i + 1], -1.0, None, ALU.mult)\
                        .then_inc(sem(name + "_max"), 1)

                def weights(i):
                    if not weigh:
                        return
                    m, h = steps[i]
                    dve.wait_ge(sem(name + "_exp"), i + 1)
                    if i >= 3:
                        read_out(dve, name, "pT", i - 3)
                    v.tensor_tensor_reduce(prob[:, i % 3, :], expd[:, i % 3, :], cnt[:, m, :], 1.0, 0.0, ALU.mult,
                                           ALU.add, rden[:, i:i + 1]).then_inc(sem(name + "_prob"), 1)

                def normalize(m):
                    cols = slice(m * H, (m + 1) * H)
                    dve.wait_ge(sem(name + "_prob"), (m + 1) * H)
                    own.link(guard(rrec[:, cols], rden[:, cols]))
                    own.link(v.reciprocal(rrec[:, cols], rrec[:, cols]))
                    dve.wait_ge(sem(name + "_sum"), (m + 1) * H)
                    b = 6 + m % 2
                    v.tensor_tensor(dst[:, m, :].rearrange("p (h c) -> p h c", h=H),
                                    banks[b][0:P, :].rearrange("p (h c) -> p h c", h=H)[:, :, 0:HD],
                                    rrec[:, cols].unsqueeze(2).to_broadcast([P, H, HD]), ALU.mult)\
                        .then_inc(free[b], 1)
                    if beside is not None:
                        dve.wait_ge(free[b], ticket[(name, "agg", m)][2])

                n = len(steps)
                for i in range(n + 2):
                    if i < n:
                        maxima(i)
                    if i >= 2:
                        weights(i - 2)
                    if i >= 7 and (i - 7) % H == 0:
                        normalize((i - 7) // H)
                    if beside is not None:
                        beside(i)
                normalize(T - 1)
                read_out(dve, name, "agg")

            def l0_take(i, m, h):
                if h == 0 and m > 0:
                    merge_scores(m)
                v.tensor_tensor_reduce(masked[:, i % 3, :], sdense[:, m % 2, 0, :, h], nmask[:, m, :], 1.0, LOWEST,
                                       ALU.add, ALU.max, rmx[:, i:i + 1]).then_inc(sem("l0_taken"), 1)
                dve.wait_ge(sem("l0_taken"), i + 1)

            def from_banks(name, mask, scale, tiles_of):
                def take(i, m, h):
                    parts = chunks_upto(tiles_of(m))
                    for c, off, w, _ in parts:
                        bank, freed = got(dve, (name, "s", i, c))
                        v.tensor_tensor_reduce(
                            masked[:, i % 3, off:off + w], bank[0:P, 0:w], mask(m, off, w), scale, -3e38,
                            ALU.add, ALU.max, (rmx if c == 0 else rmx_a)[:, i:i + 1]).then_inc(freed, 1)
                    read_out(dve, name, "s", i)
                    if len(parts) == 2:
                        own.link(v.tensor_tensor(rmx[:, i:i + 1], rmx[:, i:i + 1], rmx_a[:, i:i + 1], ALU.max))
                return take

            attend("l0", l0_take, all_tiles, True,
                   lambda o, a: v.tensor_scalar(o, a, 1e-16, None, ALU.add), te)
            own.link(v.tensor_tensor(te[:, :, :], te[:, :, :], V(0, "g_bias"), ALU.add))
            v.tensor_scalar(tc[:, :, :], te[:, :, :], 0.0, None, ALU.min).then_inc(sem("elu_min"), 1)
            dve.wait_ge(sem("elu_exp"), 1)
            own.link(v.scalar_tensor_tensor(te[:, :, :], te[:, :, :], 0.0, tc[:, :, :], ALU.max, ALU.add))
            own.link(v.scalar_tensor_tensor(te[:, :, :], te[:, :, :], -1.0, xn[:, :, :], ALU.add, ALU.add))
            layernorm(te, ta, 1e-5, (sem("ln"), 3 * T))
            affine(ta, 0, "g_gamma", "g_beta", sem("g0"))
            dve.wait_ge(sem("g0"), 1)
            own.link(v.tensor_tensor(x[:, :, :], x[:, :, :], ta[:, :, :], ALU.add))

            def route(name, gate_name, ne, nblk, bias, eps):
                for t in range(T):
                    bank, freed = got(dve, (gate_name, t))
                    if bias is None:
                        ins = v.tensor_copy(lg[:, t, 0:ne], bank[0:P, 0:ne])
                    else:
                        ins = v.tensor_tensor(lg[:, t, 0:ne], bank[0:P, 0:ne], bias, ALU.add)
                    ins.then_inc(freed, 1)
                read_out(dve, gate_name)
                wide = lambda a: a[:, :].unsqueeze(2).to_broadcast([P, T, ne])
                own.link(v.tensor_reduce(rmax[:, :], lg[:, :, 0:ne], AX.X, ALU.max))
                v.tensor_tensor(lg[:, :, 0:ne], lg[:, :, 0:ne], wide(rmax), ALU.subtract)\
                    .then_inc(sem(gate_name + "_sh"), 1)
                dve.wait_ge(sem(gate_name + "_exp"), 1)
                own.link(v.tensor_reduce(rsum[:, :], pr[:, :, 0:ne], AX.X, ALU.add))
                own.link(v.reciprocal(rinv[:, :], rsum[:, :]))
                own.link(v.tensor_tensor(pr[:, :, 0:ne], pr[:, :, 0:ne], wide(rinv), ALU.mult))
                for t in range(T):
                    own.note(v.max(top8[:, t, :], pr[:, t, 0:ne]))
                own.fence()
                for t in range(T):
                    own.note(v.max_index(topi[:, t, :], top8[:, t, :], pr[:, t, 0:ne]))
                own.fence()
                own.link(v.tensor_copy(topf[:, :, :], topi[:, :, :]))
                for t in range(T):
                    for j in range(2):
                        own.note(v.tensor_scalar(pick[:, j, t, :], iota_e[:, :], topf[:, t, j:j + 1], None,
                                                 ALU.is_equal))
                own.fence()
                v.tensor_tensor(pick16[:, :, :], pick[:, 0, :, :], pick[:, 1, :, :], ALU.add)\
                    .then_inc(sem(name + "_picked"), 1)
                own.link(v.tensor_tensor(rsum[:, :], top8[:, :, 0], top8[:, :, 1], ALU.add))
                own.link(v.tensor_scalar(rsum[:, :], rsum[:, :], eps, None, ALU.add))
                own.link(v.reciprocal(rinv[:, :], rsum[:, :]))
                own.link(v.tensor_tensor(wtop[:, :, :], top8[:, :, 0:2],
                                         rinv[:, :].unsqueeze(2).to_broadcast([P, T, 2]), ALU.mult))
                for what, dst in (("rank", rank), ("total", total)):
                    bank, freed = got(dve, (name, what))
                    v.tensor_copy(dst[:, :, :].rearrange("p t e -> p (t e)"), bank[0:P, 0:T * NE0])\
                        .then_inc(freed, 1)
                read_out(dve, name, "rank")
                read_out(dve, name, "total")
                for t in range(1, T):
                    own.note(v.tensor_tensor(rank[:, t, :], rank[:, t, :], total[:, t - 1, :], ALU.add))
                    own.link(v.tensor_tensor(total[:, t, :], total[:, t, :], total[:, t - 1, :], ALU.add))
                own.link(v.tensor_scalar(nblocks_i[:, :], total[:, T - 1, :], float(SLOTS - 1), None, ALU.add))
                own.link(v.tensor_scalar(nblocks_i[:, :], nblocks_i[:, :], SLOTS.bit_length() - 1, None,
                                         ALU.logical_shift_right))
                own.link(v.tensor_copy(nblocks[:, :], nblocks_i[:, :]))
                own.link(v.tensor_tensor(eprod[:, :, :], before_e[:, :, :],
                                         nblocks[:, :].unsqueeze(1).to_broadcast([P, NE0, NE0]), ALU.mult))
                own.link(v.tensor_reduce(first[:, :], eprod[:, :, :], AX.X, ALU.add))
                own.link(v.tensor_tensor(upto[:, :], first[:, :], nblocks[:, :], ALU.add))
                own.link(v.tensor_tensor(bcmp[:, 0:nblk, 0:ne], iota_b[:, 0:nblk].unsqueeze(2).to_broadcast([P, nblk, ne]),
                                         upto[:, 0:ne].unsqueeze(1).to_broadcast([P, nblk, ne]), ALU.is_ge))
                own.link(v.tensor_reduce(bown[:, 0:nblk], bcmp[:, 0:nblk, 0:ne], AX.X, ALU.add))
                v.tensor_scalar(bown_i[:, 0:nblk], bown[:, 0:nblk], float(ne - 1), None, ALU.min)\
                    .then_inc(sem(name + "_owners"), 1)
                own.link(v.tensor_scalar(first[:, :], first[:, :], float(SLOTS), None, ALU.mult))
                own.link(v.tensor_tensor(rank[:, :, :], rank[:, :, :],
                                         first[:, :].unsqueeze(1).to_broadcast([P, T, NE0]), ALU.add))
                for j in range(2):
                    own.link(v.tensor_tensor(pick[:, j, :, :], pick[:, j, :, :], rank[:, :, :], ALU.mult))
                    own.link(v.tensor_reduce(slotf[:, j, :], pick[:, j, :, :], AX.X, ALU.add))
                own.note(v.tensor_copy(slot_rel[:, :], slotf[:, :, :].rearrange("p j t -> p (j t)")))
                v.tensor_copy(sloti[:, :, :], slotf[:, :, :]).then_inc(sem(name + "_slots"), 1)
                own.fence()

            def experts(name, nblk, units, then):
                nu = len(units)

                def select(b, s):
                    after(dve, sem(name + "_nodes"), b - 1)
                    after(dve, sem(name + "_shift"), b)
                    v.tensor_tensor(sel[:, s, :, :], iota_s[:, :].unsqueeze(1).to_broadcast([P, 2 * T, SLOTS]),
                                    slot_rel[:, :].unsqueeze(2).to_broadcast([P, 2 * T, SLOTS]), ALU.is_equal)\
                        .then_inc(sem(name + "_sel"), 1)
                    dve.wait_ge(sem(name + "_sel"), b + 1)
                    v.tensor_scalar(slot_rel[:, :], slot_rel[:, :], float(SLOTS), None, ALU.subtract)\
                        .then_inc(sem(name + "_shift"), 1)

                def node_ids(b, s):
                    dve.wait_ge(sem(name + "_nodes"), b + 1)
                    after(dve, sem(name + "_turned"), b - 1)
                    v.tensor_copy(ids[:, s, :], banks[7][:, 0:1]).then_inc(sem(name + "_ids"), 1)

                def step(b, s):
                    if not (isinstance(b, int) and b + 2 >= nblk):
                        node_ids(b + 2, s)
                    if not (isinstance(b, int) and b + 3 >= nblk):
                        select(b + 3, 1 - s)
                    after(dve, sem(name + "_out"), b - 1)
                    for j, tiles in enumerate(units):
                        buf = j if nu == 2 else s
                        dve.wait_ge(sem(name + "_silu"), b * nu + (j + 1))
                        for i0, m0, n, rows in runs(tiles):
                            ins = v.tensor_tensor(hid[0:rows, s, m0:m0 + n, :],
                                                  banks[3 + buf][0:rows, i0 * SLOTS:(i0 + n) * SLOTS]
                                                  .rearrange("p (m n) -> p m n", n=SLOTS),
                                                  silu[0:rows, buf, i0:i0 + n, :], ALU.mult)
                        ins.then_inc(sem(name + "_mul"), 1)
                    if not (isinstance(b, int) and b == 0):
                        copy_y(b - 1, 1 - s)

                def copy_y(b, s):
                    dve.wait_ge(sem(name + "_out"), b + 1)
                    if not (isinstance(b, int) and b < 2):
                        dve.wait_ge(sem(f"{name}_stored{s}"), (b - s) * 8)
                    v.tensor_copy(ys[:, s, :], banks[5 + s][:, 0:D]).then_inc(sem(name + "_ycopied"), 1)

                select(0, 0)
                select(1, 1)
                node_ids(0, 0)
                node_ids(1, 1)
                select(2, 0)
                block_steps(dve, nblk, step)
                copy_y(nblk - 1, (nblk - 1) % 2)
                for t in range(T):
                    dve.wait_ge(sem(f"back{t}"), 2 * 16 * (1 + int(name[1])))
                    for j in range(2):
                        v.scalar_tensor_tensor(x[:, t, :], yg[:, j, t, :], wtop[:, t, j:j + 1], x[:, t, :],
                                               ALU.mult, ALU.add).then_inc(sem(name + "_added"), 1)
                        dve.wait_ge(sem(name + "_added"), 2 * t + j + 1)
                    if then is not None:
                        then(t)

            layernorm(x, xn, 1e-5, (sem("xn1"), T))
            from_fm("xnT1", fa)
            route("e0", "gate0", NE0, NBLK0, vec[:, V_GATEB:V_GATEB + NE0], 0.0)
            experts("e0", NBLK0, UNITS0, lambda t: own.note(v.bn_stats(stats[:, t, :], x[:, t, :])))

            layernorm(x, xn, 1e-5, (sem("xn2"), T), stats_of=())
            from_fm("xnT2", fa)
            for c, (off, w, _) in enumerate(CHUNKS):
                bank, freed = got(dve, ("gq", 1, c))
                for rows, to in halves(1, off, w):
                    ins = v.tensor_scalar(to, bank[rows, 0:w], fbias[rows, FB_BQ + 1:FB_BQ + 2], None, ALU.add)
                ins.then_inc(freed, 1)
            for c, (off, w, _) in enumerate(CHUNKS):
                bank, freed = got(dve, ("gk", 1, c))
                v.tensor_scalar(fc[:, 1, off:off + w], bank[:, 0:w], fbias[:, FB_BK + 1:FB_BK + 2], None, ALU.add)\
                    .then_inc(freed, 1)
            dve.wait_ge(sem("vec1_in"), 16)
            for t in range(T):
                bank, freed = got(dve, ("gvs", t))
                v.tensor_tensor(xlr[:, t, :], bank[0:P, :], Vt(1, "bv", 2 * D), ALU.add)\
                    .then_inc(freed, 1)
            heads = lambda a: a[:, :, :].rearrange("p t (h c) -> p (t h) c", h=NBLK)
            hb = lambda r: hstat[:, r, :].unsqueeze(2).to_broadcast([P, T * NBLK, DH])

            def gate_parts(t):
                skip = xlr[:, t, D:2 * D]
                own.link(v.tensor_tensor(ta[:, t, :], skip, te[:, t, :], ALU.subtract))
                for j, (a, w) in enumerate(((skip, "wg_skip"), (te[:, t, :], "wg_rst"), (ta[:, t, :], "wg_diff"))):
                    own.note(v.tensor_tensor_reduce(tb[:, t, :], a, Vt(1, w), 1.0, 0.0, ALU.mult, ALU.add,
                                                    gpart[:, j, t:t + 1]))
                    own.fence()

            def beside_l1(i):
                if i == 0:
                    own.link(v.tensor_reduce(hstat[:, 0, :], heads(xn), AX.X, ALU.add))
                elif i == 1:
                    own.link(v.tensor_scalar(hstat[:, 0, :], hstat[:, 0, :], 1.0 / DH, None, ALU.mult))
                    own.link(v.tensor_tensor(heads(td), heads(xn), hb(0), ALU.subtract))
                elif i == 2:
                    own.link(v.tensor_tensor(tc[:, :, :], td[:, :, :], td[:, :, :], ALU.mult))
                elif i == 3:
                    own.link(v.tensor_reduce(hstat[:, 1, :], heads(tc), AX.X, ALU.add))
                elif i == 4:
                    inverse_root(hstat[:, 2, :], hstat[:, 1, :], 1.0 / (DH - 1), 0.0)
                elif i == 5:
                    own.link(v.scalar_tensor_tensor(hstat[:, 1, :], hstat[:, 1, :], 1.0 / (DH - 1), hstat[:, 2, :],
                                                    ALU.mult, ALU.mult))
                    own.link(v.tensor_scalar(hstat[:, 1, :], hstat[:, 1, :], 1e-5, None, ALU.add))
                    own.link(v.reciprocal(hstat[:, 2, :], hstat[:, 1, :]))
                elif i == 6:
                    own.link(v.tensor_tensor(heads(td), heads(td), hb(2), ALU.mult))
                elif i == 8:
                    own.link(v.tensor_tensor(tc[:, :, :], td[:, :, :], V(1, "vln_w"), ALU.mult))
                elif i == 10:
                    own.link(v.tensor_tensor(tc[:, :, :], tc[:, :, :], V(1, "vln_b"), ALU.add))
                elif i == 12:
                    own.link(v.tensor_tensor(td[:, :, :], td[:, :, :], V(1, "kln_w"), ALU.mult))
                elif i == 14:
                    v.tensor_tensor(td[:, :, :], td[:, :, :], V(1, "kln_b"), ALU.add).then_inc(sem("cmix"), 1)
                elif i == 16:
                    own.link(v.tensor_tensor(x[:, :, :], x[:, :, :], xn[:, :, :], ALU.add))
                elif i >= 9 and (i - 9) % H == 0:
                    gate_parts((i - 9) // H)

            attend("l1", from_banks("l1", lambda m, off, w: nmask[:, m, off:off + w], HD ** -0.5, all_tiles),
                   all_tiles, True, lambda o, a: v.tensor_scalar(o, a, 1e-30, None, ALU.max), te, beside_l1)
            gate_parts(T - 1)
            own.link(v.tensor_tensor(gate[:, :], gpart[:, 0, :], gpart[:, 1, :], ALU.add))
            v.tensor_tensor(gate[:, :], gate[:, :], gpart[:, 2, :], ALU.add).then_inc(sem("glogit"), 1)
            for k in range(K2):
                bank, freed = got(dve, ("ckv", k))
                v.scalar_tensor_tensor(ckv[:, k, :], bank[:, 0:128], 1.0 / N, block32[:, :], ALU.mult, ALU.mult)\
                    .then_inc(freed, 1)
            dve.wait_ge(sem("gated"), 1)
            for t in range(T):
                own.note(v.scalar_tensor_tensor(te[:, t, :], ta[:, t, :], gate[:, t:t + 1], te[:, t, :], ALU.mult,
                                                ALU.add))
            own.fence()
            layernorm(te, ta, 1e-5, (sem("ln"), 4 * T))
            affine(ta, 1, "ln_w", "ln_b", sem("g1"))
            for t in range(T):
                bank, freed = got(dve, ("cout", t))
                v.tensor_tensor(x[:, t, :], bank[0:P, 0:D], x[:, t, :], ALU.add).then_inc(freed, 1)
            dve.wait_ge(sem("g1"), 1)
            own.link(v.tensor_scalar(te[:, :, :], ta[:, :, :], 0.0, vec[:, V_PRELU:V_PRELU + 1], ALU.min, ALU.mult))
            own.link(v.scalar_tensor_tensor(ta[:, :, :], ta[:, :, :], 0.0, te[:, :, :], ALU.max, ALU.add))
            read_out(dve, "cout")
            own.link(v.tensor_tensor(x[:, :, :], x[:, :, :], ta[:, :, :], ALU.add))

            layernorm(x, xn, 1e-5, (sem("xn3"), T))
            rmsnorm(xn, ta, "rms1", tb, sem("ah"))
            from_fm("ahT", fa)
            dve.wait_ge(sem("rope_in"), 16)
            for name, f in (("aq", fb_), ("ak", fc)):
                for m in range(K2):
                    for c, (off, w, _) in enumerate(CHUNKS):
                        bank, freed = got(dve, (name, m, c))
                        v.tensor_tensor(f[:, m, off:off + w], bank[:, 0:w], rope[:, 0, off:off + w],
                                        ALU.mult).then_inc(freed, 1)
                read_out(dve, name)
                for m in range(K2):
                    for c, (off, w, _) in enumerate(CHUNKS):
                        bank, freed = got(dve, (name + "r", m, c))
                        v.tensor_tensor(fd[:, m, off:off + w], bank[:, 0:w], rope[:, 1, off:off + w],
                                        ALU.mult).then_inc(freed, 1)
                        read_out(dve, name + "r", m, c)
                        for rows, to in (halves(m, off, w) if name == "aq" else [(slice(0, 128), f[:, m, off:off + w])]):
                            v.tensor_tensor(to, f[rows, m, off:off + w], fd[rows, m, off:off + w], ALU.add)\
                                .then_inc(sem("roped"), 1)
            for t in range(T):
                bank, freed = got(dve, ("av", t))
                v.tensor_copy(td[:, t, 0:128], bank[0:P, 0:128]).then_inc(freed, 1)
            attend("l2", from_banks("l2", lambda m, off, w: lower[:, (T - 1 - m) * P + off:(T - 1 - m) * P + off + w],
                                    HD ** -0.5, causal_tiles),
                   causal_tiles, False, lambda o, a: v.tensor_copy(o, a), te)
            from_fm("yT", fa)
            for t in range(T):
                bank, freed = got(dve, ("ao", t))
                v.tensor_tensor(tb[:, t, :], bank[0:P, 0:D], xn[:, t, :], ALU.add).then_inc(freed, 1)
            read_out(dve, "ao")
            rmsnorm(tb, ta, "rms2", td, sem("flat"))
            own.link(v.tensor_tensor(x[:, :, :], x[:, :, :], tb[:, :, :], ALU.add))
            from_fm("flatT", fa)
            route("e1", "gate1", NE1, NBLK1, None, 1e-9)
            experts("e1", NBLK1, UNITS1, None)

        @block.scalar
        def _(act):
            a = nc.scalar

            def from_fm(name, dst):
                for c, (off, w, _) in enumerate(CHUNKS):
                    bank, freed = got(act, (name, 0, c))
                    a.activation(dst[:, 0, off:off + w], bank[:, 0:w], ACT.Copy).then_inc(freed, 1)

            def biased(name, f, bias, func=ACT.Identity, tiles=(0,)):
                for m in tiles:
                    for c, (off, w, _) in enumerate(CHUNKS):
                        bank, freed = got(act, (name, m, c))
                        a.activation(f[:, m, off:off + w], bank[:, 0:w], func, bias=fbias[:, bias + m:bias + m + 1])\
                            .then_inc(freed, 1)

            from_fm("xnT0", fa)
            from_fm("mixhT", fb_)
            act.wait_ge(sem("fb_in"), 16)
            biased("xm", fc, FB_BX)
            act.wait_ge(sem("kmax"), 1)
            a.activation(fd[0:32, 0, :], fd[0:32, 0, :], ACT.Exp, bias=kstat[:, 1:2], accum_out=kstat[:, 2:3])\
                .then_inc(sem("kexp"), 1)
            act.wait_ge(sem("qshift"), 1)
            a.activation(te[:, :, 0:32], te[:, :, 0:32], ACT.Exp).then_inc(sem("qexp"), 1)
            for c, (off, w, _) in enumerate(CHUNKS):
                bank, freed = got(act, ("qkv", 0, c))
                a.activation(fb_[:, 0, off:off + w], bank[:, 0:w], ACT.Copy).then_inc(freed, 1)
            from_fm("h2T", fb_)
            biased("m1", mlp, FB_B1, ACT.Gelu, range(FF // 128))

            def attend(name, tiles_of, weigh):
                def exponentials(i):
                    w = tiles_of(steps[i][0]) * P
                    act.wait_ge(sem(name + "_max"), i + 1)
                    if weigh:
                        if i >= 3:
                            act.wait_ge(sem(name + "_prob"), i - 2)
                        a.activation(expd[:, i % 3, 0:w], masked[:, i % 3, 0:w], ACT.Exp, bias=rneg[:, i:i + 1])\
                            .then_inc(sem(name + "_exp"), 1)
                    else:
                        if i >= 3:
                            read_out(act, name, "pT", i - 3)
                        a.activation(prob[:, i % 3, 0:w], masked[:, i % 3, 0:w], ACT.Exp, bias=rneg[:, i:i + 1],
                                     accum_out=rden[:, i:i + 1]).then_inc(sem(name + "_prob"), 1)

                def turned_out(i):
                    if i >= 3:
                        act.wait_ge(sem(name + "_sum"), i - 2)
                    for c, off, w, _ in chunks_upto(tiles_of(steps[i][0])):
                        bank, freed = got(act, (name, "pT", i, c))
                        a.activation(probT[:, i % 3, off:off + w], bank[0:P, 0:w], ACT.Copy).then_inc(freed, 1)

                for i in range(len(steps) + 2):
                    if i < len(steps):
                        exponentials(i)
                    if i >= 2:
                        turned_out(i - 2)

            def shares(name, ne):
                act.wait_ge(sem(name + "_sh"), 1)
                a.activation(pr[:, :, 0:ne], lg[:, :, 0:ne], ACT.Exp).then_inc(sem(name + "_exp"), 1)

            def experts(name, nblk, units):
                nu = len(units)

                def copy_turned(b, s):
                    act.wait_ge(sem(name + "_turned"), b + 1)
                    after(act, sem(name + "_hid"), (b - 1) * nu)
                    a.activation(xsT[:, s, :, :], banks[0][:, 0:2 * SLOTS].rearrange("p (k n) -> p k n", k=K2),
                                 ACT.Copy).then_inc(sem(name + "_xsT"), 1)

                def store(b, s):
                    act.wait_ge(sem(name + "_ycopied"), b + 1)
                    act.dma_start(slot_y[bass.ds(b * SLOTS, SLOTS), :], ys[:, s, :])\
                        .then_inc(sem(f"{name}_stored{s}"), 16)

                def step(b, s):
                    static = isinstance(b, int)
                    if not (static and b + 1 >= nblk):
                        copy_turned(b + 1, 1 - s)
                    for j, tiles in enumerate(units):
                        buf = j if nu == 2 else s
                        act.wait_ge(sem(name + "_hid"), b * nu + (j + 1))
                        after(act, sem(name + "_mul"), b * nu + (j - 1))
                        for i0, m0, n, rows in runs(tiles):
                            ins = a.activation(silu[0:rows, buf, i0:i0 + n, :],
                                               banks[1 + buf][0:rows, i0 * SLOTS:(i0 + n) * SLOTS]
                                               .rearrange("p (m n) -> p m n", n=SLOTS), ACT.Silu)
                        ins.then_inc(sem(name + "_silu"), 1)
                    if not (static and b == 0):
                        store(b - 1, 1 - s)

                copy_turned(0, 0)
                block_steps(act, nblk, step)
                store(nblk - 1, (nblk - 1) % 2)

            attend("l0", all_tiles, True)
            act.wait_ge(sem("elu_min"), 1)
            a.activation(tc[:, :, :], tc[:, :, :], ACT.Exp).then_inc(sem("elu_exp"), 1)
            from_fm("xnT1", fa)
            shares("gate0", NE0)
            experts("e0", NBLK0, UNITS0)
            from_fm("xnT2", fa)
            act.wait_ge(sem("e0_added"), 2 * T)
            for c, (off, w, _) in enumerate(CHUNKS):
                bank, freed = got(act, ("gq", 0, c))
                for rows, to in halves(0, off, w):
                    ins = a.activation(to, bank[rows, 0:w], ACT.Identity, bias=fbias[rows, FB_BQ:FB_BQ + 1])
                ins.then_inc(freed, 1)
            biased("gk", fc, FB_BK)
            attend("l1", all_tiles, True)
            act.wait_ge(sem("glogit"), 1)
            a.activation(gate[:, :], gate[:, :], ACT.Sigmoid, bias=vec[:, V_BGATE:V_BGATE + 1])\
                .then_inc(sem("gated"), 1)
            from_fm("ahT", fa)
            attend("l2", causal_tiles, False)
            from_fm("yT", fa)
            from_fm("flatT", fa)
            shares("gate1", NE1)
            experts("e1", NBLK1, UNITS1)

        @block.gpsimd
        def _(pool):
            p = nc.gpsimd
            own = Chain(pool, sem("pool_own"))
            own.note(p.memset(ident[:, :], 0.0))
            own.note(p.memset(lower[:, :], 0.0))
            own.note(p.memset(block4[:, :], 1.0))
            own.note(p.memset(block32[:, :], 0.0))
            own.fence()
            p.affine_select(out=ident[:, :], in_=ident[:, :], compare_op=ALU.not_equal, fill=1.0, base=0,
                            pattern=[[-1, 128]], channel_multiplier=1).then_inc(sem("ident"), 2)
            p.iota(iota_n[:, :], pattern=[[1, OH]], base=0, channel_multiplier=0,
                   allow_small_or_imprecise_dtypes=True).then_inc(sem("iotas"), 1)
            p.iota(node_f[:, :], pattern=[[P, T]], base=0, channel_multiplier=1,
                   allow_small_or_imprecise_dtypes=True).then_inc(sem("iotas"), 1)
            p.iota(iota_s[:, :], pattern=[[1, SLOTS]], base=0, channel_multiplier=0,
                   allow_small_or_imprecise_dtypes=True).then_inc(sem("iotas"), 1)
            p.iota(node_id[:, :, :], pattern=[[P, T], [0, 2]], base=0, channel_multiplier=1,
                   allow_small_or_imprecise_dtypes=True).then_inc(sem("iotas"), 1)
            p.iota(iota_e[:, :], pattern=[[1, NE0]], base=0, channel_multiplier=0,
                   allow_small_or_imprecise_dtypes=True).then_inc(sem("iotas"), 1)
            own.note(p.affine_select(out=lower[:, :], in_=lower[:, :], compare_op=ALU.is_ge, fill=-BIG,
                                     base=(T - 1) * P, pattern=[[-1, N]], channel_multiplier=1))
            b4 = block4[:, :].rearrange("p (b c) -> p b c", b=NBLK)
            own.link(p.affine_select(out=b4, in_=b4, compare_op=ALU.is_ge, fill=0.0, base=0,
                                     pattern=[[-KR, NBLK], [0, DH]], channel_multiplier=1))
            own.link(p.affine_select(out=b4, in_=b4, compare_op=ALU.is_ge, fill=0.0, base=KR - 1,
                                     pattern=[[KR, NBLK], [0, DH]], channel_multiplier=-1))
            own.note(p.memset(before[:, :], 1.0))
            own.note(p.memset(before_e[:, :, :], 1.0))
            own.fence()
            own.note(p.affine_select(out=before[:, :], in_=before[:, :], compare_op=ALU.is_gt, fill=0.0, base=0,
                                     pattern=[[1, P]], channel_multiplier=-1))
            own.note(p.affine_select(out=before_e[:, :, :], in_=before_e[:, :, :], compare_op=ALU.is_gt, fill=0.0,
                                     base=0, pattern=[[1, NE0], [-1, NE0]], channel_multiplier=0))
            own.note(p.memset(ones16[:, :], 1.0))
            own.note(p.iota(iota_b[:, :], pattern=[[1, NBLK0]], base=0, channel_multiplier=0,
                            allow_small_or_imprecise_dtypes=True))
            own.fence()
            for q in range(4):
                ins = p.memset(block32[32 * q:32 * q + 32, 32 * q:32 * q + 32], 1.0)
            ins.then_inc(sem("blocks"), 1)

            def gather(g, b, j):
                late = not isinstance(g, int) or g >= LATE
                for w, tab in enumerate((xl_tab,) if late and j < XR_COLS else (xl_tab, xr_tab)):
                    p.indirect_dma_start(
                        out=gat_xr[:, b % 2, :] if late and w == 1 else gat[:, b % 2, w, j * D:(j + 1) * D],
                        out_offset=None, in_=tab,
                        in_offset=bass.IndirectOffsetOnAxis(ap=idx_ring[:, b % 4, w, j:j + 1], axis=0))\
                        .then_inc(sem(f"late{b % 2}" if late else f"gathered{b % 2}"), 16)

            def scatter(g, b, j):
                static = isinstance(g, int)
                which = 0 if static and g < SINGLE else (b + j) % 2
                after(pool, sem(f"scattered{which}"), scores_written(which, g, j, b))
                pool.sem_inc(sem("pool_turn"), 1)
                p.indirect_dma_start(
                    out=pair_scores[which], in_=sc_ring[:, b % 2, j, :], in_offset=None,
                    out_offset=bass.IndirectOffsetOnAxis(ap=idx_ring[:, b % 4, 2, j:j + 1], axis=0))\
                    .then_inc(sem(f"scattered{which}"), 16)

            def turn(g, b):
                pool.wait_ge(sem("indices"), g + 1)
                pool.wait_ge(sem("scored"), g - 1)
                pool.sem_inc(sem("pool_turn"), 1)
                for j in range(G):
                    gather(g, b, j)
                    scatter(g - 2, b - 2, j)

            pool.wait_ge(sem("tables"), 32)
            for g in range(2):
                pool.wait_ge(sem("indices"), g + 1)
                for j in range(G):
                    gather(g, g, j)
            pool.wait_ge(sem("blank0"), T * 16)
            for g in range(2, SINGLE + 2):
                turn(g, g)
            pool.wait_ge(sem("blank1"), T * 16)
            for g in range(SINGLE + 2, SINGLE + 6):
                turn(g, g)
            with pool.Fori((SINGLE + 6) // 4, NG // 4) as i:
                for b in range(4):
                    turn(i * 4 + b, b)
            for g in (NG - 2, NG - 1):
                pool.wait_ge(sem("scored"), g + 1)
                for j in range(G):
                    scatter(g, g, j)
            for w in range(2):
                pool.wait_ge(sem(f"scattered{w}"), scores_written(w, NG, 0, NG))

            def choices(name, tab, nblk):
                def gather_rows(b, s):
                    pool.wait_ge(sem(name + "_ids"), b + 1)
                    after(pool, sem(name + "_turned"), b - 1)
                    pool.sem_inc(sem("pool_turn"), 1)
                    p.indirect_dma_start(out=xs[:, s, :], out_offset=None, in_=tab,
                                         in_offset=bass.IndirectOffsetOnAxis(ap=ids[:, s, :], axis=0))\
                        .then_inc(sem(f"{name}_xs{s}"), 16)

                pool.wait_ge(sem(name + "_tab"), 16)
                block_steps(pool, nblk, gather_rows)
                for s in range(2):
                    pool.wait_ge(sem(f"{name}_stored{s}"), 16 * ((nblk + 1 - s) // 2))
                for t in range(T):
                    for j in range(2):
                        p.indirect_dma_start(out=yg[:, j, t, :], out_offset=None, in_=slot_y,
                                             in_offset=bass.IndirectOffsetOnAxis(ap=sloti[:, j, t:t + 1], axis=0))\
                            .then_inc(sem(f"back{t}"), 16)

            choices("e0", row_tab[0], NBLK0)
            pool.wait_ge(sem("e0_added"), 2 * T)
            for q in range(2):
                p.memset(fq[(1 - q) * HD:(2 - q) * HD, :, q, :], 0.0).then_inc(sem("fq_zeros"), 1)
            choices("e1", row_tab[1], NBLK1)

        @block.sync
        def _(sp):
            sp.dma_start(x[:, :, :], x_in.rearrange("(t p) d -> p t d", p=P)).then_inc(sem("x_in"), 16)
            n_lr = WOFF["lr"][1]
            sp.dma_start(wres[:, :, 0:n_lr], w0_in[:, :, 0:n_lr]).then_inc(sem("wlr_in"), 16)
            sp.dma_start(srci, src_in).then_inc(sem("edges_in"), 16)
            sp.dma_start(dsti, dst_in).then_inc(sem("edges_in"), 16)
            sp.dma_start(vec[:, 0:V_SIZE0], vec0_in.partition_broadcast(P)).then_inc(sem("vec0_in"), 16)
            sp.dma_start(fbias[:, :], fb_in).then_inc(sem("fb_in"), 16)
            sp.dma_start(wres[:, :, n_lr:W_SIZES[0]], w0_in[:, :, n_lr:]).then_inc(sem("w0_in"), 16)
            sp.wait_ge(sem("mixw0"), 1)
            for q in range(4):
                rows = slice(32 * q, 32 * q + 32)
                sp.dma_start(mixw[rows, q, :], mixw_in[:, 0:KR + DH]).then_inc(sem("mixw_in"), 16)
                for k in range(K2):
                    at = (4 * k + q) * KR
                    sp.dma_start(mixk[rows, k, at:at + KR], mixw_in[:, KR + DH:]).then_inc(sem("mixw_in"), 16)
            cells = [t.rearrange("(m p n) h -> m p (n h)", m=T, p=P) for t in pair_scores]

            def blank_cells(w, tiles):
                for m in tiles:
                    sp.dma_start(cells[w][m], cnt[:, 0:4, :].rearrange("p m n -> p (m n)"))\
                        .then_inc(sem(f"blank{w}"), 16)

            sp.wait_ge(sem("blank"), 1)
            blank_cells(0, range(3))
            read_out(sp, "lr")
            for w, tab in enumerate((xl_tab, xr_tab)):
                sp.dma_start(tab.rearrange("(t p) d -> p t d", p=P), xlr[:, :, w * D:(w + 1) * D])\
                    .then_inc(sem("tables"), 16)
            blank_cells(0, range(3, T))
            sp.dma_start(w2, w2_in).then_inc(sem("w2_in"), 16)
            rows = dst_cols_in.rearrange("(g c) p -> g (c p)", c=G)

            def dst_rows(g, s):
                after(sp, sem("onehotT"), g - (LATE + 1))
                sp.dma_start(dst_row[:, s, :], rows[bass.ds(g, 1), :].rearrange("a n -> (a n)").partition_broadcast(P))\
                    .then_inc(sem(f"dst_row{s}"), 16)

            for m in range(T):
                sp.wait_ge(sem("scored"), m + 1)
                blank_cells(1, [m])
            sp.wait_ge(sem("h2"), 1)
            dst_rows(LATE, 0)
            dst_rows(LATE + 1, 1)
            with sp.Fori(LATE // 2 + 1, NG // 2) as i:
                for s in range(2):
                    dst_rows(i * 2 + s, s)
            for w in range(2):
                sp.wait_ge(sem(f"scattered{w}"), scores_written(w, NG, 0, NG))
            for m in range(T):
                if m == 1:
                    sp.wait_ge(sem("counts_out"), 1)
                if m >= 2:
                    sp.wait_ge(sem("l0_taken"), (m - 1) * H)
                for w in range(2):
                    sp.dma_start(sdense[:, m % 2, w, :, :].rearrange("p n h -> p (n h)"), cells[w][m])\
                        .then_inc(sem(f"sdense{m % 2}"), 16)

            def expert_weights(name, nblk, nu, w_in, w_outs):
                def owned(b, *weights):
                    owner = sp.value_load(bown_i[0:1, bass.ds(b, 1)], min_val=0, max_val=w_in.shape[0] - 1)
                    return [w[bass.ds(owner, 1)].rearrange("e p n -> (e p) n") for w in weights]

                def load_out(b, s):
                    parts = owned(b, *w_outs)
                    after(sp, sem(name + "_out"), b - 1)
                    for part, slot in zip(parts, (exo, exo_r)):
                        sp.dma_start(slot[0:part.shape[0], s, 0:part.shape[1]], part)\
                            .then_inc(sem(f"{name}_wout{s}"), 16)

                def load(b, s):
                    w, = owned(b, w_in)
                    after(sp, sem(name + "_hid"), (b - 1) * nu)
                    sp.dma_start(exw[:, s, 0:w.shape[1]], w).then_inc(sem(f"{name}_in{s}"), 16)
                    if not (isinstance(b, int) and b == 0):
                        load_out(b - 1, 1 - s)

                sp.wait_ge(sem(name + "_owners"), 1)
                block_steps(sp, nblk, load)
                load_out(nblk - 1, (nblk - 1) % 2)

            def store_rows(name, tab, src):
                sp.dma_start(tab.rearrange("(t p) d -> p t d", p=P), src[:, :, :]).then_inc(sem(name + "_tab"), 16)

            sp.wait_ge(sem("xn1"), T)
            store_rows("e0", row_tab[0], xn)
            expert_weights("e0", NBLK0, 1, exp0_in, [exp0o_in])
            sp.wait_ge(sem("e0_slots"), 1)
            sp.dma_start(wres[:, :, 0:W_SIZES[1]], w1_in).then_inc(sem("w1_in"), 16)
            sp.dma_start(vec[:, 0:V_SIZE], vec1_in.partition_broadcast(P)).then_inc(sem("vec1_in"), 16)
            sp.wait_ge(sem("e0_added"), 2 * T)
            sp.dma_start(rope, rope_in).then_inc(sem("rope_in"), 16)
            read_out(sp, "l2", "agg")
            sp.wait_ge(sem("flat"), 1)
            store_rows("e1", row_tab[1], ta)
            expert_weights("e1", NBLK1, 2, exp1_in, [exp1o_in, exp1r_in])
            for t in range(T):
                sp.wait_ge(sem("e1_added"), 2 * t + 2)
                sp.dma_start(out[t * P:(t + 1) * P, :], x[:, t, :]).then_inc(sem("out"), 16)
            sp.wait_ge(sem("out"), T * 16)


def kernel(**inputs):
    import concourse.bacc as bacc
    from concourse.bass_utils import run_bass_kernel_spmd

    a = {k: np.asarray(v) for k, v in inputs.items()}

    def halves(*ws):
        w = np.concatenate(ws, axis=-1)
        return w.reshape(K2, 128, w.shape[-1]).transpose(1, 0, 2)

    def columns(v):
        return v.reshape(-1, 128).T

    l0 = [a["L0_gnn_att"], a["L0_gnn_bias"], a["L0_gnn_gamma"], a["L0_gnn_beta"], a["L0_mix_ln1_g"],
          a["L0_mix_ln1_b"], a["L0_mix_bo"], a["L0_mix_ln2_g"], a["L0_mix_ln2_b"], a["L0_mix_b2"],
          a["L0_ffn_gate_b"]]
    l1 = [a["L1_gnn_bv"], a["L1_gnn_bskip"], a["L1_gnn_Wgate"], a["L1_gnn_ln_w"], a["L1_gnn_ln_b"],
          a["L1_mix_kln_weight"], a["L1_mix_kln_bias"], a["L1_mix_vln_weight"], a["L1_mix_vln_bias"],
          a["L1_ffn_ln1_w"], a["L1_ffn_ln2_w"], a["L1_gnn_bgate"], a["L1_gnn_prelu_a"]]
    other = np.arange(D).reshape(H, 2, HD // 2)[:, ::-1].reshape(D)
    wq, wk = a["L1_ffn_wq"].T, a["L1_ffn_wk"].T
    twice = np.repeat(np.arange(128).reshape(2, HD), 2, axis=0).reshape(D)
    wk2 = wk[:, twice]
    inv_freq = 1.0 / 10000.0 ** (np.arange(0, HD, 2, dtype=np.float32) / HD)
    freqs = np.outer(np.arange(N, dtype=np.float32), inv_freq)
    emb = np.concatenate([freqs, freqs], axis=-1)
    sign = np.concatenate([-np.ones(HD // 2), np.ones(HD // 2)])
    rope = np.stack([np.tile(np.cos(emb).T, (2, 1)), np.tile((np.sin(emb) * sign).T, (2, 1))], axis=1)

    def expert(win, wgate, wout, rows):
        n_exp, _, hidden = win.shape
        w_in = np.concatenate([w.reshape(n_exp, K2, 128, hidden).transpose(0, 2, 1, 3).reshape(n_exp, 128, -1)
                               for w in (win, wgate)], axis=2)
        main = hidden // rows * rows
        w_out = wout[:, :main].reshape(n_exp, -1, rows, D).transpose(0, 2, 1, 3).reshape(n_exp, rows, -1)
        return w_in, w_out, wout[:, main:]

    exp0, exp0o, _ = expert(a["L0_ffn_w1"], a["L0_ffn_w2"], a["L0_ffn_w3"], HT0)
    exp1, exp1o, exp1r = expert(a["L1_ffn_w1"].transpose(0, 2, 1), a["L1_ffn_w3"].transpose(0, 2, 1),
                                a["L1_ffn_w2"].transpose(0, 2, 1), HT1)
    arrays = {
        "x": a["x"],
        "src": a["src"].reshape(P, EC),
        "dst": a["dst"].reshape(P, EC),
        "dst_cols": a["dst"].reshape(P, EC).T,
        "vec0": np.concatenate([v.reshape(-1) for v in l0]),
        "vec1": np.concatenate([v.reshape(-1) for v in l1]),
        "fb": np.concatenate([columns(a[n]) for n in ("L0_mix_bx", "L0_mix_b1", "L1_gnn_bq", "L1_gnn_bk")], axis=1),
        "w0": halves(a["L0_gnn_W_l"], a["L0_gnn_W_r"], a["L0_mix_Wx"], a["L0_mix_Wo"], a["L0_mix_W1"],
                     a["L0_ffn_gate_w"]),
        "w1": halves(a["L1_gnn_Wq"].T, a["L1_gnn_Wk"].T, a["L1_gnn_Wv"].T, a["L1_gnn_Wskip"].T, wq, wq[:, other],
                     wk2, wk2[:, other], a["L1_ffn_wv"].T, a["L1_ffn_wo"].T, a["L1_ffn_router_w"].T),
        "w2": a["L0_mix_W2"].reshape(FF // 128, 128, D).transpose(1, 0, 2),
        "mixw": np.concatenate([a["L0_mix_Wq"], a["L0_mix_Wv"], a["L0_mix_Wk"]], axis=1),
        "exp0": exp0,
        "exp0o": exp0o,
        "exp1": exp1,
        "exp1o": exp1o,
        "exp1r": exp1r,
        "rope": rope.astype(np.float32),
    }
    nc = bacc.Bacc("TRN2", target_bir_lowering=False, num_devices=1)
    in_map, args = {}, []
    for name, v in arrays.items():
        v = np.ascontiguousarray(v)
        in_map[f"in_{name}"] = v
        args.append(nc.dram_tensor(f"in_{name}", v.shape, mybir.dt.from_np(v.dtype), kind="ExternalInput").ap())
    args.append(nc.dram_tensor("out_x", (N, D), F32, kind="ExternalOutput").ap())
    build(nc, *args)
    return run_bass_kernel_spmd(nc, [in_map], core_ids=[0]).results[0]["out_x"]
```
